# Optimizing a Trainium2 kernel written in Bass

```python
import numpy as np
import jax
import jax.numpy as jnp

def _softmax(x, axis=-1):
    return jax.nn.softmax(x, axis=axis)

def _gelu(x):
    return jax.nn.gelu(x, approximate=True)

def _silu(x):
    return jax.nn.silu(x)

def _sigmoid(x):
    return jax.nn.sigmoid(x)

def _layernorm(x, axis=-1, eps=1e-05):
    m = jnp.mean(x, axis=axis, keepdims=True)
    v = jnp.var(x, axis=axis, keepdims=True)
    return (x - m) / jnp.sqrt(v + eps)

def _scatter_add(tgt, idx, src, axis=0):
    return tgt.at[idx].add(src)

def _segment_sum(src, seg, n):
    return jax.ops.segment_sum(src, seg, n)
kernel_name = 'mk_hybrid_d2_jaxref_r8_ac94dd'

def setup_inputs(seed: int=0):
    np.random.seed(seed)
    _w = jnp.asarray

    def _L0_attn_a_setup():
        import jax, jax.numpy as jnp
        import numpy as np
        B, S, D = (4, 256, 128)

        def _wkv(k, v, time_decay, u):
            w = -jnp.exp(time_decay)
            b, s, d = k.shape
            aa = jnp.zeros((b, d), k.dtype)
            bb = jnp.zeros((b, d), k.dtype)
            pp = jnp.full((b, d), -1e+30, k.dtype)

            def step(carry, kv):
                aa, bb, pp = carry
                kk, vv = kv
                ww = u + kk
                p = jnp.maximum(pp, ww)
                e1 = jnp.exp(pp - p)
                e2 = jnp.exp(ww - p)
                out = (e1 * aa + e2 * vv) / (e1 * bb + e2)
                ww2 = w + pp
                p2 = jnp.maximum(ww2, kk)
                e1b = jnp.exp(ww2 - p2)
                e2b = jnp.exp(kk - p2)
                return ((e1b * aa + e2b * vv, e1b * bb + e2b, p2), out)
            _, outs = jax.lax.scan(step, (aa, bb, pp), (k.transpose(1, 0, 2), v.transpose(1, 0, 2)))
            return outs.transpose(1, 0, 2)
        key = jax.random.key(seed)
        ks = jax.random.split(key, 10)
        s = 0.02
        return {'x': jax.random.normal(ks[0], (B, S, D), jnp.float32), 'time_mix_k': jax.random.uniform(ks[1], (1, 1, D), jnp.float32), 'time_mix_v': jax.random.uniform(ks[2], (1, 1, D), jnp.float32), 'time_mix_r': jax.random.uniform(ks[3], (1, 1, D), jnp.float32), 'time_decay': jax.random.normal(ks[4], (D,), jnp.float32) * 0.1, 'time_first': jax.random.normal(ks[5], (D,), jnp.float32) * 0.1, 'Wk': jax.random.normal(ks[6], (D, D), jnp.float32) * s, 'Wv': jax.random.normal(ks[7], (D, D), jnp.float32) * s, 'Wr': jax.random.normal(ks[8], (D, D), jnp.float32) * s, 'Wo': jax.random.normal(ks[9], (D, D), jnp.float32) * s}
    _L0_attn_a_in = _L0_attn_a_setup()

    def _L0_attn_b_setup():
        import jax, jax.numpy as jnp
        import numpy as np
        NUM_HEADS = 16
        key = jax.random.key(seed)
        kx, kq, kk, kv = jax.random.split(key, 4)
        N, S, D = (2, 512, 128)
        scale = 1.0 / np.sqrt(D)
        x = jax.random.normal(kx, (N, S, D), dtype=jnp.float32)
        Wq = jax.random.normal(kq, (D, D), dtype=jnp.float32) * scale
        Wk = jax.random.normal(kk, (D, D), dtype=jnp.float32) * scale
        Wv = jax.random.normal(kv, (D, D), dtype=jnp.float32) * scale
        return {'x': x, 'Wq': Wq, 'Wk': Wk, 'Wv': Wv}
    _L0_attn_b_in = _L0_attn_b_setup()

    def _L0_ffn_setup():
        import jax, jax.numpy as jnp
        import numpy as np
        B, S, D, F, E = (4, 256, 128, 512, 8)
        key = jax.random.key(seed)
        ks = jax.random.split(key, 7)
        s1 = 1.0 / np.sqrt(D)
        s2 = 1.0 / np.sqrt(F)
        x = jax.random.normal(ks[0], (B, S, D), dtype=jnp.float32)
        W1 = jax.random.uniform(ks[1], (E, D, F), jnp.float32, -s1, s1)
        b1 = jax.random.uniform(ks[2], (E, F), jnp.float32, -s1, s1)
        W2 = jax.random.uniform(ks[3], (E, F, D), jnp.float32, -s2, s2)
        b2 = jax.random.uniform(ks[4], (E, D), jnp.float32, -s2, s2)
        Wr = jax.random.uniform(ks[5], (D, E), jnp.float32, -s1, s1)
        br = jax.random.uniform(ks[6], (E,), jnp.float32, -s1, s1)
        return {'x': x, 'W1': W1, 'b1': b1, 'W2': W2, 'b2': b2, 'Wr': Wr, 'br': br}
    _L0_ffn_in = _L0_ffn_setup()

    def _L1_attn_a_setup():
        import jax, jax.numpy as jnp
        import numpy as np
        import math
        DIM, DIM_QK, DIM_V = (128, 128, 128)
        NUM_BUCKETS, MAX_DISTANCE = (32, 128)

        def silu(x):
            return x * jax.nn.sigmoid(x)

        def laplacian_attn_fn(x):
            mu = math.sqrt(0.5)
            std = math.sqrt(0.25 * math.pi)
            return (1.0 + jax.lax.erf((x - mu) / (std * math.sqrt(2.0)))) * 0.5

        def rel_pos_bias(seq_len, table, scale):
            q_pos = jnp.arange(seq_len)
            k_pos = jnp.arange(seq_len)
            rel_pos = k_pos[None, :] - q_pos[:, None]
            n = jnp.maximum(-rel_pos, 0)
            max_exact = NUM_BUCKETS // 2
            is_small = n < max_exact
            n_safe = jnp.maximum(n, 1).astype(jnp.float32)
            val_if_large = max_exact + (jnp.log(n_safe / max_exact) / math.log(MAX_DISTANCE / max_exact) * (NUM_BUCKETS - max_exact)).astype(jnp.int32)
            val_if_large = jnp.minimum(val_if_large, NUM_BUCKETS - 1)
            bucket = jnp.where(is_small, n, val_if_large)
            return table[bucket] * scale
        key = jax.random.key(seed)
        ks = jax.random.split(key, 8)
        B, S = (4, 256)
        lin_std_qk = 1.0 / math.sqrt(DIM)
        return {'x': jax.random.normal(ks[0], (B, S, DIM), dtype=jnp.float32), 'wqk': jax.random.uniform(ks[1], (DIM, DIM_QK), minval=-lin_std_qk, maxval=lin_std_qk, dtype=jnp.float32), 'bqk': jnp.zeros((DIM_QK,), dtype=jnp.float32), 'gamma': 1.0 + 0.02 * jax.random.normal(ks[2], (2, DIM_QK), dtype=jnp.float32), 'beta': jnp.zeros((2, DIM_QK), dtype=jnp.float32), 'wv': jax.random.uniform(ks[3], (DIM, DIM_V), minval=-lin_std_qk, maxval=lin_std_qk, dtype=jnp.float32), 'bv': jnp.zeros((DIM_V,), dtype=jnp.float32), 'rel_bias': jax.random.normal(ks[4], (NUM_BUCKETS,), dtype=jnp.float32)}
    _L1_attn_a_in = _L1_attn_a_setup()

    def _L1_attn_b_setup():
        import jax, jax.numpy as jnp
        import numpy as np
        import math
        DIM = 128
        D_STATE = 16
        D_CONV = 4
        EXPAND = 2
        D_INNER = EXPAND * DIM
        DT_RANK = math.ceil(DIM / 16)
        B_SZ, L_SEQ = (2, 128)

        def _mamba(x, in_proj_w, conv_w, conv_b, x_proj_w, dt_proj_w, dt_proj_b, A_log, D, out_proj_w):
            Bt, L, _ = x.shape
            xz = jnp.einsum('bld,ed->ble', x, in_proj_w)
            xin, z = jnp.split(xz, 2, axis=-1)
            xp = jnp.pad(xin, ((0, 0), (D_CONV - 1, 0), (0, 0)))
            xc = conv_b
            xc = sum((conv_w[:, 0, k] * xp[:, k:k + L, :] for k in range(D_CONV))) + conv_b
            xin = jax.nn.silu(xc)
            x_dbl = jnp.einsum('bld,ed->ble', xin, x_proj_w)
            dt, Bmat, Cmat = jnp.split(x_dbl, [DT_RANK, DT_RANK + D_STATE], axis=-1)
            delta = jax.nn.softplus(jnp.einsum('blr,dr->bld', dt, dt_proj_w) + dt_proj_b)
            A = -jnp.exp(A_log)
            deltaA = jnp.exp(jnp.einsum('bld,dn->bldn', delta, A))
            deltaBu = jnp.einsum('bld,bln,bld->bldn', delta, Bmat, xin)

            def combine(left, right):
                a_l, b_l = left
                a_r, b_r = right
                return (a_l * a_r, a_r * b_l + b_r)
            _, hs = jax.lax.associative_scan(combine, (deltaA, deltaBu), axis=1)
            y = jnp.einsum('bldn,bln->bld', hs, Cmat) + xin * D
            y = y * jax.nn.silu(z)
            return jnp.einsum('bld,od->blo', y, out_proj_w)
        key = jax.random.key(seed)
        ks = jax.random.split(key, 9)
        std_in = D_INNER ** (-0.5)
        std_dim = DIM ** (-0.5)
        x = jax.random.normal(ks[0], (B_SZ, L_SEQ, DIM), dtype=jnp.float32)
        in_proj_w = jax.random.uniform(ks[1], (2 * D_INNER, DIM), minval=-std_in, maxval=std_in, dtype=jnp.float32)
        conv_w = jax.random.uniform(ks[2], (D_INNER, 1, D_CONV), minval=-std_in, maxval=std_in, dtype=jnp.float32)
        conv_b = jax.random.uniform(ks[3], (D_INNER,), minval=-std_in, maxval=std_in, dtype=jnp.float32)
        x_proj_w = jax.random.uniform(ks[4], (DT_RANK + 2 * D_STATE, D_INNER), minval=-0.1, maxval=0.1, dtype=jnp.float32)
        dt_proj_w = jax.random.uniform(ks[5], (D_INNER, DT_RANK), minval=-std_in, maxval=std_in, dtype=jnp.float32)
        dt_proj_b = jax.random.uniform(ks[6], (D_INNER,), minval=-4.0, maxval=-2.0, dtype=jnp.float32)
        A_log = jnp.log(jnp.broadcast_to(jnp.arange(1, D_STATE + 1, dtype=jnp.float32), (D_INNER, D_STATE)))
        D = jnp.ones((D_INNER,), dtype=jnp.float32)
        out_proj_w = jax.random.uniform(ks[7], (DIM, D_INNER), minval=-std_dim, maxval=std_dim, dtype=jnp.float32)
        return {'x': x, 'in_proj_w': in_proj_w, 'conv_w': conv_w, 'conv_b': conv_b, 'x_proj_w': x_proj_w, 'dt_proj_w': dt_proj_w, 'dt_proj_b': dt_proj_b, 'A_log': A_log, 'D': D, 'out_proj_w': out_proj_w}
    _L1_attn_b_in = _L1_attn_b_setup()

    def _L1_ffn_setup():
        import jax, jax.numpy as jnp
        import numpy as np
        B, T, D, H, E = (4, 256, 128, 256, 8)
        TOP_K = int(E * 0.25)
        key = jax.random.key(seed)
        ks = jax.random.split(key, 6)
        x = jax.random.normal(ks[0], (B, T, D), dtype=jnp.float32)
        gate = jax.random.normal(ks[1], (D, E), dtype=jnp.float32)
        W1 = jax.random.normal(ks[2], (E, D, H), dtype=jnp.float32) * D ** (-0.5)
        b1 = jnp.zeros((E, H), dtype=jnp.float32)
        W2 = jax.random.normal(ks[3], (E, H, D), dtype=jnp.float32) * H ** (-0.5)
        b2 = jnp.zeros((E, D), dtype=jnp.float32)
        return {'x': x, 'gate': gate, 'W1': W1, 'b1': b1, 'W2': W2, 'b2': b2}
    _L1_ffn_in = _L1_ffn_setup()
    _d = {'L0_attn_a_x': _L0_attn_a_in['x'], 'L0_attn_a_time_mix_k': _L0_attn_a_in['time_mix_k'], 'L0_attn_a_time_mix_v': _L0_attn_a_in['time_mix_v'], 'L0_attn_a_time_mix_r': _L0_attn_a_in['time_mix_r'], 'L0_attn_a_time_decay': _L0_attn_a_in['time_decay'], 'L0_attn_a_time_first': _L0_attn_a_in['time_first'], 'L0_attn_a_Wk': _L0_attn_a_in['Wk'], 'L0_attn_a_Wv': _L0_attn_a_in['Wv'], 'L0_attn_a_Wr': _L0_attn_a_in['Wr'], 'L0_attn_a_Wo': _L0_attn_a_in['Wo'], 'L0_attn_b_Wq': _L0_attn_b_in['Wq'], 'L0_attn_b_Wk': _L0_attn_b_in['Wk'], 'L0_attn_b_Wv': _L0_attn_b_in['Wv'], 'L0_ffn_W1': _L0_ffn_in['W1'], 'L0_ffn_b1': _L0_ffn_in['b1'], 'L0_ffn_W2': _L0_ffn_in['W2'], 'L0_ffn_b2': _L0_ffn_in['b2'], 'L0_ffn_Wr': _L0_ffn_in['Wr'], 'L0_ffn_br': _L0_ffn_in['br'], 'L1_attn_a_wqk': _L1_attn_a_in['wqk'], 'L1_attn_a_bqk': _L1_attn_a_in['bqk'], 'L1_attn_a_gamma': _L1_attn_a_in['gamma'], 'L1_attn_a_beta': _L1_attn_a_in['beta'], 'L1_attn_a_wv': _L1_attn_a_in['wv'], 'L1_attn_a_bv': _L1_attn_a_in['bv'], 'L1_attn_a_rel_bias': _L1_attn_a_in['rel_bias'], 'L1_attn_b_in_proj_w': _L1_attn_b_in['in_proj_w'], 'L1_attn_b_conv_w': _L1_attn_b_in['conv_w'], 'L1_attn_b_conv_b': _L1_attn_b_in['conv_b'], 'L1_attn_b_x_proj_w': _L1_attn_b_in['x_proj_w'], 'L1_attn_b_dt_proj_w': _L1_attn_b_in['dt_proj_w'], 'L1_attn_b_dt_proj_b': _L1_attn_b_in['dt_proj_b'], 'L1_attn_b_A_log': _L1_attn_b_in['A_log'], 'L1_attn_b_D': _L1_attn_b_in['D'], 'L1_attn_b_out_proj_w': _L1_attn_b_in['out_proj_w'], 'L1_ffn_gate': _L1_ffn_in['gate'], 'L1_ffn_W1': _L1_ffn_in['W1'], 'L1_ffn_b1': _L1_ffn_in['b1'], 'L1_ffn_W2': _L1_ffn_in['W2'], 'L1_ffn_b2': _L1_ffn_in['b2']}
    _x0 = _d['L0_attn_a_x']
    _d['L0_attn_a_x'] = jax.random.normal(jax.random.fold_in(jax.random.key(seed), 1), (8, 512, 128), dtype=_x0.dtype)
    del _x0
    return _d

def reference(L0_attn_a_x, L0_attn_a_time_mix_k, L0_attn_a_time_mix_v, L0_attn_a_time_mix_r, L0_attn_a_time_decay, L0_attn_a_time_first, L0_attn_a_Wk, L0_attn_a_Wv, L0_attn_a_Wr, L0_attn_a_Wo, L0_attn_b_Wq, L0_attn_b_Wk, L0_attn_b_Wv, L0_ffn_W1, L0_ffn_b1, L0_ffn_W2, L0_ffn_b2, L0_ffn_Wr, L0_ffn_br, L1_attn_a_wqk, L1_attn_a_bqk, L1_attn_a_gamma, L1_attn_a_beta, L1_attn_a_wv, L1_attn_a_bv, L1_attn_a_rel_bias, L1_attn_b_in_proj_w, L1_attn_b_conv_w, L1_attn_b_conv_b, L1_attn_b_x_proj_w, L1_attn_b_dt_proj_w, L1_attn_b_dt_proj_b, L1_attn_b_A_log, L1_attn_b_D, L1_attn_b_out_proj_w, L1_ffn_gate, L1_ffn_W1, L1_ffn_b1, L1_ffn_W2, L1_ffn_b2):

    def _L0_attn_a_ref(x, time_mix_k, time_mix_v, time_mix_r, time_decay, time_first, Wk, Wv, Wr, Wo):
        import jax, jax.numpy as jnp
        import numpy as np
        B, S, D = (4, 256, 128)

        def _wkv(k, v, time_decay, u):
            w = -jnp.exp(time_decay)
            b, s, d = k.shape
            aa = jnp.zeros((b, d), k.dtype)
            bb = jnp.zeros((b, d), k.dtype)
            pp = jnp.full((b, d), -1e+30, k.dtype)

            def step(carry, kv):
                aa, bb, pp = carry
                kk, vv = kv
                ww = u + kk
                p = jnp.maximum(pp, ww)
                e1 = jnp.exp(pp - p)
                e2 = jnp.exp(ww - p)
                out = (e1 * aa + e2 * vv) / (e1 * bb + e2)
                ww2 = w + pp
                p2 = jnp.maximum(ww2, kk)
                e1b = jnp.exp(ww2 - p2)
                e2b = jnp.exp(kk - p2)
                return ((e1b * aa + e2b * vv, e1b * bb + e2b, p2), out)
            _, outs = jax.lax.scan(step, (aa, bb, pp), (k.transpose(1, 0, 2), v.transpose(1, 0, 2)))
            return outs.transpose(1, 0, 2)
        shifted = jnp.concatenate([jnp.zeros_like(x[:, :1, :]), x[:, :-1, :]], axis=1)
        xk = x * time_mix_k + shifted * (1.0 - time_mix_k)
        xv = x * time_mix_v + shifted * (1.0 - time_mix_v)
        xr = x * time_mix_r + shifted * (1.0 - time_mix_r)
        k = jnp.einsum('bsd,ed->bse', xk, Wk)
        v = jnp.einsum('bsd,ed->bse', xv, Wv)
        r = jax.nn.sigmoid(jnp.einsum('bsd,ed->bse', xr, Wr))
        wkv = _wkv(k, v, time_decay, time_first)
        out = jnp.einsum('bsd,ed->bse', r * wkv, Wo)
        return out

    def _L0_attn_b_ref(x, Wq, Wk, Wv):
        import jax, jax.numpy as jnp
        import numpy as np
        NUM_HEADS = 16
        N, S, D = x.shape
        H = NUM_HEADS
        hd = D // H
        q = (x @ Wq.T).reshape(N, S, H, hd).transpose(0, 2, 1, 3)
        k = (x @ Wk.T).reshape(N, S, H, hd).transpose(0, 2, 1, 3)
        v = (x @ Wv.T).reshape(N, S, H, hd).transpose(0, 2, 1, 3)
        energy = jnp.einsum('nhqd,nhkd->nhqk', q, k)
        attn = jax.nn.softmax(energy / jnp.sqrt(jnp.float32(hd)), axis=3)
        out = jnp.einsum('nhql,nhld->nhqd', attn, v)
        return out.transpose(0, 2, 1, 3).reshape(N, S, D)

    def _L0_ffn_ref(x, W1, b1, W2, b2, Wr, br):
        import jax, jax.numpy as jnp
        import numpy as np
        B, S, D, F, E = (4, 256, 128, 512, 8)
        b, s, d = x.shape
        e = Wr.shape[1]
        logits = x @ Wr + br
        idx = jnp.argmax(logits, axis=-1)
        probs = jax.nn.softmax(logits, axis=-1)
        gates = jnp.take_along_axis(probs, idx[..., None], axis=-1)[..., 0]
        xf = x.reshape(-1, d)
        idxf = idx.reshape(-1)
        gf = gates.reshape(-1)
        out = jnp.zeros_like(xf)
        for ei in range(e):
            h = jax.nn.gelu(xf @ W1[ei] + b1[ei], approximate=False)
            y = h @ W2[ei] + b2[ei]
            mask = (idxf == ei).astype(xf.dtype)
            out = out + y * (gf * mask)[:, None]
        return out.reshape(b, s, d)

    def _L1_attn_a_ref(x, wqk, bqk, gamma, beta, wv, bv, rel_bias):
        import jax, jax.numpy as jnp
        import numpy as np
        import math
        DIM, DIM_QK, DIM_V = (128, 128, 128)
        NUM_BUCKETS, MAX_DISTANCE = (32, 128)

        def silu(x):
            return x * jax.nn.sigmoid(x)

        def laplacian_attn_fn(x):
            mu = math.sqrt(0.5)
            std = math.sqrt(0.25 * math.pi)
            return (1.0 + jax.lax.erf((x - mu) / (std * math.sqrt(2.0)))) * 0.5

        def rel_pos_bias(seq_len, table, scale):
            q_pos = jnp.arange(seq_len)
            k_pos = jnp.arange(seq_len)
            rel_pos = k_pos[None, :] - q_pos[:, None]
            n = jnp.maximum(-rel_pos, 0)
            max_exact = NUM_BUCKETS // 2
            is_small = n < max_exact
            n_safe = jnp.maximum(n, 1).astype(jnp.float32)
            val_if_large = max_exact + (jnp.log(n_safe / max_exact) / math.log(MAX_DISTANCE / max_exact) * (NUM_BUCKETS - max_exact)).astype(jnp.int32)
            val_if_large = jnp.minimum(val_if_large, NUM_BUCKETS - 1)
            bucket = jnp.where(is_small, n, val_if_large)
            return table[bucket] * scale
        B, S, _ = x.shape
        qk = silu(x @ wqk + bqk)
        q = qk * gamma[0] + beta[0]
        k = qk * gamma[1] + beta[1]
        v = silu(x @ wv + bv)
        scale = 1.0 / S
        sim = jnp.einsum('bid,bjd->bij', q, k) * scale
        sim = sim + rel_pos_bias(S, rel_bias, DIM_QK ** 0.5)[None, :, :]
        attn = laplacian_attn_fn(sim)
        causal_mask = jnp.triu(jnp.ones((S, S), dtype=bool), k=1)
        attn = jnp.where(causal_mask[None, :, :], 0.0, attn)
        return jnp.einsum('bij,bjd->bid', attn, v)

    def _L1_attn_b_ref(x, in_proj_w, conv_w, conv_b, x_proj_w, dt_proj_w, dt_proj_b, A_log, D, out_proj_w):
        import jax, jax.numpy as jnp
        import numpy as np
        import math
        DIM = 128
        D_STATE = 16
        D_CONV = 4
        EXPAND = 2
        D_INNER = EXPAND * DIM
        DT_RANK = math.ceil(DIM / 16)
        B_SZ, L_SEQ = (2, 128)

        def _mamba(x, in_proj_w, conv_w, conv_b, x_proj_w, dt_proj_w, dt_proj_b, A_log, D, out_proj_w):
            Bt, L, _ = x.shape
            xz = jnp.einsum('bld,ed->ble', x, in_proj_w)
            xin, z = jnp.split(xz, 2, axis=-1)
            xp = jnp.pad(xin, ((0, 0), (D_CONV - 1, 0), (0, 0)))
            xc = conv_b
            xc = sum((conv_w[:, 0, k] * xp[:, k:k + L, :] for k in range(D_CONV))) + conv_b
            xin = jax.nn.silu(xc)
            x_dbl = jnp.einsum('bld,ed->ble', xin, x_proj_w)
            dt, Bmat, Cmat = jnp.split(x_dbl, [DT_RANK, DT_RANK + D_STATE], axis=-1)
            delta = jax.nn.softplus(jnp.einsum('blr,dr->bld', dt, dt_proj_w) + dt_proj_b)
            A = -jnp.exp(A_log)
            deltaA = jnp.exp(jnp.einsum('bld,dn->bldn', delta, A))
            deltaBu = jnp.einsum('bld,bln,bld->bldn', delta, Bmat, xin)

            def combine(left, right):
                a_l, b_l = left
                a_r, b_r = right
                return (a_l * a_r, a_r * b_l + b_r)
            _, hs = jax.lax.associative_scan(combine, (deltaA, deltaBu), axis=1)
            y = jnp.einsum('bldn,bln->bld', hs, Cmat) + xin * D
            y = y * jax.nn.silu(z)
            return jnp.einsum('bld,od->blo', y, out_proj_w)
        return _mamba(x, in_proj_w, conv_w, conv_b, x_proj_w, dt_proj_w, dt_proj_b, A_log, D, out_proj_w)

    def _L1_ffn_ref(x, gate, W1, b1, W2, b2):
        import jax, jax.numpy as jnp
        import numpy as np
        B, T, D, H, E = (4, 256, 128, 256, 8)
        TOP_K = int(E * 0.25)
        raw_gate = jax.nn.softmax(jnp.einsum('btd,de->bte', x, gate), axis=-1)
        topk_scores, topk_idx = jax.lax.top_k(raw_gate, TOP_K)
        mask = jax.nn.one_hot(topk_idx, E, dtype=raw_gate.dtype).sum(axis=-2)
        gate_topk = mask * raw_gate
        gate_topk = gate_topk / jnp.maximum(gate_topk.sum(axis=-1, keepdims=True), 1e-12)
        h = jax.nn.relu(jnp.einsum('btd,edh->beth', x, W1) + b1[None, :, None, :])
        expert_out = jnp.einsum('beth,ehd->betd', h, W2) + b2[None, :, None, :]
        out = jnp.einsum('bte,betd->btd', gate_topk, expert_out)
        return out
    x = L0_attn_a_x
    x = x + _L0_attn_a_ref(_layernorm(x, axis=-1), L0_attn_a_time_mix_k, L0_attn_a_time_mix_v, L0_attn_a_time_mix_r, L0_attn_a_time_decay, L0_attn_a_time_first, L0_attn_a_Wk, L0_attn_a_Wv, L0_attn_a_Wr, L0_attn_a_Wo)
    x = x + _L0_ffn_ref(_layernorm(x, axis=-1), L0_ffn_W1, L0_ffn_b1, L0_ffn_W2, L0_ffn_b2, L0_ffn_Wr, L0_ffn_br)
    x = x + _L0_attn_b_ref(_layernorm(x, axis=-1), L0_attn_b_Wq, L0_attn_b_Wk, L0_attn_b_Wv)
    x = x + _L0_ffn_ref(_layernorm(x, axis=-1), L0_ffn_W1, L0_ffn_b1, L0_ffn_W2, L0_ffn_b2, L0_ffn_Wr, L0_ffn_br)
    x = x + _L1_attn_a_ref(_layernorm(x, axis=-1), L1_attn_a_wqk, L1_attn_a_bqk, L1_attn_a_gamma, L1_attn_a_beta, L1_attn_a_wv, L1_attn_a_bv, L1_attn_a_rel_bias)
    x = x + _L1_ffn_ref(_layernorm(x, axis=-1), L1_ffn_gate, L1_ffn_W1, L1_ffn_b1, L1_ffn_W2, L1_ffn_b2)
    x = x + _L1_attn_b_ref(_layernorm(x, axis=-1), L1_attn_b_in_proj_w, L1_attn_b_conv_w, L1_attn_b_conv_b, L1_attn_b_x_proj_w, L1_attn_b_dt_proj_w, L1_attn_b_dt_proj_b, L1_attn_b_A_log, L1_attn_b_D, L1_attn_b_out_proj_w)
    x = x + _L1_ffn_ref(_layernorm(x, axis=-1), L1_ffn_gate, L1_ffn_W1, L1_ffn_b1, L1_ffn_W2, L1_ffn_b2)
    return x

_drawn_inputs = setup_inputs


def setup_inputs(seed=0):
    import zlib

    import numpy as np

    out = dict(_drawn_inputs(seed))
    spreads = {'L1_attn_a_bqk': (0.0, 2.0),
     'L1_attn_a_beta': (0.0, 2.0),
     'L1_attn_a_bv': (0.0, 0.1),
     'L1_attn_b_D': (1.0, 0.6),
     'L1_ffn_b1': (0.0, 0.8),
     'L1_ffn_b2': (0.0, 0.8)}
    factors = {'L0_attn_a_time_mix_k': 8.0,
     'L0_attn_a_time_mix_v': 8.0,
     'L0_attn_a_time_mix_r': 8.0,
     'L0_attn_a_time_decay': 8.0,
     'L0_attn_a_time_first': 8.0,
     'L0_attn_a_Wk': 8.0,
     'L0_attn_a_Wv': 7.832,
     'L0_attn_a_Wr': 8.0,
     'L0_attn_a_Wo': 7.722,
     'L0_ffn_b1': 19.343,
     'L0_ffn_b2': 10.353,
     'L0_ffn_br': 4.729,
     'L1_attn_a_wqk': 8.0,
     'L1_attn_a_gamma': 64.0,
     'L1_attn_b_in_proj_w': 8.0,
     'L1_attn_b_conv_w': 8.0,
     'L1_attn_b_conv_b': 8.0,
     'L1_attn_b_x_proj_w': 8.0,
     'L1_attn_b_dt_proj_w': 8.0,
     'L1_attn_b_dt_proj_b': 8.0,
     'L1_attn_b_A_log': 8.0,
     'L1_attn_b_out_proj_w': 8.0}
    for name, (base, spread) in spreads.items():
        noise = np.random.default_rng([zlib.crc32(name.encode()), seed]).standard_normal(out[name].shape)
        drawn = base * np.exp(spread * noise) if base else spread * noise
        out[name] = jnp.asarray(drawn.astype(out[name].dtype))
    for name, factor in factors.items():
        out[name] = (out[name] * factor).astype(out[name].dtype)
    return out
```

```python
from contextlib import ExitStack
import math

import concourse.bass as bass
from concourse import mybir

F32 = mybir.dt.float32
F32R = mybir.dt.float32r
ALU = mybir.AluOpType
ACT = mybir.ActivationFunctionType
AX_X = mybir.AxisListType.X

P = 128
BATCHES = 8
S = 512
TILES = S // P
EPS = 1e-5
BIG = 1e30


class Names:
    pass


def count(b, per, n):
    loop, constant = b
    return loop * (2 * per) + (constant * per + n)


def after(b, n):
    return b[0], b[1] + n


def credit(eng, sem, n):
    eng.nop().then_inc(sem, n)


class Steps:

    def __init__(self, eng, sem, per):
        self.eng, self.sem, self.per, self.n = eng, sem, per, 0

    def begin(self, b):
        assert self.n in (0, self.per), (self.n, self.per)
        self.b, self.n = b, 0

    def done(self, instruction):
        self.n += 1
        instruction.then_inc(self.sem, 1)
        self.eng.wait_ge(self.sem, count(self.b, self.per, self.n))


def rows(b, tile=0, tiles=TILES):
    loop, constant = b
    return bass.ds(loop * (2 * S) + (constant * S + tile * P), tiles * P)


def by_tile(ap):
    return ap.rearrange("p (t d) -> p t d", t=TILES)


def over_batches(eng, body):
    with eng.Fori(0, BATCHES // 2) as loop:
        for half in range(2):
            body((loop, half))




def take_statistics(dve, nc, m, s, b, stage, steps):
    loop, n = b
    first = loop * (2 * S) + n * S if n < 2 else (loop * 2 + n) % BATCHES * S
    dve.wait_ge(s.normed, count(b, 1, 8 * stage + 1))
    statistics_of(dve, nc, m, s, bass.ds(first, S), n % 2, steps)


def statistics_of(dve, nc, m, s, columns, h, steps):
    x = m.x[:, columns]
    for t in range(TILES):
        last = dve.bn_stats(m.bn[:, h, t, :], x[:, t * P:(t + 1) * P])
    steps.done(last)
    even, odd, mv, half = m.bn[:, h, :, 0:3], m.bn[:, h, :, 3:6], m.mean_var[:, h], m.half_stats
    dve.tensor_tensor(half[:, 0, :], even[:, :, 1], odd[:, :, 1], ALU.add)
    dve.tensor_tensor(half[:, 1, :], even[:, :, 1], odd[:, :, 1], ALU.subtract)
    steps.done(dve.tensor_tensor(half[:, 2, :], even[:, :, 2], odd[:, :, 2], ALU.add))
    dve.tensor_scalar(mv[:, :, 0], half[:, 0, :], 0.5, None, ALU.mult)
    dve.scalar_tensor_tensor(half[:, 3, :], half[:, 1, :], 0.25, half[:, 1, :], ALU.mult, ALU.mult)
    steps.done(dve.tensor_scalar(half[:, 4, :], half[:, 2, :], 1.0 / P, EPS, ALU.mult, ALU.add))
    dve.tensor_tensor(mv[:, :, 1], half[:, 3, :], half[:, 4, :], ALU.add).then_inc(s.stats, 1)


def normalise(pool, nc, m, s, b, stage):
    h = b[1] % 2
    mv, rstd = m.mean_var[:, h], m.rstd[:, h]
    pool.wait_ge(s.stats, count(b, 1, 8 * stage + 1))
    pool.tensor_tensor(rstd, mv[:, :, 1], m.minus_half[:, :], ALU.pow).then_inc(s.rstd, 1)
    pool.wait_ge(s.transposed, count(b, 1, 8 * stage + 1))
    wide = [P, TILES, P]
    pool.tensor_tensor(by_tile(m.xn[:, h, :]), by_tile(m.x[:, rows(b)]), mv[:, :, 0:1].to_broadcast(wide),
                       ALU.subtract).then_inc(s.centred, 1)
    pool.wait_ge(s.rstd, count(b, 1, 8 * stage + 1))
    pool.wait_ge(s.centred, count(b, 1, 8 * stage + 1))
    pool.tensor_tensor(by_tile(m.xn[:, h, :]), by_tile(m.xn[:, h, :]), rstd.unsqueeze(2).to_broadcast(wide),
                       ALU.mult).then_inc(s.normed, 1)


def transpose_batch(pe, nc, m, s, b, stage):
    pe.wait_ge(s.normed, count(b, 1, 8 * stage + 3))
    pe.wait_ge(s.xt, count(b, 1, 8 * stage + 1))
    for t in range(TILES):
        last = pe.transpose(m.bank[0][:, t * P:(t + 1) * P], m.xn[:, b[1] % 2, t * P:(t + 1) * P], m.ident[:, :])
    last.then_inc(s.transposed, 1)


def keep_transposed(act, nc, m, s, b, stage):
    act.wait_ge(s.transposed, count(b, 1, 8 * stage + 3))
    act.activation(m.xt[:, b[1] % 2, 1:S + 1], m.bank[0][:, :], ACT.Copy).then_inc(s.xt, 1)


def xt_ready(eng, s, b, stage):
    eng.wait_ge(s.xt, count(b, 1, 8 * stage + 2))




def experts_tensor(pe, nc, m, s, f, stage):
    NB, E = f.blocks, 8
    outs = E + 1
    credit(pe, f.out, 3)

    def second_layer(b, e):
        h = b[1]
        pe.wait_ge(f.hidden, count(b, E * NB, (e + 1) * NB + 4))
        pe.wait_ge(f.added, count(b, outs, e + 1))
        out = m.bank[6 + (h * outs + e) % 2]
        for t in range(TILES):
            for j in range(NB):
                last = pe.matmul(out[:, t * P:(t + 1) * P], f.hid[:, e % 2, j, t * P:(t + 1) * P],
                                 f.w2[:, (e * NB + j) * P:(e * NB + j + 1) * P], start=j == 0, stop=j == NB - 1)
        last.then_inc(f.out, 1)

    def body(b):
        h = b[1]
        xt = m.xt[:, h, 1:S + 1]
        transpose_batch(pe, nc, m, s, b, stage)
        xt_ready(pe, s, b, stage)
        pe.wait_ge(f.gates_kept, count(b, 1, 1))
        for t in range(TILES):
            last = pe.matmul(m.bank[1][:, t * E:(t + 1) * E], xt[:, t * P:(t + 1) * P], f.wr[:, :], start=True, stop=True)
        last.then_inc(f.logits, 1)
        for e in range(E):
            for j in range(NB):
                n = e * NB + j
                pe.wait_ge(f.hidden, count(b, E * NB, n + 1))
                pe.matmul(m.bank[2 + n % 4][:, :], f.w1[:, e, j * P:(j + 1) * P], xt, start=True, stop=True).then_inc(f.first, 1)
            if e:
                second_layer(b, e - 1)
        second_layer(b, E - 1)
        pe.wait_ge(f.gates, count(b, 1, 1))
        for t in range(TILES):
            last = pe.transpose(m.bank[1][0:E, t * P:(t + 1) * P], m.gates[:, t, :], m.ident[:, :])
        last.then_inc(f.gates_turned, 1)
        pe.wait_ge(f.gates_kept, count(b, 1, 2))
        pe.wait_ge(f.added, count(b, outs, E + 1))
        out = m.bank[6 + (h * outs + E) % 2]
        for t in range(TILES):
            last = pe.matmul(out[:, t * P:(t + 1) * P], m.gates_t[0:E, t * P:(t + 1) * P], f.b2[:, :], start=True, stop=True)
        last.then_inc(f.out, 1)

    over_batches(pe, body)


def experts_scalar(act, nc, m, s, f, stage):
    NB, E = f.blocks, 8
    outs = E + 1
    credit(act, f.hidden, 4)
    credit(act, f.gates_kept, 1)

    def body(b):
        keep_transposed(act, nc, m, s, b, stage)
        act.wait_ge(f.shifted, count(b, 1, 1))
        act.activation(m.r_exp[:, :], m.r_d[:, :], ACT.Exp).then_inc(f.exps, 1)
        for e in range(E):
            act.wait_ge(f.out, count(b, outs, e + 2 if e >= 2 else e + 1))
            for j in range(NB):
                n = e * NB + j
                act.wait_ge(f.first, count(b, E * NB, n + 1))
                act.activation(f.hid[:, e % 2, j, :], m.bank[2 + n % 4][:, :], f.func,
                               bias=f.b1[:, n:n + 1]).then_inc(f.hidden, 1)
        act.wait_ge(f.gates_turned, count(b, 1, 1))
        act.activation(m.gates_t[0:E, :], m.bank[1][0:E, :], ACT.Copy).then_inc(f.gates_kept, 1)

    over_batches(act, body)


def experts_pool(pool, nc, m, s, f, stage):
    over_batches(pool, lambda b: normalise(pool, nc, m, s, b, stage))


def experts_vector(dve, nc, m, s, f, stage):
    E = 8
    outs = E + 1
    credit(dve, f.added, 2)
    steps = Steps(dve, f.steps, 8 + 3 if f.top == 1 else 21 + 3)

    def wide(column):
        return column.unsqueeze(2).to_broadcast([P, TILES, E])

    order = m.order[:, :].rearrange("p (t e) -> p t e", e=E)

    def first_largest(source, hot, peak, top):
        steps.done(dve.tensor_tensor(hot, source, wide(peak), ALU.is_equal))
        steps.done(dve.tensor_tensor(hot, hot, order, ALU.mult))
        steps.done(dve.reduce_max(top, hot, AX_X))
        steps.done(dve.tensor_tensor(hot, hot, wide(top), ALU.is_equal))

    def body(b):
        steps.begin(b)
        lg, d, ex = (v.rearrange("p (t e) -> p t e", e=E) for v in (m.r_l[:, :], m.r_d[:, :], m.r_exp[:, :]))
        hot = m.r_hot[:, :].rearrange("p (t e) -> p t e", e=E)
        two = m.r_two[:, :].rearrange("p (t e) -> p t e", e=E)
        peak, top, total = m.r_col[:, 0, :], m.r_col[:, 1, :], m.r_col[:, 2, :]
        dve.wait_ge(f.logits, count(b, 1, 1))
        ps = m.bank[1][:, 0:TILES * E]
        if f.top == 1:
            steps.done(dve.tensor_tensor(m.r_l[:, :], ps, f.br, ALU.add))
        else:
            steps.done(dve.tensor_copy(m.r_l[:, :], ps))
        steps.done(dve.reduce_max(peak, lg, AX_X))
        dve.tensor_tensor(d, lg, wide(peak), ALU.subtract).then_inc(f.shifted, 1)
        if f.top == 1:
            first_largest(lg, hot, peak, top)
            dve.wait_ge(f.exps, count(b, 1, 1))
            steps.done(dve.reduce_sum(total, ex, AX_X))
            steps.done(dve.reciprocal(total, total))
            dve.tensor_tensor(m.gates[:, :, :], hot, wide(total), ALU.mult).then_inc(f.gates, 1)
        else:
            dve.wait_ge(f.exps, count(b, 1, 1))
            steps.done(dve.reduce_sum(total, ex, AX_X))
            steps.done(dve.reciprocal(total, total))
            steps.done(dve.tensor_tensor(ex, ex, wide(total), ALU.mult))
            steps.done(dve.reduce_max(peak, ex, AX_X))
            first_largest(ex, hot, peak, top)
            steps.done(dve.scalar_tensor_tensor(m.r_l[:, :], m.r_hot[:, :], -2.0, m.r_exp[:, :], ALU.mult, ALU.add))
            steps.done(dve.reduce_max(peak, lg, AX_X))
            first_largest(lg, two, peak, top)
            steps.done(dve.tensor_tensor(two, two, hot, ALU.add))
            steps.done(dve.tensor_tensor(ex, ex, two, ALU.mult))
            steps.done(dve.reduce_sum(total, ex, AX_X))
            steps.done(dve.tensor_scalar(total, total, 1e-12, None, ALU.max))
            steps.done(dve.reciprocal(total, total))
            dve.tensor_tensor(m.gates[:, :, :], ex, wide(total), ALU.mult).then_inc(f.gates, 1)
        dve.wait_ge(f.gates, count(b, 1, 1))
        for e in range(outs):
            dve.wait_ge(f.out, count(b, outs, e + 4))
            dve.wait_ge(f.added, count(b, outs, e + 2))
            out = m.bank[6 + (b[1] * outs + e) % 2]
            if e < E:
                for t in range(TILES):
                    last = dve.scalar_tensor_tensor(m.x[:, rows(b, t, 1)], out[:, t * P:(t + 1) * P], m.gates[:, t, e:e + 1],
                                                    m.x[:, rows(b, t, 1)], ALU.mult, ALU.add)
            else:
                last = dve.tensor_tensor(m.x[:, rows(b)], out[:, :], m.x[:, rows(b)], ALU.add)
            last.then_inc(f.added, 1)
            if e == E // 2:
                take_statistics(dve, nc, m, s, after(b, 1), stage, steps)

    over_batches(dve, body)




def rwkv_tensor(pe, nc, m, s, f, stage):
    pe.wait_ge(f.weights_mixed, 6)

    def body(b):
        h = b[1] % 2
        now, before = m.xt[:, h, 1:S + 1], m.xt[:, h, 0:S]
        transpose_batch(pe, nc, m, s, b, stage)
        xt_ready(pe, s, b, stage)
        for n in range(3):
            pe.matmul(m.bank[2 + n][:, :], f.w_now[:, n, :], now, start=True, stop=False)
            pe.matmul(m.bank[2 + n][:, :], f.w_before[:, n, :], before, start=False, stop=True).then_inc(f.kvr, 1)
        pe.wait_ge(f.mixed, count(b, 1, 1))
        pe.wait_ge(f.added, count(b, 1, 1))
        for t in range(TILES):
            last = pe.matmul(m.bank[1][:, t * P:(t + 1) * P], f.rw[:, t * P:(t + 1) * P], f.wo[:, :], start=True, stop=True)
        last.then_inc(f.out, 1)

    over_batches(pe, body)


def rwkv_scalar(act, nc, m, s, f, stage):
    act.wait_ge(f.decayed, 1)

    def body(b):
        keep_transposed(act, nc, m, s, b, stage)
        for n, func, scale in ((0, ACT.Copy, 1.0), (1, ACT.Copy, 1.0), (2, ACT.Tanh, 0.5)):
            act.wait_ge(f.kvr, count(b, 3, n + 1))
            act.activation(f.kvr_kept[:, n, :], m.bank[2 + n][:, :], func, scale=scale).then_inc(f.kept, 1)
        act.wait_ge(f.less, count(b, 2, 2))
        act.wait_ge(f.less_pool, count(b, 2, 2))
        act.activation(f.e[:, 0, :], f.d[:, 0, :], ACT.Exp, bias=f.decay[:, 1:2]).then_inc(f.exps, 1)
        act.activation(f.e[:, 1:4, :], f.d[:, 1:4, :], ACT.Exp).then_inc(f.exps, 1)
        act.wait_ge(f.below, count(b, 1, 1))
        act.activation(f.log[:, :], f.den[:, :], ACT.Ln).then_inc(f.logs, 1)
        act.wait_ge(f.logs, count(b, 1, 1))
        act.activation(f.inverse[:, :], f.log[:, :], ACT.Exp, scale=-1.0).then_inc(f.inverses, 1)

    over_batches(act, body)


def rwkv_vector(dve, nc, m, s, f, stage):
    credit(dve, f.added, 1)
    steps = Steps(dve, f.steps, 4 + 3)
    k, v, tanh_r = (f.kvr_kept[:, n, :] for n in range(3))
    u, old, new = f.first[:, :], f.largest[:, 0:S], f.largest[:, 1:S + 1]

    def body(b):
        steps.begin(b)
        dve.wait_ge(f.kept, count(b, 3, 1))
        dve.tensor_tensor_scan(new, f.decay[:, 1:2].to_broadcast([P, S]), k, -BIG, ALU.add, ALU.max).then_inc(f.maxima, 1)
        dve.wait_ge(f.maxima, count(b, 1, 1))
        dve.scalar_tensor_tensor(f.top[:, :], k, u, old, ALU.add, ALU.max).then_inc(f.tops, 1)
        dve.tensor_tensor(f.d[:, 1, :], k, new, ALU.subtract).then_inc(f.less, 1)
        dve.wait_ge(f.tops, count(b, 1, 1))
        dve.scalar_tensor_tensor(f.d[:, 3, :], k, u, f.top[:, :], ALU.add, ALU.subtract).then_inc(f.less, 1)
        dve.wait_ge(f.exps, count(b, 2, 2))
        dve.tensor_tensor_scan(f.sum_w[:, 1:S + 1], f.e[:, 0, :], f.e[:, 1, :], 0.0, ALU.mult, ALU.add).then_inc(f.sums, 1)
        steps.done(dve.tensor_tensor(f.ev[:, :], f.e[:, 1, :], v, ALU.mult))
        dve.tensor_tensor_scan(f.sum_wv[:, 1:S + 1], f.e[:, 0, :], f.ev[:, :], 0.0, ALU.mult, ALU.add).then_inc(f.sums, 1)
        dve.wait_ge(f.scaled, count(b, 2, 1))
        dve.tensor_tensor(f.den[:, :], f.ew[:, 0, :], f.e[:, 3, :], ALU.add).then_inc(f.below, 1)
        steps.done(dve.tensor_tensor(f.num[:, :], f.e[:, 3, :], v, ALU.mult))
        dve.wait_ge(f.scaled, count(b, 2, 2))
        steps.done(dve.tensor_tensor(f.num[:, :], f.ew[:, 1, :], f.num[:, :], ALU.add))
        steps.done(dve.scalar_tensor_tensor(f.num[:, :], tanh_r, 1.0, f.num[:, :], ALU.add, ALU.mult))
        dve.wait_ge(f.inverses, count(b, 1, 1))
        dve.scalar_tensor_tensor(f.rw[:, :], f.num[:, :], 0.5, f.inverse[:, :], ALU.mult, ALU.mult).then_inc(f.mixed, 1)
        dve.wait_ge(f.out, count(b, 1, 1))
        dve.tensor_tensor(m.x[:, rows(b)], m.bank[1][:, :], m.x[:, rows(b)], ALU.add).then_inc(f.added, 1)
        dve.wait_ge(f.added, count(b, 1, 2))
        take_statistics(dve, nc, m, s, after(b, 1), stage, steps)

    over_batches(dve, body)


def rwkv_pool(pool, nc, m, s, f, stage):
    old, new = f.largest[:, 0:S], f.largest[:, 1:S + 1]

    def body(b):
        normalise(pool, nc, m, s, b, stage)
        pool.wait_ge(f.maxima, count(b, 1, 1))
        pool.tensor_tensor(f.d[:, 0, :], old, new, ALU.subtract).then_inc(f.less_pool, 1)
        pool.wait_ge(f.tops, count(b, 1, 1))
        pool.tensor_tensor(f.d[:, 2, :], old, f.top[:, :], ALU.subtract).then_inc(f.less_pool, 1)
        for n, total in ((0, f.sum_w), (1, f.sum_wv)):
            pool.wait_ge(f.sums, count(b, 2, n + 1))
            pool.tensor_tensor(f.ew[:, n, :], f.e[:, 2, :], total[:, 0:S], ALU.mult).then_inc(f.scaled, 1)

    over_batches(pool, body)



NHEADS, HD = 16, 8
HALF_HEADS = NHEADS // 2
PAIRS = [(i, j) for i in range(3) for j in range(3)]
ONES = len(PAIRS) * HD
SLOTS = 16
RING = 3 + SLOTS * TILES
TAKE_QK = 4
STACKS = 16 * (2 * len(PAIRS) + 1)


def ring(b, n):
    return count(b, RING, 2 + n), 2 + (b[1] + n) % 2


def score_place(slot, tile, with_qk):
    n = 1 + slot * TILES + tile
    return n + 2 if slot >= TAKE_QK and with_qk else n


def rounds(eng, body):
    body((0, 0), None, None)
    body((0, 1), (0, 0), None)
    with eng.Fori(0, (BATCHES - 2) // 2) as loop:
        for half in range(2):
            body((loop, half + 2), (loop, half + 1), (loop, half))
    body(None, (0, BATCHES - 1), (0, BATCHES - 2))
    body(None, None, (0, BATCHES - 1))


def heads_fill_vector(dve, f):
    dve.memset(f.qs[64:P, :, :, :], 0.0)
    dve.memset(f.ks[64:P, :, :, :], 1.0).then_inc(f.stack_cleared, 1)


def heads_fill_pool(pool, f):
    pool.memset(f.nothing[:, :], 0.0)
    pool.memset(f.zero[:, :], 0.0)
    pool.memset(f.v[:, :, :, :, :], 0.0).then_inc(f.cleared, 1)
    pool.wait_ge(f.cleared, 1)
    pool.memset(f.v[:, :, :, :, HD:HD + 1], 1.0).then_inc(f.cleared, 1)
    pool.wait_ge(f.cleared, 2)


def heads_tensor(pe, nc, m, s, f, stage):
    credit(pe, f.scored, 4 * SLOTS)
    credit(pe, f.summed, 2)
    credit(pe, f.turned, 1)

    def take_qk(new, now):
        transpose_batch(pe, nc, m, s, new, stage)
        xt_ready(pe, s, new, stage)
        for n, w in ((0, f.wq), (1, f.wk)):
            value, bank = ring(now, 17 + n) if now else (n, 2 + n)
            pe.wait_ge(f.ring_read, value + 1)
            pe.matmul(m.bank[bank][:, :], w[:, :], m.xt[:, new[1] % 2, 1:S + 1], start=True, stop=True).then_inc(f.ring_made, 1)

    def take_v(now):
        value, bank = ring(now, 0)
        xt = m.xt[:, now[1] % 2, 1:S + 1]
        pe.wait_ge(f.ring_read, value + 1)
        for t in range(TILES):
            last = pe.matmul(m.bank[bank][:, t * P:(t + 1) * P], xt[:, t * P:(t + 1) * P], f.wv[:, :], start=True, stop=True)
        last.then_inc(f.ring_made, 1)

    def scores(now, head, tile, with_qk):
        value, bank = ring(now, score_place(head, tile, with_qk))
        h = now[1] % 2
        pe.wait_ge(f.ring_read, value + 1)
        pe.matmul(m.bank[bank][:, :], f.qs[:, h, head, tile * P:(tile + 1) * P], f.ks[:, h, head, :],
                  start=True, stop=True).then_inc(f.ring_made, 1)

    def shifted_scores(b, slot):
        group, tile, h = slot // 4, slot % 4, b[1] % 2
        for n in range(2):
            pe.wait_ge(f.exps, count(b, 2 * SLOTS, 2 * slot + n + 1))
            for j in (2 * n, 2 * n + 1):
                head = 4 * group + j
                last = pe.matmul(m.bank[4 + j][:, :], f.ks[:, h, head, tile * P:(tile + 1) * P], f.qs[:, h, head, :],
                                 start=True, stop=True)
            last.then_inc(f.scored, 1)

    def weighted_sums(b, slot):
        group, tile, h = slot // 4, slot % 4, b[1] % 2
        if tile == 0:
            pe.wait_ge(f.out_kept, count(b, 4, group + 1))
        pe.wait_ge(f.exps, count(b, 2 * SLOTS, 2 * slot + 2 + 2))
        for j in range(4):
            last = pe.matmul(m.bank[1][32 * j:32 * j + 32, :], f.v[:, h, tile, 4 * group + j, :], f.p[:, slot % 2, j, :],
                             start=tile == 0, stop=tile == 3)
        last.then_inc(f.summed, 1)

    def turn_maxima(b, half):
        pe.wait_ge(f.half_maxima, count(b, 2, half + 1))
        for t in range(TILES):
            last = pe.transpose(m.bank[0][0:HALF_HEADS, t * P:(t + 1) * P],
                                f.maxima[:, t, half * HALF_HEADS:(half + 1) * HALF_HEADS], m.ident[:, :])
        last.then_inc(f.maxima_turned, 1)

    def turn_sums(b, group):
        pe.wait_ge(f.out_kept, count(b, 4, group + 1 + 1))
        for t in range(TILES):
            last = pe.transpose(m.bank[0][:, t * P:(t + 1) * P], f.o[:, t * P:(t + 1) * P], m.ident[:, :])
        last.then_inc(f.turned, 1)

    def body(new, now, former):
        if now:
            take_v(now)
        for slot in range(SLOTS):
            if slot == TAKE_QK and new:
                if former:
                    pe.wait_ge(f.less_rests, count(former, 2, 2))
                take_qk(new, now)
            if now:
                if slot % HALF_HEADS == 0:
                    pe.wait_ge(f.stacked[slot // HALF_HEADS], count(now, STACKS, STACKS))
            for tile in range(TILES):
                if former and tile == 0:
                    if slot % HALF_HEADS == 0:
                        pe.wait_ge(f.lowered[slot // HALF_HEADS], count(former, 48, 48))
                    shifted_scores(former, slot)
                if now:
                    scores(now, slot, tile, bool(new))
            if former and slot:
                weighted_sums(former, slot - 1)
            if former and slot == 2:
                pe.wait_ge(f.added, count(former, 4, 1))
                turn_maxima(former, 1)
            if slot in (6, 10, 14) and former:
                group = slot // 4 - 1
                if group == 0:
                    pe.wait_ge(f.less_rests, count(former, 2, 2))
                pe.wait_ge(f.added, count(former, 4, group + 1))
                if group == 2 and now:
                    pe.wait_ge(f.less_rests, count(now, 2, 1))
                turn_sums(former, group)
            if now and slot == 12:
                if former:
                    pe.wait_ge(f.added, count(former, 4, 3))
                turn_maxima(now, 0)
        if former:
            weighted_sums(former, SLOTS - 1)
            pe.wait_ge(f.added, count(former, 4, 4))
            turn_sums(former, 3)

    rounds(pe, body)


def heads_scalar(act, nc, m, s, f, stage):
    credit(act, f.exps, 2)
    credit(act, f.out_kept, 1)

    def highs(new, now):
        keep_transposed(act, nc, m, s, new, stage)
        if new[1]:
            for half in range(2):
                act.wait_ge(f.stacked[half], count(new, STACKS, 0))
        for n in range(2):
            value, bank = ring(now, 17 + n) if now else (n, 2 + n)
            act.wait_ge(f.ring_made, value + 1)
            act.activation(f.part[:, n, 0, :], m.bank[bank][:, :], ACT.Copy).then_inc(f.highs, 1)

    def minus_maxima(b, half):
        act.wait_ge(f.maxima_turned, count(b, 2, half + 1))
        if half or b[1]:
            act.wait_ge(f.lowered[1 - half], count(b, 48, 48 * half))
        act.activation(f.less[:, 0, :], m.bank[0][0:HALF_HEADS, :], ACT.Copy, scale=-1.0).then_inc(f.less_highs, 1)

    def body(new, now, former):
        for slot in range(SLOTS):
            if slot == TAKE_QK and new:
                highs(new, now)
            if former:
                act.wait_ge(f.summed, count(former, SLOTS, slot + 1))
                for n in range(2):
                    act.wait_ge(f.scored, count(former, 2 * SLOTS, 4 * SLOTS + 2 * slot + n + 1))
                    act.activation(f.p[:, slot % 2, 2 * n:2 * n + 2, :], m.banks[:, 4 + 2 * n:6 + 2 * n, :], ACT.Exp,
                                   scale=1.0 / math.sqrt(HD)).then_inc(f.exps, 1)
                if slot and slot % 4 == 0:
                    keep_sums(former, slot // 4 - 1)
                if slot == 2:
                    minus_maxima(former, 1)
            if now and slot == 12:
                minus_maxima(now, 0)
        if former:
            keep_sums(former, 3)

    def keep_sums(b, group):
        act.wait_ge(f.summed, count(b, SLOTS, 2 + 4 * group + 4))
        act.wait_ge(f.turned, count(b, 4, group + 1))
        act.activation(f.o[:, :], m.bank[1][:, :], ACT.Copy).then_inc(f.out_kept, 1)

    rounds(act, body)


def heads_vector(dve, nc, m, s, f, stage):
    credit(dve, f.ring_read, 2)
    credit(dve, f.added, 1)
    steps = Steps(dve, f.steps, 4 * 2)

    def rests(new, now):
        for n in range(2):
            value, bank = ring(now, 17 + n) if now else (n, 2 + n)
            dve.wait_ge(f.highs, count(new, 2, n + 1))
            dve.tensor_tensor(f.rest[:, n, :], m.bank[bank][:, :], f.part[:, n, 0, :], ALU.subtract).then_inc(f.ring_read, 1)

    def keep_v(now):
        value, bank = ring(now, 0)
        dve.wait_ge(f.ring_made, value + 1)
        dve.tensor_copy(f.v[:, now[1] % 2, :, :, 0:HD], m.bank[bank][:, :].rearrange("p (t h d) -> p t h d", t=TILES, h=NHEADS)
                        ).then_inc(f.ring_read, 1)

    def maxima(now, head, with_qk):
        for tile in range(TILES):
            value, bank = ring(now, score_place(head, tile, with_qk))
            dve.wait_ge(f.ring_made, value + 1)
            dve.reduce_max(f.maxima[:, tile, head:head + 1], m.bank[bank][:, :], AX_X).then_inc(f.ring_read, 1)
        if head % HALF_HEADS == HALF_HEADS - 1:
            dve.wait_ge(f.ring_read, value + 1 + 2)
            dve.nop().then_inc(f.half_maxima, 1)

    def rest_of_maxima(b, half):
        dve.wait_ge(f.less_highs, count(b, 2, half + 1))
        dve.scalar_tensor_tensor(f.less_rest[:, :], m.bank[0][0:HALF_HEADS, :], -1.0, f.less[:, 0, :],
                                 ALU.mult, ALU.subtract).then_inc(f.less_rests, 1)

    def add_sums(b, group):
        o = m.bank[0][:, :].rearrange("p (t j c) -> p t j c", t=TILES, j=4)
        x = m.x[:, rows(b)].rearrange("p (t h d) -> p t h d", t=TILES, h=NHEADS)[:, :, 4 * group:4 * group + 4, :]
        dve.wait_ge(f.turned, count(b, 4, group + 1 + 1))
        steps.b, steps.n = b, 2 * group
        steps.done(dve.reciprocal(f.inverse[:, :, :], o[:, :, :, HD]))
        steps.done(dve.tensor_tensor(f.mean[:, :, :, :], o[:, :, :, 0:HD], f.inverse[:, :, :].unsqueeze(3).to_broadcast([P, TILES, 4, HD]),
                                     ALU.mult))
        dve.tensor_tensor(x, f.mean[:, :, :, :], x, ALU.add).then_inc(f.added, 1)
        dve.wait_ge(f.added, count(b, 4, group + 2))

    def body(new, now, former):
        if now:
            keep_v(now)
        for slot in range(SLOTS):
            if slot == TAKE_QK and new:
                rests(new, now)
            if now:
                maxima(now, slot, bool(new))
            if former and slot == 3:
                rest_of_maxima(former, 1)
            if former and slot in (7, 11, 15):
                add_sums(former, slot // 4 - 1)
            if now and slot == 13:
                rest_of_maxima(now, 0)
        if former:
            add_sums(former, 3)
        if new:
            ahead_steps.b, ahead_steps.n = new, 0
            take_statistics(dve, nc, m, s, after(new, 1), stage, ahead_steps)

    ahead_steps = Steps(dve, f.ahead_steps, 3)
    dve.wait_ge(f.cleared, 2)
    rounds(dve, body)


def heads_pool(pool, nc, m, s, f, stage):
    def less(b, half):
        pool.wait_ge(f.less_rests, count(b, 2, half + 1))
        pool.tensor_tensor(f.less[:, 1, :], f.less_rest[:, :], f.zero[0:HALF_HEADS, :].to_broadcast([HALF_HEADS, S]), ALU.add).then_inc(f.less_middles, 1)
        pool.wait_ge(f.less_middles, count(b, 2, half + 1))
        pool.tensor_tensor(f.less[:, 2, :], f.less_rest[:, :], f.less[:, 1, :], ALU.subtract).then_inc(f.less_parted, 1)

    def body(new, now, former):
        if new:
            normalise(pool, nc, m, s, new, stage)
        if former:
            less(former, 1)
        if new:
            value = ring(now, 19)[0] if now else 2
            pool.wait_ge(f.ring_read, value + 2)
            pool.tensor_tensor(f.part[:, :, 1, :], f.rest[:, :, :], f.zero[:, :].unsqueeze(2).to_broadcast([P, 2, S]), ALU.add).then_inc(f.middles, 1)
            pool.wait_ge(f.middles, count(new, 1, 1))
            pool.tensor_tensor(f.part[:, :, 2, :], f.rest[:, :, :], f.part[:, :, 1, :], ALU.subtract).then_inc(f.parted, 1)
        if now:
            less(now, 0)

    rounds(pool, body)


def heads_sync(sp, nc, m, s, f, stage):
    def stack(b, half):
        h, heads = b[1] % 2, slice(half * HALF_HEADS, (half + 1) * HALF_HEADS)
        free = sp.to_reg(count(b, 2 * SLOTS, SLOTS * (half + 1)))
        sp.wait_ge(f.parted, count(b, 1, 1))
        sp.wait_ge(f.scored, free)
        rows_of = slice(half * HALF_HEADS * HD, (half + 1) * HALF_HEADS * HD)
        for pair, parts in enumerate(PAIRS):
            for n, stacked in ((0, f.qs), (1, f.ks)):
                sp.dma_start(stacked[pair * HD:(pair + 1) * HD, h, heads, :],
                             f.part[rows_of, n, parts[n], :]).then_inc(f.stacked[half], 16)
        sp.dma_start(f.qs[ONES:ONES + 3, h, heads, :], f.nothing[0:3, :].unsqueeze(1).to_broadcast([3, HALF_HEADS, S])).then_inc(f.stacked[half], 16)

    def lower(b, half):
        h, heads = b[1] % 2, slice(half * HALF_HEADS, (half + 1) * HALF_HEADS)
        sp.wait_ge(f.less_parted, count(b, 2, half + 1))
        for part in range(3):
            sp.dma_start(f.qs[ONES + part:ONES + part + 1, h, heads, :], f.less[:, part, :]).then_inc(f.lowered[half], 16)

    def body(new, now, former):
        if former:
            lower(former, 1)
        if new:
            stack(new, 0)
        if now:
            lower(now, 0)
        if new:
            stack(new, 1)

    sp.wait_ge(f.stack_cleared, 1)
    sp.wait_ge(f.cleared, 2)
    rounds(sp, body)



DEVIATION = math.sqrt(0.25 * math.pi)
TINY = 2.0 ** -60
CENTRE = math.sqrt(0.5)


def laplace_tensor(pe, nc, m, s, f, stage):
    def body(b):
        xt = m.xt[:, b[1] % 2, 1:S + 1]
        transpose_batch(pe, nc, m, s, b, stage)
        xt_ready(pe, s, b, stage)
        for t in range(TILES):
            last = pe.matmul(m.bank[3][:, t * P:(t + 1) * P], xt[:, t * P:(t + 1) * P], f.wv[:, :], start=True, stop=True)
        last.then_inc(f.values, 1)
        pe.matmul(m.bank[2][:, :], f.wqk[:, :], xt, start=True, stop=True).then_inc(f.shared, 1)
        pe.wait_ge(f.queries, count(b, 1, 1))
        pe.wait_ge(f.keys, count(b, 1, 1))
        for j in range(TILES):
            pe.matmul(m.bank[4 + j][:, 0:S - j * P], f.k[:, j * P:(j + 1) * P], f.q[:, j * P:S],
                      start=True, stop=True).then_inc(f.scores, 1)
        pe.wait_ge(f.values_made, count(b, 1, 1))
        pe.wait_ge(f.added, count(b, 1, 1))
        pe.wait_ge(f.weights, count(b, TILES, TILES))
        for i in range(TILES):
            for j in range(i + 1):
                last = pe.matmul(m.bank[1][:, i * P:(i + 1) * P], f.p[:, j, (i - j) * P:(i - j + 1) * P],
                                 f.v[:, j * P:(j + 1) * P], start=j == 0, stop=j == i)
        last.then_inc(f.out, 1)

    over_batches(pe, body)


def laplace_scalar(act, nc, m, s, f, stage):
    def body(b):
        keep_transposed(act, nc, m, s, b, stage)
        act.wait_ge(f.values_biased, count(b, 1, 1))
        act.activation(f.sv[:, :], f.vb[:, :], ACT.Sigmoid).then_inc(f.value_gates, 1)
        act.wait_ge(f.shared, count(b, 1, 1))
        act.activation(f.sq[:, :], m.bank[2][:, :], ACT.Sigmoid, bias=f.bqk[:, :]).then_inc(f.gates, 1)
        for j in range(TILES):
            w = S - j * P
            act.wait_ge(f.arguments, count(b, TILES, j + 1))
            act.activation(f.sign[:, j, 0:w], f.y[:, j, 0:w], ACT.Sign)
            act.wait_ge(f.sizes, count(b, TILES, j + 1))
            act.activation(f.g[:, j, 0:w], f.size[:, j, 0:w], ACT.Gelu).then_inc(f.gelus, 1)

    over_batches(act, body)


def laplace_vector(dve, nc, m, s, f, stage):
    credit(dve, f.added, 1)
    dve.wait_ge(f.skewed, 16)
    steps = Steps(dve, f.steps, 1 + 4 * TILES + 3)

    def body(b):
        steps.begin(b)
        dve.wait_ge(f.values, count(b, 1, 1))
        dve.tensor_tensor(f.vb[:, :], m.bank[3][:, :], f.bv[:, :], ALU.add).then_inc(f.values_biased, 1)
        dve.wait_ge(f.gates, count(b, 1, 1))
        steps.done(dve.scalar_tensor_tensor(f.qk[:, :], m.bank[2][:, :], f.bqk[:, :], f.sq[:, :], ALU.add, ALU.mult))
        dve.tensor_scalar(f.q[:, :], f.qk[:, :], f.gb[:, 0:1], f.gb[:, 2:3], ALU.mult, ALU.add).then_inc(f.queries, 1)
        dve.tensor_scalar(f.k[:, :], f.qk[:, :], f.gb[:, 1:2], f.gb[:, 3:4], ALU.mult, ALU.add).then_inc(f.keys, 1)
        dve.wait_ge(f.value_gates, count(b, 1, 1))
        dve.tensor_tensor(f.v[:, :], f.vb[:, :], f.sv[:, :], ALU.mult).then_inc(f.values_made, 1)
        for j in range(TILES):
            w = S - j * P
            dve.wait_ge(f.scores, count(b, TILES, j + 1))
            dve.scalar_tensor_tensor(f.y[:, j, 0:w], m.bank[4 + j][:, 0:w], 1.0 / (S * DEVIATION),
                                     f.toeplitz[:, 0:w], ALU.mult, ALU.add).then_inc(f.arguments, 1)
            dve.wait_ge(f.arguments, count(b, TILES, j + 1))
            steps.done(dve.scalar_tensor_tensor(f.size[:, j, 0:w], f.y[:, j, 0:w], -1.0, f.y[:, j, 0:w], ALU.mult, ALU.max))
            dve.tensor_scalar(f.size[:, j, 0:w], f.size[:, j, 0:w], TINY, 8.0, ALU.max, ALU.min).then_inc(f.sizes, 1)
        for j in range(TILES):
            w = S - j * P
            dve.wait_ge(f.gelus, count(b, TILES, j + 1))
            steps.done(dve.reciprocal(f.size[:, j, 0:w], f.size[:, j, 0:w]))
            steps.done(dve.tensor_tensor(f.g[:, j, 0:w], f.g[:, j, 0:w], f.size[:, j, 0:w], ALU.mult))
            steps.done(dve.scalar_tensor_tensor(f.g[:, j, 0:w], f.g[:, j, 0:w], -0.5, f.sign[:, j, 0:w], ALU.add, ALU.mult))
            dve.scalar_tensor_tensor(f.p[:, j, 0:w], f.g[:, j, 0:w], 0.5, f.causal[:, 0:w],
                                     ALU.add, ALU.mult).then_inc(f.weights, 1)
        dve.wait_ge(f.out, count(b, 1, 1))
        dve.tensor_tensor(m.x[:, rows(b)], m.bank[1][:, :], m.x[:, rows(b)], ALU.add).then_inc(f.added, 1)
        dve.wait_ge(f.added, count(b, 1, 2))
        take_statistics(dve, nc, m, s, after(b, 1), stage, steps)

    over_batches(dve, body)



HALVES, GROUPS, STATES = 2, 16, 16
JUST = P // GROUPS
TAPS = 4
SMALL_EXP = 2.0 ** -7


def channel_group(i):
    return i % 4 * 4 + i // 4


def mamba_tensor(pe, nc, m, s, f, stage):
    NG = HALVES * GROUPS

    def spread(b, n):
        half, g = divmod(n, GROUPS)
        chosen = f.choose[:, channel_group(g), :]
        pe.wait_ge(f.decays, count(b, NG, n + 1))
        pe.matmul(m.bank[2 + n % 2][:, :], chosen, f.high[:, 0, half, :], start=True, stop=False)
        pe.matmul(m.bank[2 + n % 2][:, :], chosen, f.low[:, 0, half, :], start=False, stop=True).then_inc(f.spread, 1)
        pe.wait_ge(f.driven, count(b, NG, n + 1))
        pe.matmul(m.bank[4 + n % 2][:, :], chosen, f.high[:, 1, half, :], start=True, stop=False)
        pe.matmul(m.bank[4 + n % 2][:, :], chosen, f.low[:, 1, half, :], start=False, stop=True).then_inc(f.spread, 1)

    def add_states(b, n):
        half, g = divmod(n, GROUPS)
        quarter, within = g % 4, g // 4
        pe.wait_ge(f.weighed, count(b, NG, n + 1 + 4))
        pe.matmul(m.bank[6 + half][32 * quarter:32 * quarter + 32, :], f.gather[:, within, :], f.hc[:, n % 4, :],
                  start=within == 0, stop=within == 3).then_inc(f.summed, 1)

    def body(b):
        h = b[1] % 2
        xt = m.xt[:, h, 1:S + 1]
        transpose_batch(pe, nc, m, s, b, stage)
        xt_ready(pe, s, b, stage)
        pe.wait_ge(f.decays, count(b, NG, 2))
        pe.wait_ge(f.driven, count(b, NG, 2))
        for n in range(4):
            pe.matmul(m.bank[2 + n][:, :], f.w_in[:, n, :], xt, start=True, stop=True).then_inc(f.inner, 1)
        pe.wait_ge(f.x_made, count(b, 1, 1))
        pe.wait_ge(f.x_kept, count(b, 2, 2))
        for half in range(HALVES):
            last = pe.matmul(m.bank[2][0:JUST, :], f.w_dt[:, half, :], f.x[:, half, :], start=half == 0, stop=half == 1)
        last.then_inc(f.projected, 1)
        pe.wait_ge(f.ended, count(b, HALVES, 2))
        for n in range(2):
            for half in range(HALVES):
                last = pe.matmul(m.bank[6 + n][:, :], f.w_bc[:, half, n, :], f.x[:, half, :], start=half == 0, stop=half == 1)
            last.then_inc(f.projected, 1)
        pe.wait_ge(f.z_kept, count(b, 4, 4))
        pe.wait_ge(f.projections_kept, count(b, 3, 1))
        for half in range(HALVES):
            last = pe.matmul(m.bank[4 + half][:, :], f.w_delta[:, half, :], f.dt[:, :], start=True, stop=True)
        last.then_inc(f.delta_made, 1)
        pe.wait_ge(f.projections_kept, count(b, 3, 3))
        pe.wait_ge(f.highs, count(b, 2, 2))
        pe.wait_ge(f.lows, count(b, 2, 2))
        LAG = 3
        for n in range(NG + LAG):
            if n < NG:
                spread(b, n)
            if n >= LAG:
                add_states(b, n - LAG)
        pe.wait_ge(f.gated, count(b, 1, 1))
        pe.wait_ge(f.added, count(b, 1, 1))
        for t in range(TILES):
            for half in range(HALVES):
                last = pe.matmul(m.bank[1][:, t * P:(t + 1) * P], f.y[:, half, t * P:(t + 1) * P], f.w_out[:, half, :],
                                 start=half == 0, stop=half == 1)
        last.then_inc(f.out, 1)

    pe.wait_ge(f.chosen, 1)
    over_batches(pe, body)


def mamba_scalar(act, nc, m, s, f, stage):
    NG = HALVES * GROUPS
    credit(act, f.decays, 2)
    act.activation(f.rates[:, :], f.rates[:, :], ACT.Exp).then_inc(f.rate_exps, 1)
    act.wait_ge(f.rates_ready, 1)
    steps = Steps(act, f.scalar_steps, 2)

    def body(b):
        steps.begin(b)
        keep_transposed(act, nc, m, s, b, stage)
        for half in range(HALVES):
            act.wait_ge(f.inner, count(b, 4, half + 1))
            act.activation(f.padded[:, half, TAPS - 1:], m.bank[2 + half][:, :], ACT.Copy).then_inc(f.x_kept, 1)
        for half in range(HALVES):
            act.wait_ge(f.inner, count(b, 4, half + 3))
            act.activation(f.z_half[:, half, :], m.bank[4 + half][:, :], ACT.Copy, scale=0.5).then_inc(f.z_kept, 1)
            act.activation(f.z_tanh[:, half, :], m.bank[4 + half][:, :], ACT.Tanh, scale=0.5).then_inc(f.z_kept, 1)
        act.wait_ge(f.convolved, count(b, 1, 1))
        act.activation(f.x_tanh[:, :, :], f.conv[:, :, :], ACT.Tanh).then_inc(f.x_tanhs, 1)
        act.wait_ge(f.projected, count(b, 3, 1))
        act.activation(f.dt[:, :], m.bank[2][0:JUST, :], ACT.Copy).then_inc(f.projections_kept, 1)
        for n in range(2):
            act.wait_ge(f.projected, count(b, 3, n + 2))
            act.activation(f.bc[:, n, :], m.bank[6 + n][:, :], ACT.Copy).then_inc(f.projections_kept, 1)
        act.wait_ge(f.biased, count(b, 1, 1))
        steps.done(act.activation(f.small[:, :, :], f.v[:, :, :], ACT.Abs))
        steps.done(act.activation(f.small[:, :, :], f.small[:, :, :], ACT.Exp, scale=-1.0))
        act.activation(f.delta[:, :, :], f.small[:, :, :], ACT.Ln, bias=f.one[:, :]).then_inc(f.logs, 1)
        act.wait_ge(f.deltas, count(b, 1, 1))
        act.activation(f.high[:, 0, :, :], f.delta[:, :, :], ACT.Copy).then_inc(f.highs, 1)
        act.wait_ge(f.inputs, count(b, 1, 1))
        act.activation(f.high[:, 1, :, :], f.du[:, :, :], ACT.Copy).then_inc(f.highs, 1)
        for n in range(NG):
            half, g = divmod(n, GROUPS)
            act.wait_ge(f.spread, count(b, 2 * NG, 2 * n + 1))
            act.wait_ge(f.states, count(b, NG, n + 1))
            col = half * GROUPS + channel_group(g)
            act.activation(f.keep[:, n % 4, :], m.bank[2 + n % 2][:, :], ACT.Exp,
                           scale=f.rates[:, col:col + 1]).then_inc(f.decays, 1)

    over_batches(act, body)


def mamba_vector(dve, nc, m, s, f, stage):
    NG = HALVES * GROUPS
    dve.wait_ge(f.rate_exps, 1)
    dve.memset(f.one[:, :], 1.0)
    dve.memset(f.padded[:, :, 0:TAPS - 1], 0.0)
    dve.tensor_scalar(f.taps[:, :, :], f.taps[:, :, :], 0.5, None, ALU.mult)
    dve.wait_ge(f.raw_loaded, 16)
    dve.tensor_copy(f.choose[:, :, :], f.raw[:, :, :]).then_inc(f.chosen, 1)
    dve.tensor_scalar(f.rates[:, :], f.rates[:, :], -1.0, None, ALU.mult).then_inc(f.rates_ready, 1)
    dve.wait_ge(f.rates_ready, 1)
    credit(dve, f.driven, 2)
    credit(dve, f.states, 3)
    credit(dve, f.ended, 2)
    credit(dve, f.added, 1)
    steps = Steps(dve, f.steps, (TAPS - 1) + 4 + 2 + 3)

    def body(b):
        steps.begin(b)
        dve.wait_ge(f.x_kept, count(b, 2, 2))
        for k in range(TAPS):
            for half in range(HALVES):
                tap, out = f.padded[:, half, k:k + S], f.conv[:, half, :]
                w = f.taps[:, half, k:k + 1]
                if k == 0:
                    last = dve.tensor_scalar(out, tap, w, f.taps[:, half, TAPS:TAPS + 1], ALU.mult, ALU.add)
                else:
                    last = dve.scalar_tensor_tensor(out, tap, w, out, ALU.mult, ALU.add)
            if k < TAPS - 1:
                steps.done(last)
        last.then_inc(f.convolved, 1)
        dve.wait_ge(f.x_tanhs, count(b, 1, 1))
        dve.scalar_tensor_tensor(f.x[:, :, :], f.x_tanh[:, :, :], 1.0, f.conv[:, :, :], ALU.add, ALU.mult).then_inc(f.x_made, 1)
        dve.wait_ge(f.delta_made, count(b, 1, 1))
        for half in range(HALVES):
            last = dve.tensor_scalar(f.v[:, half, :], m.bank[4 + half][:, :], f.delta_bias[:, half:half + 1], None, ALU.add)
        last.then_inc(f.biased, 1)
        dve.wait_ge(f.logs, count(b, 1, 1))
        dve.wait_ge(f.z_kept, count(b, 4, 4))
        e, t = f.small[:, :, :], f.series[:, :, :]
        dve.tensor_scalar(f.is_small[:, :, :], e, SMALL_EXP, None, ALU.is_lt)
        steps.done(dve.tensor_scalar(t, e, 1.0 / 3, -0.5, ALU.mult, ALU.add))
        steps.done(dve.tensor_tensor(t, t, e, ALU.mult))
        steps.done(dve.scalar_tensor_tensor(t, t, 1.0, e, ALU.add, ALU.mult))
        dve.scalar_tensor_tensor(f.z[:, :, :], f.z_tanh[:, :, :], 1.0, f.z_half[:, :, :], ALU.add, ALU.mult)
        steps.done(dve.copy_predicated(f.delta[:, :, :], f.is_small[:, :, :], t))
        dve.scalar_tensor_tensor(f.delta[:, :, :], f.v[:, :, :], 0.0, f.delta[:, :, :], ALU.max, ALU.add).then_inc(f.deltas, 1)
        dve.wait_ge(f.deltas, count(b, 1, 1))
        dve.tensor_tensor(f.du[:, :, :], f.delta[:, :, :], f.x[:, :, :], ALU.mult).then_inc(f.inputs, 1)
        for n, whole in ((0, f.delta), (1, f.du)):
            dve.wait_ge(f.highs, count(b, 2, n + 1))
            dve.tensor_tensor(f.low[:, n, :, :], whole[:, :, :], f.high[:, n, :, :].bitcast(F32), ALU.subtract).then_inc(f.lows, 1)

        def drive(n):
            dve.wait_ge(f.spread, count(b, 2 * NG, 2 * n + 2))
            dve.tensor_tensor(f.drive[:, n % 4, :], m.bank[4 + n % 2][:, :], f.bc[:, 0, :], ALU.mult).then_inc(f.driven, 1)

        def scan(n):
            dve.wait_ge(f.decays, count(b, NG, n + 1 + 2))
            dve.wait_ge(f.driven, count(b, NG, n + 1 + 2))
            dve.wait_ge(f.weighed, count(b, NG, n + 1))
            dve.tensor_tensor_scan(f.state[:, n % 4, :], f.keep[:, n % 4, :], f.drive[:, n % 4, :], 0.0,
                                   ALU.mult, ALU.add).then_inc(f.states, 1)

        def end(half):
            dve.wait_ge(f.summed, count(b, NG, (half + 1) * GROUPS) + 0)
            steps.done(dve.scalar_tensor_tensor(f.y[:, half, :], f.x[:, half, :], f.skip[:, half:half + 1], m.bank[6 + half][:, :],
                                                ALU.mult, ALU.add))

        for n in range(NG + 1):
            if n < NG:
                drive(n)
            if n:
                scan(n - 1)
        for half in range(HALVES):
            end(half)
        dve.tensor_tensor(f.y[:, :, :], f.y[:, :, :], f.z[:, :, :], ALU.mult).then_inc(f.gated, 1)
        dve.nop().then_inc(f.ended, 2)
        dve.wait_ge(f.out, count(b, 1, 1))
        dve.tensor_tensor(m.x[:, rows(b)], m.bank[1][:, :], m.x[:, rows(b)], ALU.add).then_inc(f.added, 1)
        dve.wait_ge(f.added, count(b, 1, 2))
        take_statistics(dve, nc, m, s, after(b, 1), stage, steps)

    over_batches(dve, body)


def mamba_pool(pool, nc, m, s, f, stage):
    NG = HALVES * GROUPS
    credit(pool, f.weighed, 4)

    def body(b):
        normalise(pool, nc, m, s, b, stage)
        for n in range(NG):
            pool.wait_ge(f.states, count(b, NG, n + 1 + 3))
            if n > 3:
                pool.wait_ge(f.summed, count(b, NG, n - 3))
            pool.tensor_tensor(f.hc[:, n % 4, :], f.state[:, n % 4, :], f.bc[:, 1, :], ALU.mult).then_inc(f.weighed, 1)

    over_batches(pool, body)


def mamba_sync(sp, nc, a, f):
    sp.dma_start(f.raw[:, :, :], a["choose"]).then_inc(f.raw_loaded, 16)



RWKV, HEADS, LAPLACE, MAMBA, TOP1, TOP2 = "rwkv heads laplace mamba top1 top2".split()
STAGES = [RWKV, TOP1, HEADS, TOP1, LAPLACE, TOP2, MAMBA, TOP2]


WINDOW = S + P


def laplace_buffers(tmp, f):
    f.q, f.k, f.v, f.vb, f.sv, f.sq, f.qk = (tmp("lap_" + n, [P, S]) for n in "q k v vb sv sq qk".split())
    f.y, f.size, f.sign, f.g, f.p = (tmp("lap_" + n, [P, TILES, S]) for n in "y size sign g p".split())


def laplace_constants(nc, a, sb, sem, loads, setup, m):
    f = Names()
    f.values, f.shared, f.queries, f.keys, f.scores, f.values_made, f.added = (
        sem("lap_" + n) for n in "values shared queries keys scores values_made added".split())
    f.weights, f.out, f.values_biased, f.value_gates, f.gates, f.arguments, f.sizes = (
        sem("lap_" + n) for n in "weights out values_biased value_gates gates arguments sizes".split())
    f.gelus, f.steps, f.row, f.row_kept, f.rows_stored, f.skewed = (
        sem("lap_" + n) for n in "gelus steps row row_kept rows_stored skewed".split())
    f.wqk, f.wv, f.bqk, f.gb = sb("wqk", [P, P]), sb("wv", [P, P]), sb("bqk", [P, 1]), sb("gb", [P, 4])
    f.bv, f.toeplitz, f.causal = sb("bv", [P, S]), sb("toeplitz", [P, S]), sb("causal", [P, S])
    buckets, table, row = sb("buckets", [32, WINDOW]), sb("table", [32, 1]), sb("bias_row", [1, WINDOW])
    loads += [(f.wqk[:, :], a["wqk"]), (f.wv[:, :], a["wv"]), (f.bqk[:, :], a["bqk"]), (f.gb[:, :], a["gb"]),
              (f.bv[:, :], a["bv"].partition_broadcast(P)), (f.causal[:, :], a["causal"]),
              (buckets[:, :], a["buckets"]), (table[:, :], a["table"])]
    scratch = nc.dram_tensor("bias_rows", (P * WINDOW,), F32)
    half = WINDOW // 2

    def look_up(pe):
        for n in range(2):
            last = pe.matmul(m.bank[6 + n][0:1, 0:half], table[:, :], buckets[:, n * half:(n + 1) * half], start=True, stop=True)
        last.then_inc(f.row, 1)

    def scale(dve):
        dve.wait_ge(f.row, 1)
        for n in range(2):
            last = dve.tensor_scalar(row[:, n * half:(n + 1) * half], m.bank[6 + n][0:1, 0:half],
                                     math.sqrt(P) / DEVIATION, -CENTRE / DEVIATION, ALU.mult, ALU.add)
        last.then_inc(f.row_kept, 1)

    def skew(sp):
        sp.wait_ge(f.row_kept, 1)
        sp.dma_start(bass.AP(tensor=scratch, offset=0, ap=[[WINDOW, P], [1, WINDOW]]), row[0:1, :].unsqueeze(1).to_broadcast([1, P, WINDOW])).then_inc(f.rows_stored, 16)
        sp.wait_ge(f.rows_stored, 16)
        sp.dma_start(f.toeplitz[:, :], bass.AP(tensor=scratch, offset=P - 1, ap=[[WINDOW - 1, P], [1, S]])).then_inc(f.skewed, 16)

    setup.tensor.append(look_up)
    setup.vector.append(scale)
    setup.sync.append(skew)
    return f


def rwkv_memory(nc, a, sb, tmp, sem, loads, setup, m):
    f = Names()
    f.weights_mixed, f.decayed, f.kvr, f.kept, f.mixed, f.added, f.out = (
        sem("rwkv_" + n) for n in "weights_mixed decayed kvr kept mixed added out".split())
    f.less, f.less_pool, f.exps, f.below, f.logs, f.inverses, f.steps = (
        sem("rwkv_" + n) for n in "less less_pool exps below logs inverses steps".split())
    f.maxima, f.tops, f.sums, f.scaled, f.decay_exp, f.mixes, f.prepared = (
        sem("rwkv_" + n) for n in "maxima tops sums scaled decay_exp mixes prepared".split())
    f.w_now, f.w_before, f.wo = sb("w_now", [P, 3, P]), sb("w_before", [P, 3, P]), sb("wo", [P, P])
    f.mix, f.unmix, f.decay, f.first = sb("mix", [P, 3]), sb("unmix", [P, 3]), sb("decay", [P, 2]), sb("first", [P, 1])
    f.kvr_kept = tmp("kvr_kept", [P, 3, S])
    f.largest, f.sum_w, f.sum_wv = (tmp(n, [P, S + 1]) for n in ("largest", "sum_w", "sum_wv"))
    f.top, f.ev, f.num, f.den, f.log, f.inverse, f.rw = (tmp("rwkv_" + n, [P, S]) for n in "top ev num den log inverse rw".split())
    f.d, f.e, f.ew = tmp("less", [P, 4, S]), tmp("exps", [P, 4, S]), tmp("rwkv_ew", [P, 2, S])
    loads += [(f.w_now[:, :, :], a["wkvr"]), (f.wo[:, :], a["wo"]), (f.mix[:, :], a["mix"]), (f.decay[:, 0:1], a["decay"]),
              (f.first[:, :], a["first"])]

    def decay_scalar(act):
        act.activation(f.decay[:, 1:2], f.decay[:, 0:1], ACT.Exp).then_inc(f.decay_exp, 1)

    def mix_vector(dve):
        dve.wait_ge(f.decay_exp, 1)
        dve.tensor_scalar(f.decay[:, 1:2], f.decay[:, 1:2], -1.0, None, ALU.mult).then_inc(f.decayed, 1)
        dve.tensor_scalar(f.unmix[:, :], f.mix[:, :], -1.0, 1.0, ALU.mult, ALU.add).then_inc(f.mixes, 1)
        dve.wait_ge(f.mixes, 1)
        for n in range(3):
            dve.tensor_scalar(f.w_before[:, n, :], f.w_now[:, n, :], f.unmix[:, n:n + 1], None, ALU.mult).then_inc(f.weights_mixed, 1)
        dve.wait_ge(f.weights_mixed, 3)
        for n in range(3):
            dve.tensor_scalar(f.w_now[:, n, :], f.w_now[:, n, :], f.mix[:, n:n + 1], None, ALU.mult).then_inc(f.weights_mixed, 1)
        dve.memset(f.largest[:, 0:1], -BIG)
        dve.memset(f.sum_w[:, 0:1], 0.0)
        dve.memset(f.sum_wv[:, 0:1], 0.0).then_inc(f.prepared, 1)
        dve.wait_ge(f.prepared, 1)
        dve.wait_ge(f.decayed, 1)

    setup.scalar.append(decay_scalar)
    setup.vector.append(mix_vector)
    return f


def mamba_memory(nc, a, sb, tmp, sem, loads):
    f = Names()
    f.decays, f.spread, f.driven, f.weighed, f.summed, f.inner, f.x_made = (
        sem("mamba_" + n) for n in "decays spread driven weighed summed inner x_made".split())
    f.x_kept, f.projected, f.ended, f.z_kept, f.projections_kept, f.delta_made, f.highs = (
        sem("mamba_" + n) for n in "x_kept projected ended z_kept projections_kept delta_made highs".split())
    f.lows, f.gated, f.added, f.out, f.chosen, f.rates_ready, f.scalar_steps = (
        sem("mamba_" + n) for n in "lows gated added out chosen rates_ready scalar_steps".split())
    f.convolved, f.x_tanhs, f.biased, f.logs, f.deltas, f.inputs, f.states = (
        sem("mamba_" + n) for n in "convolved x_tanhs biased logs deltas inputs states".split())
    f.steps, f.rate_exps, f.raw_loaded = (
        sem("mamba_" + n) for n in "steps rate_exps raw_loaded".split())
    f.w_in, f.w_dt, f.w_bc = sb("w_in", [P, 4, P]), sb("w_dt", [P, HALVES, JUST]), sb("w_bc", [P, HALVES, 2, P])
    f.w_delta, f.w_out = sb("w_delta", [JUST, HALVES, P]), sb("w_out", [P, HALVES, P])
    f.taps, f.delta_bias, f.skip = sb("taps", [P, HALVES, TAPS + 1]), sb("delta_bias", [P, HALVES]), sb("skip", [P, HALVES])
    f.rates, f.one = sb("rates", [P, HALVES * GROUPS]), sb("one", [P, 1])
    f.choose, f.gather = sb("choose", [P, GROUPS, P], F32R), sb("gather", [P, 4, 32])
    f.raw = tmp("choose_raw", [P, GROUPS, P])
    f.padded = tmp("padded", [P, HALVES, TAPS - 1 + S])
    f.conv, f.x_tanh, f.z_half, f.z_tanh, f.z, f.x, f.v, f.small, f.series, f.delta, f.du, f.y = (
        tmp("m_" + n, [P, HALVES, S]) for n in "conv x_tanh z_half z_tanh z x v small series delta du y".split())
    f.is_small = tmp("is_small", [P, HALVES, S], mybir.dt.uint32)
    f.high, f.low = tmp("high", [P, 2, HALVES, S], F32R), tmp("low", [P, 2, HALVES, S], F32R)
    f.dt, f.bc = tmp("dt", [JUST, S]), tmp("bc", [P, 2, S])
    f.keep, f.drive, f.state, f.hc = (tmp("m_" + n, [P, 4, S]) for n in "keep drive state hc".split())
    loads += [(f.w_in[:, :, :], a["w_in"]), (f.w_dt[:, :, :], a["w_dt"]), (f.w_bc[:, :, :, :], a["w_bc"]),
              (f.w_delta[:, :, :], a["w_delta"]), (f.w_out[:, :, :], a["w_out"]), (f.taps[:, :, :], a["taps"]),
              (f.delta_bias[:, :], a["delta_bias"]), (f.skip[:, :], a["skip"]), (f.rates[:, :], a["a_log"]),
              (f.gather[:, :, :], a["gather"])]

    return f


def heads_weights(a, sb, sem, loads):
    f = Names()
    f.scored, f.summed, f.turned, f.ring_read, f.ring_made, f.exps, f.out_kept = (
        sem("heads_" + n) for n in "scored summed turned ring_read ring_made exps out_kept".split())
    f.half_maxima, f.maxima_turned, f.highs, f.less_highs, f.steps, f.ahead_steps, f.less_rests = (
        sem("heads_" + n) for n in "half_maxima maxima_turned highs less_highs steps ahead_steps less_rests".split())
    f.added, f.middles, f.parted, f.less_middles, f.less_parted, f.stacked0, f.stacked1 = (
        sem("heads_" + n) for n in "added middles parted less_middles less_parted stacked0 stacked1".split())
    f.lowered0, f.lowered1, f.cleared, f.stack_cleared = (
        sem("heads_" + n) for n in "lowered0 lowered1 cleared stack_cleared".split())
    f.stacked, f.lowered = (f.stacked0, f.stacked1), (f.lowered0, f.lowered1)
    f.wq, f.wk, f.wv = (sb("h_w" + n, [P, P]) for n in "qkv")
    loads += [(f.wq[:, :], a["h_wq"]), (f.wk[:, :], a["h_wk"]), (f.wv[:, :], a["h_wv"])]
    return f


def heads_buffers(tmp, f):
    BF16 = mybir.dt.bfloat16
    f.part, f.rest = tmp("part", [P, 2, 3, S], BF16), tmp("rest", [P, 2, S])
    f.less, f.less_rest = tmp("h_less", [HALF_HEADS, 3, S], BF16), tmp("less_rest", [HALF_HEADS, S])
    f.p, f.o = tmp("h_p", [P, 2, 4, S]), tmp("h_o", [P, S])
    f.maxima, f.inverse, f.mean = tmp("maxima", [P, TILES, NHEADS]), tmp("h_inverse", [P, TILES, 4]), tmp("h_mean", [P, TILES, 4, HD])
    f.qs, f.ks = (tmp(n, [P, 2, NHEADS, S], BF16) for n in ("qs", "ks"))
    f.zero = tmp("zero", [P, 1])
    f.nothing = tmp("nothing", [4, S], BF16)
    f.v = tmp("h_v", [P, 2, TILES, NHEADS, 32])


def build(nc, a, out, stages):
    ctx = ExitStack()
    with ctx:
        def sem(name):
            return ctx.enter_context(nc.semaphore(name))

        def into(stack):
            return lambda name, shape, dtype=F32: stack.enter_context(nc.sbuf_tensor(name, shape, dtype))

        sb = into(ctx)

        m = Names()
        m.banks = ctx.enter_context(nc.psum_tensor("banks", [P, 8, 512], F32))
        m.bank = [m.banks[:, i, :] for i in range(8)]
        m.x = sb("x", [P, BATCHES * S])
        m.ident = sb("ident", [P, P])
        m.minus_half = sb("minus_half", [P, TILES])
        m.bn = sb("bn", [P, 2, TILES, 6])
        m.mean_var = sb("mean_var", [P, 2, TILES, 2])
        m.half_stats = sb("half_stats", [P, 5, TILES])
        m.rstd = sb("rstd", [P, 2, TILES])
        m.xn = sb("xn", [P, 2, S])
        m.xt = sb("xt", [P, 2, S + 1])
        m.order = sb("order", [P, TILES * 8])
        m.r_l, m.r_d, m.r_exp, m.r_hot, m.r_two = (sb(n, [P, TILES * 8]) for n in ("r_l", "r_d", "r_exp", "r_hot", "r_two"))
        m.r_col = sb("r_col", [P, 3, TILES])
        m.gates = sb("gates", [P, TILES, 8])
        m.gates_t = sb("gates_t", [8, S])
        s = Names()
        s.loaded, s.filled, s.stats, s.rstd, s.centred, s.normed, s.transposed = (
            sem("s_" + n) for n in "loaded filled stats rstd centred normed transposed".split())
        s.xt, s.first_steps, s.stage, s.stored, s.late = (
            sem("s_" + n) for n in "xt first_steps stage stored late".split())

        loads, late_loads = [], []
        x_view = a["x"].rearrange("b (t p) d -> p b t d", p=P)
        for b in range(BATCHES):
            loads.append((by_tile(m.x[:, b * S:(b + 1) * S]), x_view[:, b]))
        loads += [(m.ident[:, :], a["ident"]), (m.order[:, :], a["order"])]

        plans = [None] * len(stages)
        setup = Names()
        setup.tensor, setup.vector, setup.scalar, setup.sync = [], [], [], []

        def experts_weights(pre, blocks, into, take):
            w = Names()
            w.w1 = into(pre + "w1", [P, 8, blocks * P])
            w.w2 = into(pre + "w2", [P, 8 * blocks * P])
            w.b1 = into(pre + "b1", [P, 8 * blocks])
            w.b2 = into(pre + "b2", [8, P])
            w.wr = into(pre + "wr", [P, 8])
            take += [(w.w1[:, :, :], a[pre + "w1"].rearrange("e d f -> d e f")),
                     (w.w2[:, :].rearrange("p (e j d) -> p e j d", e=8, j=blocks), a[pre + "w2"].rearrange("e (j p) d -> p e j d", p=P)),
                     (w.b1[:, :], a[pre + "b1"]), (w.b2[:, :], a[pre + "b2"]), (w.wr[:, :], a[pre + "wr"])]
            return w

        def experts_plan(n, w, blocks, top, func):
            f = Names()
            f.blocks, f.top, f.func = blocks, top, func
            f.w1, f.w2, f.b1, f.b2, f.wr = w.w1, w.w2, w.b1, w.b2, w.wr
            if top == 1:
                f.br = w.br
            f.gates_kept, f.logits, f.first, f.hidden, f.out, f.added, f.gates = (
                sem(f"st{n}_" + name) for name in "gates_kept logits first hidden out added gates".split())
            f.gates_turned, f.shifted, f.exps, f.steps = (
                sem(f"st{n}_" + name) for name in "gates_turned shifted exps steps".split())
            with ExitStack() as own:
                f.hid = into(own)(f"hid{n}", [P, 2, 4, S])
            plans[n] = (f, experts_tensor, experts_scalar, experts_vector, experts_pool)

        if LAPLACE in stages:
            lap = laplace_constants(nc, a, sb, sem, loads, setup, m)
        with ExitStack() as early:
            if TOP1 in stages:
                w = experts_weights("t1", 4, into(early), loads)
                br = into(early)("t1br", [P, TILES * 8])
                w.br = br[:, :]
                loads.append((w.br, a["t1br"].partition_broadcast(P)))
            if HEADS in stages:
                heads = heads_weights(a, into(early), sem, loads)
            if RWKV in stages:
                with ExitStack() as own:
                    f = rwkv_memory(nc, a, into(early), into(own), sem, loads, setup, m)
                    plans[stages.index(RWKV)] = (f, rwkv_tensor, rwkv_scalar, rwkv_vector, rwkv_pool)
            if HEADS in stages:
                with ExitStack() as own:
                    heads_buffers(into(own), heads)
                    plans[stages.index(HEADS)] = (heads, heads_tensor, heads_scalar, heads_vector, heads_pool)
            for n, kind in enumerate(stages):
                if kind == TOP1:
                    experts_plan(n, w, 4, 1, ACT.Gelu)
        if TOP2 in stages:
            w = experts_weights("t2", 2, sb, late_loads)
        if MAMBA in stages:
            with ExitStack() as own:
                mamba = mamba_memory(nc, a, sb, into(own), sem, late_loads)
                plans[stages.index(MAMBA)] = (mamba, mamba_tensor, mamba_scalar, mamba_vector, mamba_pool)
        for n, kind in enumerate(stages):
            if kind == TOP2:
                experts_plan(n, w, 2, 2, ACT.Relu)
        if LAPLACE in stages:
            with ExitStack() as own:
                laplace_buffers(into(own), lap)
                plans[stages.index(LAPLACE)] = (lap, laplace_tensor, laplace_scalar, laplace_vector, experts_pool)

        block = ctx.enter_context(nc.Block())

        def between(eng, n):
            eng.drain().then_inc(s.stage, 1)
            eng.wait_ge(s.stage, 4 * (n + 1))

        late = max([n + 1 for n, kind in enumerate(stages) if kind in (RWKV, TOP1, HEADS)], default=0)
        filling = stages.index(HEADS) - 1 if HEADS in stages else None

        def arrived(eng, kind, n):
            if kind in (TOP2, MAMBA) and late_loads:
                eng.wait_ge(s.late, 16 * len(late_loads))

        @block.sync
        def _(sp):
            for tile, dram in loads:
                sp.dma_start(tile, dram).then_inc(s.loaded, 16)
            for do in setup.sync:
                do(sp)
            if late_loads and late == 0:
                for tile, dram in late_loads:
                    sp.dma_start(tile, dram).then_inc(s.late, 16)
            for n, kind in enumerate(stages):
                if n:
                    sp.wait_ge(s.stage, 4 * n)
                if n == late and n:
                    for tile, dram in late_loads:
                        sp.dma_start(tile, dram).then_inc(s.late, 16)
                if kind == HEADS:
                    heads_sync(sp, nc, m, s, heads, n)
                if kind == MAMBA:
                    mamba_sync(sp, nc, a, mamba)
            sp.wait_ge(s.stage, 4 * len(stages))
            for b in range(BATCHES):
                sp.dma_start(out.rearrange("b (t p) d -> p b t d", p=P)[:, b], by_tile(m.x[:, b * S:(b + 1) * S])).then_inc(s.stored, 16)
            sp.wait_ge(s.stored, 16 * BATCHES)

        @block.tensor
        def _(pe):
            pe.wait_ge(s.loaded, 16 * len(loads))
            credit(pe, s.transposed, 2)
            for do in setup.tensor:
                do(pe)
            for n, (f, tensor, _, _, _) in enumerate(plans):
                arrived(pe, stages[n], n)
                tensor(pe, nc, m, s, f, n)
                between(pe, n)

        @block.scalar
        def _(act):
            act.wait_ge(s.loaded, 16 * len(loads))
            act.wait_ge(s.filled, 1)
            credit(act, s.xt, 1)
            for do in setup.scalar:
                do(act)
            for n, (f, _, scalar, _, _) in enumerate(plans):
                arrived(act, stages[n], n)
                scalar(act, nc, m, s, f, n)
                between(act, n)

        @block.vector
        def _(dve):
            dve.wait_ge(s.loaded, 16 * len(loads))
            first = Steps(dve, s.first_steps, 3)
            first.begin((0, 0))
            for do in setup.vector:
                do(dve)
            statistics_of(dve, nc, m, s, bass.ds(0, S), 0, first)
            if filling == -1:
                heads_fill_vector(dve, heads)
            for n, (f, _, _, vector, _) in enumerate(plans):
                if filling == n:
                    heads_fill_vector(dve, heads)
                arrived(dve, stages[n], n)
                vector(dve, nc, m, s, f, n)
                between(dve, n)

        @block.gpsimd
        def _(pool):
            pool.wait_ge(s.loaded, 16 * len(loads))
            pool.memset(m.minus_half[:, :], -0.5)
            pool.memset(m.xt[:, :, 0:1], 0.0).then_inc(s.filled, 1)
            pool.wait_ge(s.filled, 1)
            credit(pool, s.normed, 2)
            if filling == -1:
                heads_fill_pool(pool, heads)
            for n, (f, _, _, _, run) in enumerate(plans):
                if filling == n:
                    heads_fill_pool(pool, heads)
                arrived(pool, stages[n], n)
                run(pool, nc, m, s, f, n)
                between(pool, n)




def lay_out(i, np):
    def f(v):
        return np.ascontiguousarray(np.asarray(v))

    d = {"x": f(i["L0_attn_a_x"]), "ident": np.eye(P, dtype=np.float32)}
    d["order"] = f(np.tile(np.arange(8, 0, -1, dtype=np.float32), (P, TILES)))
    for pre, w1, b1, w2, b2, wr in (("t1", "L0_ffn_W1", "L0_ffn_b1", "L0_ffn_W2", "L0_ffn_b2", "L0_ffn_Wr"),
                                    ("t2", "L1_ffn_W1", "L1_ffn_b1", "L1_ffn_W2", "L1_ffn_b2", "L1_ffn_gate")):
        d[pre + "w1"], d[pre + "w2"], d[pre + "b2"], d[pre + "wr"] = f(i[w1]), f(i[w2]), f(i[b2]), f(i[wr])
        d[pre + "b1"] = f(np.asarray(i[b1]).reshape(-1, P).T)
    d["wqk"], d["wv"], d["table"] = f(i["L1_attn_a_wqk"]), f(i["L1_attn_a_wv"]), f(i["L1_attn_a_rel_bias"]).reshape(32, 1)
    d["bqk"] = f(i["L1_attn_a_bqk"]).reshape(P, 1)
    d["gb"] = f(np.concatenate([np.asarray(i["L1_attn_a_gamma"]), np.asarray(i["L1_attn_a_beta"])]).T)
    d["bv"] = f(np.tile(np.asarray(i["L1_attn_a_bv"]), TILES))
    key, query = np.arange(P)[:, None], np.arange(S)[None]
    d["causal"] = f(np.where(query >= key, np.float32(1), np.float32(0)))
    n = np.maximum(np.arange(WINDOW) - (P - 1), 0)
    large = 16 + (np.log(np.maximum(n, 1).astype(np.float32) / 16) / math.log(128 / 16) * 16).astype(np.int32)
    bucket = np.where(n < 16, n, np.minimum(large, 31))
    d["buckets"] = f((np.arange(32)[:, None] == bucket[None]).astype(np.float32))
    d["wkvr"] = f(np.stack([np.asarray(i["L0_attn_a_" + w]).T for w in ("Wk", "Wv", "Wr")], 1))
    d["wo"] = f(np.asarray(i["L0_attn_a_Wo"]).T)
    d["mix"] = f(np.stack([np.asarray(i["L0_attn_a_time_mix_" + w]).reshape(P) for w in "kvr"], 1))
    d["decay"], d["first"] = f(i["L0_attn_a_time_decay"]).reshape(P, 1), f(i["L0_attn_a_time_first"]).reshape(P, 1)
    w = {n: np.asarray(i["L1_attn_b_" + n]) for n in ("in_proj_w", "conv_w", "conv_b", "x_proj_w", "dt_proj_w", "dt_proj_b",
                                                       "A_log", "D", "out_proj_w")}
    d["w_in"] = f(w["in_proj_w"].reshape(4, P, P).transpose(2, 0, 1))
    by_half = w["x_proj_w"].T.reshape(HALVES, P, -1).transpose(1, 0, 2)
    d["w_dt"] = f(by_half[:, :, :JUST])
    d["w_bc"] = f(np.tile(by_half[:, :, JUST:].reshape(P, HALVES, 2, 1, STATES), (1, 1, 1, JUST, 1)).reshape(P, HALVES, 2, P))
    d["w_delta"] = f(w["dt_proj_w"].T.reshape(JUST, HALVES, P))
    d["w_out"] = f(w["out_proj_w"].T.reshape(HALVES, P, P).transpose(1, 0, 2))
    d["taps"] = f(np.concatenate([w["conv_w"][:, 0], w["conv_b"][:, None]], 1).reshape(HALVES, P, TAPS + 1).transpose(1, 0, 2))
    d["delta_bias"], d["skip"] = f(w["dt_proj_b"].reshape(HALVES, P).T), f(w["D"].reshape(HALVES, P).T)
    d["a_log"] = f(w["A_log"].reshape(HALVES * GROUPS, JUST * STATES).T)
    part, channel = np.arange(P), np.arange(P)
    d["choose"] = f((channel[:, None, None] == np.arange(GROUPS)[None, :, None] * JUST + part // STATES).astype(np.float32))
    d["gather"] = f((np.arange(32)[None, None] == np.arange(4)[None, :, None] * JUST + (part // STATES)[:, None, None]).astype(np.float32))
    for n in "qkv":
        w = np.asarray(i["L0_attn_b_W" + n]).T
        if n != "v":
            w = w.reshape(P, 2, HALF_HEADS, HD).transpose(0, 1, 3, 2).reshape(P, P)
        d["h_w" + n] = f(w)
    d["t1br"] = f(np.tile(np.asarray(i["L0_ffn_br"]), TILES))
    return d


def kernel(**inputs):
    import numpy as np
    import concourse.bacc as bacc
    from concourse.bass_utils import run_bass_kernel_spmd

    nc = bacc.Bacc("TRN2", target_bir_lowering=False, num_devices=1)
    arrays = {f"in_{k}": v for k, v in lay_out(inputs, np).items()}
    aps = {k[3:]: nc.dram_tensor(k, v.shape, mybir.dt.from_np(v.dtype), kind="ExternalInput").ap() for k, v in arrays.items()}
    out = nc.dram_tensor("out_x", (BATCHES, S, P), F32, kind="ExternalOutput").ap()
    build(nc, aps, out, STAGES)
    r = run_bass_kernel_spmd(nc, [arrays], core_ids=[0])
    return r.results[0]["out_x"]
```

```python
from contextlib import ExitStack
import math

import concourse.bass as bass
from concourse import mybir

F32 = mybir.dt.float32
F32R = mybir.dt.float32r
ALU = mybir.AluOpType
ACT = mybir.ActivationFunctionType
AX_X = mybir.AxisListType.X

P = 128
BATCHES = 8
S = 512
TILES = S // P
EPS = 1e-5
BIG = 1e30


class Names:
    pass


def count(b, per, n):
    loop, constant = b
    return loop * (2 * per) + (constant * per + n)


def after(b, n):
    return b[0], b[1] + n


def credit(eng, sem, n):
    eng.nop().then_inc(sem, n)


class Steps:

    def __init__(self, eng, sem, per):
        self.eng, self.sem, self.per, self.n = eng, sem, per, 0

    def begin(self, b):
        assert self.n in (0, self.per), (self.n, self.per)
        self.b, self.n = b, 0

    def mark(self, instruction):
        self.n += 1
        instruction.then_inc(self.sem, 1)

    def need(self):
        self.eng.wait_ge(self.sem, count(self.b, self.per, self.n))

    def done(self, instruction):
        self.mark(instruction)
        self.need()


class Beside:

    def __init__(self, steps):
        self.steps = steps
        self.turn = next(steps)

    def until(self, turn):
        while self.turn <= turn:
            self.turn = next(self.steps, BATCHES * S)


def rows(b, tile=0, tiles=TILES):
    loop, constant = b
    return bass.ds(loop * (2 * S) + (constant * S + tile * P), tiles * P)


def by_tile(ap):
    return ap.rearrange("p (t d) -> p t d", t=TILES)


def over_batches(eng, body):
    with eng.Fori(0, BATCHES // 2) as loop:
        for half in range(2):
            body((loop, half))


def rounds(eng, body):
    body((0, 0), None, None)
    body((0, 1), (0, 0), None)
    with eng.Fori(0, (BATCHES - 2) // 2) as loop:
        for half in range(2):
            body((loop, half + 2), (loop, half + 1), (loop, half))
    body(None, (0, BATCHES - 1), (0, BATCHES - 2))
    body(None, None, (0, BATCHES - 1))




def take_statistics(dve, nc, m, s, b, stage, steps):
    loop, n = b
    first = loop * (2 * S) + n * S if n < 2 else (loop * 2 + n) % BATCHES * S
    dve.wait_ge(s.normed, count(b, 1, 8 * stage + 1))
    statistics_of(dve, nc, m, s, bass.ds(first, S), n % 2, steps)


def statistics_of(dve, nc, m, s, columns, h, steps):
    x = m.x[:, columns]
    for t in range(TILES):
        last = dve.bn_stats(m.bn[:, h, t, :], x[:, t * P:(t + 1) * P])
    steps.done(last)
    even, odd, mv, half = m.bn[:, h, :, 0:3], m.bn[:, h, :, 3:6], m.mean_var[:, h], m.half_stats
    dve.tensor_tensor(half[:, 0, :], even[:, :, 1], odd[:, :, 1], ALU.add)
    dve.tensor_tensor(half[:, 1, :], even[:, :, 1], odd[:, :, 1], ALU.subtract)
    steps.done(dve.tensor_tensor(half[:, 2, :], even[:, :, 2], odd[:, :, 2], ALU.add))
    dve.tensor_scalar(mv[:, :, 0], half[:, 0, :], 0.5, None, ALU.mult)
    dve.scalar_tensor_tensor(half[:, 3, :], half[:, 1, :], 0.25, half[:, 1, :], ALU.mult, ALU.mult)
    steps.done(dve.tensor_scalar(half[:, 4, :], half[:, 2, :], 1.0 / P, EPS, ALU.mult, ALU.add))
    dve.tensor_tensor(mv[:, :, 1], half[:, 3, :], half[:, 4, :], ALU.add).then_inc(s.stats, 1)


def normalise(pool, nc, m, s, b, stage):
    h = b[1] % 2
    mv, rstd = m.mean_var[:, h], m.rstd[:, h]
    pool.wait_ge(s.stats, count(b, 1, 8 * stage + 1))
    pool.tensor_tensor(rstd, mv[:, :, 1], m.minus_half[:, :], ALU.pow).then_inc(s.rstd, 1)
    pool.wait_ge(s.transposed, count(b, 1, 8 * stage + 1))
    wide = [P, TILES, P]
    pool.tensor_tensor(by_tile(m.xn[:, h, :]), by_tile(m.x[:, rows(b)]), mv[:, :, 0:1].to_broadcast(wide),
                       ALU.subtract).then_inc(s.centred, 1)
    pool.wait_ge(s.rstd, count(b, 1, 8 * stage + 1))
    pool.wait_ge(s.centred, count(b, 1, 8 * stage + 1))
    pool.tensor_tensor(by_tile(m.xn[:, h, :]), by_tile(m.xn[:, h, :]), rstd.unsqueeze(2).to_broadcast(wide),
                       ALU.mult).then_inc(s.normed, 1)


def transpose_batch(pe, nc, m, s, b, stage):
    pe.wait_ge(s.normed, count(b, 1, 8 * stage + 3))
    pe.wait_ge(s.xt, count(b, 1, 8 * stage + 1))
    for t in range(TILES):
        last = pe.transpose(m.bank[0][:, t * P:(t + 1) * P], m.xn[:, b[1] % 2, t * P:(t + 1) * P], m.ident[:, :])
    last.then_inc(s.transposed, 1)


def keep_transposed(act, nc, m, s, b, stage):
    act.wait_ge(s.transposed, count(b, 1, 8 * stage + 3))
    act.activation(m.xt[:, b[1] % 2, 1:S + 1], m.bank[0][:, :], ACT.Copy).then_inc(s.xt, 1)


def xt_ready(eng, s, b, stage):
    eng.wait_ge(s.xt, count(b, 1, 8 * stage + 2))




def experts_tensor(pe, nc, m, s, f, stage):
    NB, E = f.blocks, 8
    outs = E + 1
    if f.use == 0:
        credit(pe, f.out, 3)

    def second_layer(b, u, e):
        h = b[1]
        pe.wait_ge(f.hidden, count(u, E * NB, (e + 1) * NB + 4))
        pe.wait_ge(f.added, count(u, outs, e + 1))
        out = m.bank[6 + (h * outs + e) % 2]
        for t in range(TILES):
            for j in range(NB):
                last = pe.matmul(out[:, t * P:(t + 1) * P], f.hid[:, e % 2, j, t * P:(t + 1) * P],
                                 f.w2[:, (e * NB + j) * P:(e * NB + j + 1) * P], start=j == 0, stop=j == NB - 1)
        last.then_inc(f.out, 1)

    def body(b):
        u = after(b, BATCHES * f.use)
        h = b[1]
        xt = m.xt[:, h, 1:S + 1]
        transpose_batch(pe, nc, m, s, b, stage)
        xt_ready(pe, s, b, stage)
        pe.wait_ge(f.gates_kept, count(u, 1, 1))
        for t in range(TILES):
            last = pe.matmul(m.bank[1][:, t * E:(t + 1) * E], xt[:, t * P:(t + 1) * P], f.wr[:, :], start=True, stop=True)
        last.then_inc(f.logits, 1)
        for e in range(E):
            if e == 0:
                pe.wait_ge(f.x_low, count(u, 1, 1))
            pe.wait_ge(f.split, 2 * E * f.use + E + e + 1)
            for j in range(NB):
                n = e * NB + j
                pe.wait_ge(f.hidden, count(u, E * NB, n + 1))
                out, block = m.bank[2 + n % 4][:, :], slice(j * P, (j + 1) * P)
                pe.matmul(out, f.w_high[:, e, block], f.xh[:, h, :], start=True, stop=False)
                pe.matmul(out, f.w_high[:, e, block], f.xl[:, h, :], start=False, stop=False)
                pe.matmul(out, f.w_low[:, e, block], f.xh[:, h, :], start=False, stop=True).then_inc(f.first, 1)
            if e:
                second_layer(b, u, e - 1)
        second_layer(b, u, E - 1)
        pe.wait_ge(f.gates, count(u, 1, 1))
        for t in range(TILES):
            last = pe.transpose(m.bank[1][0:E, t * P:(t + 1) * P], m.gates[:, t, :], m.ident[:, :])
        last.then_inc(f.gates_turned, 1)
        pe.wait_ge(f.gates_kept, count(u, 1, 2))
        pe.wait_ge(f.added, count(u, outs, E + 1))
        out = m.bank[6 + (h * outs + E) % 2]
        for t in range(TILES):
            last = pe.matmul(out[:, t * P:(t + 1) * P], m.gates_t[0:E, t * P:(t + 1) * P], f.b2[:, :], start=True, stop=True)
        last.then_inc(f.out, 1)

    over_batches(pe, body)


def experts_scalar(act, nc, m, s, f, stage):
    NB, E = f.blocks, 8
    outs = E + 1
    if f.use == 0:
        credit(act, f.hidden, 4)
        credit(act, f.gates_kept, 1)

    def body(b):
        u = after(b, BATCHES * f.use)
        act.wait_ge(s.transposed, count(b, 1, 8 * stage + 3))
        act.activation(f.xh[:, b[1] % 2, :], m.bank[0][:, :], ACT.Copy).then_inc(f.x_high, 1)
        keep_transposed(act, nc, m, s, b, stage)
        act.wait_ge(f.shifted, count(u, 1, 1))
        act.activation(m.r_exp[:, :], m.r_d[:, :], ACT.Exp).then_inc(f.exps, 1)
        for e in range(E):
            act.wait_ge(f.out, count(u, outs, e + 2 if e >= 2 else e + 1))
            for j in range(NB):
                n = e * NB + j
                act.wait_ge(f.first, count(u, E * NB, n + 1))
                act.activation(f.hid[:, e % 2, j, :], m.bank[2 + n % 4][:, :], f.func,
                               bias=f.b1[:, n:n + 1]).then_inc(f.hidden, 1)
        act.wait_ge(f.gates_turned, count(u, 1, 1))
        act.activation(m.gates_t[0:E, :], m.bank[1][0:E, :], ACT.Copy).then_inc(f.gates_kept, 1)

    over_batches(act, body)


def experts_pool(pool, nc, m, s, f, stage):
    over_batches(pool, lambda b: normalise(pool, nc, m, s, b, stage))


def experts_vector(dve, nc, m, s, f, stage):
    E = 8
    outs = E + 1
    if f.use == 0:
        credit(dve, f.added, 2)
    steps = Steps(dve, f.steps, 8 + 3 if f.top == 1 else 21 + 3)

    def wide(column):
        return column.unsqueeze(2).to_broadcast([P, TILES, E])

    order = m.order[:, :].rearrange("p (t e) -> p t e", e=E)

    def first_largest(source, hot, peak, top):
        steps.done(dve.tensor_tensor(hot, source, wide(peak), ALU.is_equal))
        steps.done(dve.tensor_tensor(hot, hot, order, ALU.mult))
        steps.done(dve.reduce_max(top, hot, AX_X))
        steps.done(dve.tensor_tensor(hot, hot, wide(top), ALU.is_equal))

    def body(b):
        u = after(b, BATCHES * f.use)
        steps.begin(u)
        lg, d, ex = (v.rearrange("p (t e) -> p t e", e=E) for v in (m.r_l[:, :], m.r_d[:, :], m.r_exp[:, :]))
        hot = m.r_hot[:, :].rearrange("p (t e) -> p t e", e=E)
        two = m.r_two[:, :].rearrange("p (t e) -> p t e", e=E)
        peak, top, total = m.r_col[:, 0, :], m.r_col[:, 1, :], m.r_col[:, 2, :]
        dve.wait_ge(f.x_high, count(u, 1, 1))
        xt_ready(dve, s, b, stage)
        dve.tensor_tensor(f.xl[:, b[1] % 2, :], m.xt[:, b[1] % 2, 1:S + 1], f.xh[:, b[1] % 2, :].bitcast(F32), ALU.subtract).then_inc(f.x_low, 1)
        dve.wait_ge(f.logits, count(u, 1, 1))
        ps = m.bank[1][:, 0:TILES * E]
        if f.top == 1:
            steps.done(dve.tensor_tensor(m.r_l[:, :], ps, f.br, ALU.add))
        else:
            steps.done(dve.tensor_copy(m.r_l[:, :], ps))
        steps.done(dve.reduce_max(peak, lg, AX_X))
        dve.tensor_tensor(d, lg, wide(peak), ALU.subtract).then_inc(f.shifted, 1)
        if f.top == 1:
            first_largest(lg, hot, peak, top)
            dve.wait_ge(f.exps, count(u, 1, 1))
            steps.done(dve.reduce_sum(total, ex, AX_X))
            steps.done(dve.reciprocal(total, total))
            dve.tensor_tensor(m.gates[:, :, :], hot, wide(total), ALU.mult).then_inc(f.gates, 1)
        else:
            dve.wait_ge(f.exps, count(u, 1, 1))
            steps.done(dve.reduce_sum(total, ex, AX_X))
            steps.done(dve.reciprocal(total, total))
            steps.done(dve.tensor_tensor(ex, ex, wide(total), ALU.mult))
            steps.done(dve.reduce_max(peak, ex, AX_X))
            first_largest(ex, hot, peak, top)
            steps.done(dve.scalar_tensor_tensor(m.r_l[:, :], m.r_hot[:, :], -2.0, m.r_exp[:, :], ALU.mult, ALU.add))
            steps.done(dve.reduce_max(peak, lg, AX_X))
            first_largest(lg, two, peak, top)
            steps.done(dve.tensor_tensor(two, two, hot, ALU.add))
            steps.done(dve.tensor_tensor(ex, ex, two, ALU.mult))
            steps.done(dve.reduce_sum(total, ex, AX_X))
            steps.done(dve.tensor_scalar(total, total, 1e-12, None, ALU.max))
            steps.done(dve.reciprocal(total, total))
            dve.tensor_tensor(m.gates[:, :, :], ex, wide(total), ALU.mult).then_inc(f.gates, 1)
        dve.wait_ge(f.gates, count(u, 1, 1))
        for e in range(outs):
            dve.wait_ge(f.out, count(u, outs, e + 4))
            dve.wait_ge(f.added, count(u, outs, e + 2))
            out = m.bank[6 + (b[1] * outs + e) % 2]
            if e < E:
                for t in range(TILES):
                    last = dve.scalar_tensor_tensor(m.x[:, rows(b, t, 1)], out[:, t * P:(t + 1) * P], m.gates[:, t, e:e + 1],
                                                    m.x[:, rows(b, t, 1)], ALU.mult, ALU.add)
            else:
                last = dve.tensor_tensor(m.x[:, rows(b)], out[:, :], m.x[:, rows(b)], ALU.add)
            last.then_inc(f.added, 1)
            if e == E // 2:
                take_statistics(dve, nc, m, s, after(b, 1), stage, steps)

    for e in range(E):
        dve.tensor_copy(f.w_high[:, e, :], f.w1[:, e, :]).then_inc(f.split, 1)
    dve.wait_ge(f.split, 2 * E * f.use + E)
    for e in range(E):
        dve.tensor_tensor(f.w_low[:, e, :], f.w1[:, e, :], f.w_high[:, e, :].bitcast(F32), ALU.subtract).then_inc(f.split, 1)
    over_batches(dve, body)






def rwkv_tensor(pe, nc, m, s, f, stage):
    pe.wait_ge(f.weights_mixed, 6)

    def body(new, now, former):
        if new:
            h = new[1] % 2
            after_it, before = m.xt[:, h, 1:S + 1], m.xt[:, h, 0:S]
            transpose_batch(pe, nc, m, s, new, stage)
            xt_ready(pe, s, new, stage)
            for n in range(3):
                if new[1]:
                    pe.wait_ge(f.kept, count(new, 3, n - 2))
                pe.matmul(m.bank[2 + n][:, :], f.w_now[:, n, :], after_it, start=True, stop=False)
                pe.matmul(m.bank[2 + n][:, :], f.w_before[:, n, :], before, start=False, stop=True).then_inc(f.kvr, 1)
        if now:
            pe.wait_ge(f.mixed, count(now, 1, 1))
            pe.wait_ge(f.added, count(now, 1, 1))
            for t in range(TILES):
                last = pe.matmul(m.bank[1][:, t * P:(t + 1) * P], f.rw[:, t * P:(t + 1) * P], f.wo[:, :], start=True, stop=True)
            last.then_inc(f.out, 1)

    rounds(pe, body)


def rwkv_scalar(act, nc, m, s, f, stage):
    act.wait_ge(f.decayed, 1)

    def body(new, now, former):
        if new:
            h = new[1] % 2
            keep_transposed(act, nc, m, s, new, stage)
            if former:
                act.wait_ge(f.mixed, count(former, 1, 1))
            for n, func, scale in ((0, ACT.Copy, 1.0), (1, ACT.Copy, 1.0), (2, ACT.Tanh, 0.5)):
                act.wait_ge(f.kvr, count(new, 3, n + 1))
                act.activation(f.kvr_kept[:, h, n, :], m.bank[2 + n][:, :], func, scale=scale).then_inc(f.kept, 1)
        if now:
            act.wait_ge(f.below, count(now, 1, 1))
            act.activation(f.log[:, :], f.den[:, :], ACT.Ln).then_inc(f.logs, 1)
            act.wait_ge(f.logs, count(now, 1, 1))
            act.activation(f.inverse[:, :], f.log[:, :], ACT.Exp, scale=-1.0).then_inc(f.inverses, 1)
        if new:
            act.wait_ge(f.less, count(new, 2, 2))
            act.wait_ge(f.less_pool, count(new, 2, 2))
            act.activation(f.e[:, h, 0, :], f.d[:, h, 0, :], ACT.Exp, bias=f.decay[:, 1:2]).then_inc(f.exps, 1)
            act.activation(f.e[:, h, 1:4, :], f.d[:, h, 1:4, :], ACT.Exp).then_inc(f.exps, 1)

    rounds(act, body)


def rwkv_vector(dve, nc, m, s, f, stage):
    credit(dve, f.added, 1)
    steps = Steps(dve, f.steps, 3)
    ahead = Steps(dve, f.ahead_steps, 3)
    u = f.first[:, :]

    def body(new, now, former):
        if now:
            h = now[1] % 2
            v, tanh_r = f.kvr_kept[:, h, 1, :], f.kvr_kept[:, h, 2, :]
            steps.begin(now)
            dve.wait_ge(f.exps, count(now, 2, 2))
            dve.tensor_tensor_scan(f.sum_w[:, h, 1:S + 1], f.e[:, h, 0, :], f.e[:, h, 1, :], 0.0, ALU.mult, ALU.add).then_inc(f.sums, 1)
            steps.done(dve.tensor_tensor(f.ev[:, :], f.e[:, h, 1, :], v, ALU.mult))
            dve.tensor_tensor_scan(f.sum_wv[:, h, 1:S + 1], f.e[:, h, 0, :], f.ev[:, :], 0.0, ALU.mult, ALU.add).then_inc(f.sums, 1)
        if former:
            dve.wait_ge(f.out, count(former, 1, 1))
            dve.tensor_tensor(m.x[:, rows(former)], m.bank[1][:, :], m.x[:, rows(former)], ALU.add).then_inc(f.added, 1)
        if now:
            dve.tensor_tensor(f.num[:, :], f.e[:, h, 3, :], v, ALU.mult).then_inc(f.terms, 1)
        if new:
            n = new[1] % 2
            k, old, largest = f.kvr_kept[:, n, 0, :], f.largest[:, n, 0:S], f.largest[:, n, 1:S + 1]
            dve.wait_ge(f.kept, count(new, 3, 1))
            dve.tensor_tensor_scan(largest, f.decay[:, 1:2].to_broadcast([P, S]), k, -BIG, ALU.add, ALU.max).then_inc(f.maxima, 1)
        if now:
            dve.wait_ge(f.scaled, count(now, 2, 1))
            dve.tensor_tensor(f.den[:, :], f.ew[:, 0, :], f.e[:, h, 3, :], ALU.add).then_inc(f.below, 1)
        if new:
            dve.wait_ge(f.maxima, count(new, 1, 1))
            dve.scalar_tensor_tensor(f.top[:, :], k, u, old, ALU.add, ALU.max).then_inc(f.tops, 1)
            dve.tensor_tensor(f.d[:, n, 1, :], k, largest, ALU.subtract).then_inc(f.less, 1)
            dve.wait_ge(f.tops, count(new, 1, 1))
            dve.scalar_tensor_tensor(f.d[:, n, 3, :], k, u, f.top[:, :], ALU.add, ALU.subtract).then_inc(f.less, 1)
        if now:
            dve.wait_ge(f.terms, count(now, 1, 1))
            dve.wait_ge(f.scaled, count(now, 2, 2))
            steps.done(dve.tensor_tensor(f.num[:, :], f.ew[:, 1, :], f.num[:, :], ALU.add))
            steps.done(dve.scalar_tensor_tensor(f.num[:, :], tanh_r, 1.0, f.num[:, :], ALU.add, ALU.mult))
            dve.wait_ge(f.inverses, count(now, 1, 1))
            dve.scalar_tensor_tensor(f.rw[:, :], f.num[:, :], 0.5, f.inverse[:, :], ALU.mult, ALU.mult).then_inc(f.mixed, 1)
        if new:
            if former:
                dve.wait_ge(f.added, count(former, 1, 2))
            ahead.begin(new)
            take_statistics(dve, nc, m, s, after(new, 1), stage, ahead)

    rounds(dve, body)


def rwkv_pool(pool, nc, m, s, f, stage):
    def body(new, now, former):
        if new:
            normalise(pool, nc, m, s, new, stage)
        if now:
            h = now[1] % 2
            for n, total in ((0, f.sum_w), (1, f.sum_wv)):
                pool.wait_ge(f.sums, count(now, 2, n + 1))
                pool.tensor_tensor(f.ew[:, n, :], f.e[:, h, 2, :], total[:, h, 0:S], ALU.mult).then_inc(f.scaled, 1)
        if new:
            h = new[1] % 2
            pool.wait_ge(f.maxima, count(new, 1, 1))
            pool.tensor_tensor(f.d[:, h, 0, :], f.largest[:, h, 0:S], f.largest[:, h, 1:S + 1], ALU.subtract).then_inc(f.less_pool, 1)
            pool.wait_ge(f.tops, count(new, 1, 1))
            pool.tensor_tensor(f.d[:, h, 2, :], f.largest[:, h, 0:S], f.top[:, :], ALU.subtract).then_inc(f.less_pool, 1)

    rounds(pool, body)



NHEADS, HD = 16, 8
HALF_HEADS = NHEADS // 2
PAIRS = [(i, j) for i in range(3) for j in range(3)]
ONES = len(PAIRS) * HD
SLOTS = 16
RING = 3 + SLOTS * TILES
TAKE_QK = 4
STACKS = 16 * (2 * len(PAIRS) + 1)


def ring(b, n):
    return count(b, RING, 2 + n), 2 + (b[1] + n) % 2


def score_place(slot, tile, with_qk):
    n = 1 + slot * TILES + tile
    return n + 2 if slot >= TAKE_QK and with_qk else n


def heads_fill(pool, s, f, stage):
    pool.wait_ge(s.normed, BATCHES * stage + 2)
    pool.memset(f.qs[64:P, :, :, :], 0.0).then_inc(f.stack_cleared, 1)
    pool.wait_ge(f.stack_cleared, 1)
    pool.memset(f.ks[64:P, :, :, :], 1.0).then_inc(f.stack_cleared, 1)
    pool.wait_ge(f.stack_cleared, 2)


def heads_tensor(pe, nc, m, s, f, stage):
    credit(pe, f.scored, 4 * SLOTS)
    credit(pe, f.summed, 2)
    credit(pe, f.turned, 1)

    def take_qk(new, now):
        transpose_batch(pe, nc, m, s, new, stage)
        xt_ready(pe, s, new, stage)
        for n, w in ((0, f.wq), (1, f.wk)):
            value, bank = ring(now, 17 + n) if now else (n, 2 + n)
            pe.wait_ge(f.ring_read, value + 1)
            pe.matmul(m.bank[bank][:, :], w[:, :], m.xt[:, new[1] % 2, 1:S + 1], start=True, stop=True).then_inc(f.ring_made, 1)

    def take_v(now):
        value, bank = ring(now, 0)
        xt = m.xt[:, now[1] % 2, 1:S + 1]
        pe.wait_ge(f.ring_read, value + 1)
        for t in range(TILES):
            last = pe.matmul(m.bank[bank][:, t * P:(t + 1) * P], xt[:, t * P:(t + 1) * P], f.wv[:, :], start=True, stop=True)
        last.then_inc(f.ring_made, 1)

    def scores(now, head, tile, with_qk):
        value, bank = ring(now, score_place(head, tile, with_qk))
        h = now[1] % 2
        pe.wait_ge(f.ring_read, value + 1)
        pe.matmul(m.bank[bank][:, :], f.qs[:, h, head, tile * P:(tile + 1) * P], f.ks[:, h, head, :],
                  start=True, stop=True).then_inc(f.ring_made, 1)

    def shifted_scores(b, slot):
        group, tile, h = slot // 4, slot % 4, b[1] % 2
        for n in range(2):
            pe.wait_ge(f.exps, count(b, 2 * SLOTS, 2 * slot + n + 1))
            for j in (2 * n, 2 * n + 1):
                head = 4 * group + j
                last = pe.matmul(m.bank[4 + j][:, :], f.ks[:, h, head, tile * P:(tile + 1) * P], f.qs[:, h, head, :],
                                 start=True, stop=True)
            last.then_inc(f.scored, 1)

    def weighted_sums(b, slot):
        group, tile, h = slot // 4, slot % 4, b[1] % 2
        if tile == 0:
            pe.wait_ge(f.out_kept, count(b, 4, group + 1))
        pe.wait_ge(f.exps, count(b, 2 * SLOTS, 2 * slot + 2 + 2))
        for j in range(4):
            last = pe.matmul(m.bank[1][32 * j:32 * j + 32, :], f.v[:, h, tile, 4 * group + j, :], f.p[:, slot % 2, j, :],
                             start=tile == 0, stop=tile == 3)
        last.then_inc(f.summed, 1)

    def turn_maxima(b, half):
        pe.wait_ge(f.half_maxima, count(b, 2, half + 1))
        for t in range(TILES):
            last = pe.transpose(m.bank[0][0:HALF_HEADS, t * P:(t + 1) * P],
                                f.maxima[:, t, half * HALF_HEADS:(half + 1) * HALF_HEADS], m.ident[:, :])
        last.then_inc(f.maxima_turned, 1)

    def turn_sums(b, group):
        pe.wait_ge(f.out_kept, count(b, 4, group + 1 + 1))
        for t in range(TILES):
            last = pe.transpose(m.bank[0][:, t * P:(t + 1) * P], f.o[:, t * P:(t + 1) * P], m.ident[:, :])
        last.then_inc(f.turned, 1)

    def body(new, now, former):
        if now:
            take_v(now)
        for slot in range(SLOTS):
            if slot == TAKE_QK and new:
                if former:
                    pe.wait_ge(f.less_rests, count(former, 2, 2))
                take_qk(new, now)
            if now:
                if slot % HALF_HEADS == 0:
                    pe.wait_ge(f.stacked[slot // HALF_HEADS], count(now, STACKS, STACKS))
            for tile in range(TILES):
                if former and tile == 0:
                    if slot % HALF_HEADS == 0:
                        pe.wait_ge(f.lowered[slot // HALF_HEADS], count(former, 48, 48))
                    shifted_scores(former, slot)
                if now:
                    scores(now, slot, tile, bool(new))
            if former and slot:
                weighted_sums(former, slot - 1)
            if former and slot == 2:
                pe.wait_ge(f.added, count(former, 4, 1))
                turn_maxima(former, 1)
            if slot in (6, 10, 14) and former:
                group = slot // 4 - 1
                if group == 0:
                    pe.wait_ge(f.less_rests, count(former, 2, 2))
                pe.wait_ge(f.added, count(former, 4, group + 1))
                if group == 2 and now:
                    pe.wait_ge(f.less_rests, count(now, 2, 1))
                turn_sums(former, group)
            if now and slot == 12:
                if former:
                    pe.wait_ge(f.added, count(former, 4, 3))
                turn_maxima(now, 0)
        if former:
            weighted_sums(former, SLOTS - 1)
            pe.wait_ge(f.added, count(former, 4, 4))
            turn_sums(former, 3)

    rounds(pe, body)


def heads_scalar(act, nc, m, s, f, stage):
    credit(act, f.exps, 2)
    credit(act, f.out_kept, 1)

    def highs(new, now):
        keep_transposed(act, nc, m, s, new, stage)
        if new[1]:
            for half in range(2):
                act.wait_ge(f.stacked[half], count(new, STACKS, 0))
        for n in range(2):
            value, bank = ring(now, 17 + n) if now else (n, 2 + n)
            act.wait_ge(f.ring_made, value + 1)
            act.activation(f.part[:, n, 0, :], m.bank[bank][:, :], ACT.Copy).then_inc(f.highs, 1)

    def minus_maxima(b, half):
        act.wait_ge(f.maxima_turned, count(b, 2, half + 1))
        if half or b[1]:
            act.wait_ge(f.lowered[1 - half], count(b, 48, 48 * half))
        act.activation(f.less[:, 0, :], m.bank[0][0:HALF_HEADS, :], ACT.Copy, scale=-1.0).then_inc(f.less_highs, 1)

    def body(new, now, former):
        for slot in range(SLOTS):
            if slot == TAKE_QK and new:
                highs(new, now)
            if former:
                act.wait_ge(f.summed, count(former, SLOTS, slot + 1))
                for n in range(2):
                    act.wait_ge(f.scored, count(former, 2 * SLOTS, 4 * SLOTS + 2 * slot + n + 1))
                    act.activation(f.p[:, slot % 2, 2 * n:2 * n + 2, :], m.banks[:, 4 + 2 * n:6 + 2 * n, :], ACT.Exp,
                                   scale=1.0 / math.sqrt(HD)).then_inc(f.exps, 1)
                if slot and slot % 4 == 0:
                    keep_sums(former, slot // 4 - 1)
                if slot == 2:
                    minus_maxima(former, 1)
            if now and slot == 12:
                minus_maxima(now, 0)
        if former:
            keep_sums(former, 3)

    def keep_sums(b, group):
        act.wait_ge(f.summed, count(b, SLOTS, 2 + 4 * group + 4))
        act.wait_ge(f.turned, count(b, 4, group + 1))
        act.activation(f.o[:, :], m.bank[1][:, :], ACT.Copy).then_inc(f.out_kept, 1)

    rounds(act, body)


def heads_vector(dve, nc, m, s, f, stage):
    credit(dve, f.ring_read, 2)
    credit(dve, f.added, 1)
    steps = Steps(dve, f.steps, 4 * 2)

    def rests(new, now):
        for n in range(2):
            value, bank = ring(now, 17 + n) if now else (n, 2 + n)
            dve.wait_ge(f.highs, count(new, 2, n + 1))
            dve.tensor_tensor(f.rest[:, n, :], m.bank[bank][:, :], f.part[:, n, 0, :], ALU.subtract).then_inc(f.ring_read, 1)

    def keep_v(now):
        value, bank = ring(now, 0)
        dve.wait_ge(f.ring_made, value + 1)
        dve.tensor_copy(f.v[:, now[1] % 2, :, :, 0:HD], m.bank[bank][:, :].rearrange("p (t h d) -> p t h d", t=TILES, h=NHEADS)
                        ).then_inc(f.ring_read, 1)

    def maxima(now, head, with_qk):
        for tile in range(TILES):
            value, bank = ring(now, score_place(head, tile, with_qk))
            dve.wait_ge(f.ring_made, value + 1)
            dve.reduce_max(f.maxima[:, tile, head:head + 1], m.bank[bank][:, :], AX_X).then_inc(f.ring_read, 1)
        if head % HALF_HEADS == HALF_HEADS - 1:
            dve.wait_ge(f.ring_read, value + 1 + 2)
            dve.nop().then_inc(f.half_maxima, 1)

    def rest_of_maxima(b, half):
        dve.wait_ge(f.less_highs, count(b, 2, half + 1))
        dve.scalar_tensor_tensor(f.less_rest[:, :], m.bank[0][0:HALF_HEADS, :], -1.0, f.less[:, 0, :],
                                 ALU.mult, ALU.subtract).then_inc(f.less_rests, 1)

    def add_sums(b, group):
        o = m.bank[0][:, :].rearrange("p (t j c) -> p t j c", t=TILES, j=4)
        x = m.x[:, rows(b)].rearrange("p (t h d) -> p t h d", t=TILES, h=NHEADS)[:, :, 4 * group:4 * group + 4, :]
        dve.wait_ge(f.turned, count(b, 4, group + 1 + 1))
        steps.b, steps.n = b, 2 * group
        steps.done(dve.reciprocal(f.inverse[:, :, :], o[:, :, :, HD]))
        steps.done(dve.tensor_tensor(f.mean[:, :, :, :], o[:, :, :, 0:HD], f.inverse[:, :, :].unsqueeze(3).to_broadcast([P, TILES, 4, HD]),
                                     ALU.mult))
        dve.tensor_tensor(x, f.mean[:, :, :, :], x, ALU.add).then_inc(f.added, 1)
        dve.wait_ge(f.added, count(b, 4, group + 2))

    def body(new, now, former):
        if now:
            keep_v(now)
        for slot in range(SLOTS):
            if slot == TAKE_QK and new:
                rests(new, now)
            if now:
                maxima(now, slot, bool(new))
            if former and slot == 3:
                rest_of_maxima(former, 1)
            if former and slot in (7, 11, 15):
                add_sums(former, slot // 4 - 1)
            if now and slot == 13:
                rest_of_maxima(now, 0)
        if former:
            add_sums(former, 3)
        if new:
            ahead_steps.b, ahead_steps.n = new, 0
            take_statistics(dve, nc, m, s, after(new, 1), stage, ahead_steps)

    ahead_steps = Steps(dve, f.ahead_steps, 3)
    dve.memset(f.v[:, :, :, :, :], 0.0).then_inc(f.cleared, 1)
    dve.wait_ge(f.cleared, 1)
    dve.memset(f.v[:, :, :, :, HD:HD + 1], 1.0).then_inc(f.cleared, 1)
    dve.wait_ge(f.cleared, 2)
    rounds(dve, body)


def heads_pool(pool, nc, m, s, f, stage):
    def less(b, half):
        pool.wait_ge(f.less_rests, count(b, 2, half + 1))
        pool.tensor_tensor(f.less[:, 1, :], f.less_rest[:, :], f.zero[0:HALF_HEADS, :].to_broadcast([HALF_HEADS, S]), ALU.add).then_inc(f.less_middles, 1)
        pool.wait_ge(f.less_middles, count(b, 2, half + 1))
        pool.tensor_tensor(f.less[:, 2, :], f.less_rest[:, :], f.less[:, 1, :], ALU.subtract).then_inc(f.less_parted, 1)

    def body(new, now, former):
        if new:
            normalise(pool, nc, m, s, new, stage)
        if former:
            less(former, 1)
        if new:
            value = ring(now, 19)[0] if now else 2
            pool.wait_ge(f.ring_read, value + 2)
            pool.tensor_tensor(f.part[:, :, 1, :], f.rest[:, :, :], f.zero[:, :].unsqueeze(2).to_broadcast([P, 2, S]), ALU.add).then_inc(f.middles, 1)
            pool.wait_ge(f.middles, count(new, 1, 1))
            pool.tensor_tensor(f.part[:, :, 2, :], f.rest[:, :, :], f.part[:, :, 1, :], ALU.subtract).then_inc(f.parted, 1)
        if now:
            less(now, 0)

    pool.memset(f.nothing[:, :], 0.0)
    pool.memset(f.zero[:, :], 0.0).then_inc(f.zeroed, 1)
    pool.wait_ge(f.zeroed, 1)
    rounds(pool, body)


def heads_sync(sp, nc, m, s, f, stage):
    def stack(b, half):
        h, heads = b[1] % 2, slice(half * HALF_HEADS, (half + 1) * HALF_HEADS)
        free = sp.to_reg(count(b, 2 * SLOTS, SLOTS * (half + 1)))
        sp.wait_ge(f.parted, count(b, 1, 1))
        sp.wait_ge(f.scored, free)
        rows_of = slice(half * HALF_HEADS * HD, (half + 1) * HALF_HEADS * HD)
        for pair, parts in enumerate(PAIRS):
            for n, stacked in ((0, f.qs), (1, f.ks)):
                sp.dma_start(stacked[pair * HD:(pair + 1) * HD, h, heads, :],
                             f.part[rows_of, n, parts[n], :]).then_inc(f.stacked[half], 16)
        sp.dma_start(f.qs[ONES:ONES + 3, h, heads, :], f.nothing[0:3, :].unsqueeze(1).to_broadcast([3, HALF_HEADS, S])).then_inc(f.stacked[half], 16)

    def lower(b, half):
        h, heads = b[1] % 2, slice(half * HALF_HEADS, (half + 1) * HALF_HEADS)
        sp.wait_ge(f.less_parted, count(b, 2, half + 1))
        for part in range(3):
            sp.dma_start(f.qs[ONES + part:ONES + part + 1, h, heads, :], f.less[:, part, :]).then_inc(f.lowered[half], 16)

    def body(new, now, former):
        if former:
            lower(former, 1)
        if new:
            stack(new, 0)
        if now:
            lower(now, 0)
        if new:
            stack(new, 1)

    sp.wait_ge(f.stack_cleared, 2)
    sp.wait_ge(f.zeroed, 1)
    rounds(sp, body)



DEVIATION = math.sqrt(0.25 * math.pi)
TINY = 2.0 ** -24
CENTRE = math.sqrt(0.5)
STARTS = [sum(S - i * P for i in range(j)) for j in range(TILES + 1)]
PAIRED = STARTS[TILES]


def laplace_tensor(pe, nc, m, s, f, stage):
    def body(new, now, former):
        if new:
            xt = m.xt[:, new[1] % 2, 1:S + 1]
            transpose_batch(pe, nc, m, s, new, stage)
            xt_ready(pe, s, new, stage)
            if new[1]:
                pe.wait_ge(f.queries, count(new, 1, 0))
            pe.matmul(m.bank[2][:, :], f.wqk[:, :], xt, start=True, stop=True).then_inc(f.shared, 1)
            if new[1]:
                pe.wait_ge(f.values_biased, count(new, 1, 0))
            for t in range(TILES):
                last = pe.matmul(m.bank[3][:, t * P:(t + 1) * P], xt[:, t * P:(t + 1) * P], f.wv[:, :], start=True, stop=True)
            last.then_inc(f.values, 1)
            pe.wait_ge(f.queries, count(new, 1, 1))
            pe.wait_ge(f.keys, count(new, 1, 1))
            if new[1]:
                pe.wait_ge(f.arguments, count(new, TILES, 0))
            for j in range(TILES):
                pe.matmul(m.bank[4 + j][:, 0:S - j * P], f.k[:, j * P:(j + 1) * P], f.q[:, j * P:S],
                          start=True, stop=True).then_inc(f.scores, 1)
        if now:
            h = now[1] % 2
            pe.wait_ge(f.values_made, count(now, 1, 1))
            pe.wait_ge(f.added, count(now, 1, 1))
            pe.wait_ge(f.weights, count(now, 2, 2))
            for i in range(TILES):
                for j in range(i + 1):
                    at = STARTS[j] + (i - j) * P
                    last = pe.matmul(m.bank[1][:, i * P:(i + 1) * P], f.p[:, at:at + P],
                                     f.v[:, h, j * P:(j + 1) * P], start=j == 0, stop=j == i)
            last.then_inc(f.out, 1)

    rounds(pe, body)


def laplace_scalar(act, nc, m, s, f, stage):
    steps = Steps(act, f.scalar_steps, 1)

    def body(new, now, former):
        if now:
            h = now[1] % 2
            if former:
                act.wait_ge(f.weights, count(former, 2, 2))
            act.wait_ge(f.sizes, count(now, 1, 1))
            act.activation(f.g[:, :], f.size[:, h, :], ACT.Gelu).then_inc(f.gelus, 1)
            steps.begin(now)
            steps.done(act.activation(f.inverse[:, :], f.size[:, h, :], ACT.Ln))
            act.activation(f.inverse[:, :], f.inverse[:, :], ACT.Exp, scale=-1.0).then_inc(f.inverses, 1)
        if new:
            keep_transposed(act, nc, m, s, new, stage)
            act.wait_ge(f.shared, count(new, 1, 1))
            if new[1]:
                act.wait_ge(f.queries, count(new, 1, 0))
            act.activation(f.sq[:, :], m.bank[2][:, :], ACT.Sigmoid, bias=f.bqk[:, :]).then_inc(f.gates, 1)
            act.wait_ge(f.values_biased, count(new, 1, 1))
            act.activation(f.sv[:, :], f.vb[:, :], ACT.Sigmoid).then_inc(f.value_gates, 1)
            h = new[1] % 2
            act.wait_ge(f.arguments, count(new, TILES, TILES))
            act.activation(f.size[:, h, :], f.y[:, :], ACT.Abs).then_inc(f.absolutes, 1)
            act.activation(f.sign[:, h, :], f.y[:, :], ACT.Sign).then_inc(f.signs, 1)

    rounds(act, body)


def laplace_vector(dve, nc, m, s, f, stage):
    credit(dve, f.added, 1)
    dve.wait_ge(f.skewed, 16)
    steps = Steps(dve, f.steps, 1)
    ahead = Steps(dve, f.ahead_steps, 3)

    def body(new, now, former):
        if former:
            dve.wait_ge(f.out, count(former, 1, 1))
            dve.tensor_tensor(m.x[:, rows(former)], m.bank[1][:, :], m.x[:, rows(former)], ALU.add).then_inc(f.added, 1)
        if new:
            if former:
                dve.wait_ge(f.added, count(former, 1, 2))
            ahead.begin(new)
            take_statistics(dve, nc, m, s, after(new, 1), stage, ahead)
        if now:
            dve.wait_ge(f.inverses, count(now, 1, 1))
            dve.tensor_tensor(f.g[:, :], f.g[:, :], f.inverse[:, :], ALU.mult).then_inc(f.phis, 1)
        if new:
            dve.wait_ge(f.values, count(new, 1, 1))
            if new[1]:
                dve.wait_ge(f.value_gates, count(new, 1, 0))
            dve.tensor_tensor(f.vb[:, :], m.bank[3][:, :], f.bv[:, :], ALU.add).then_inc(f.values_biased, 1)
        if now:
            dve.wait_ge(f.phis, count(now, 1, 1))
            dve.wait_ge(f.signs, count(now, 1, 1))
            dve.scalar_tensor_tensor(f.g[:, :], f.g[:, :], -0.5, f.sign[:, now[1] % 2, :], ALU.add, ALU.mult).then_inc(f.halves, 1)
        if new:
            dve.wait_ge(f.gates, count(new, 1, 1))
            steps.begin(new)
            steps.done(dve.scalar_tensor_tensor(f.qk[:, :], m.bank[2][:, :], f.bqk[:, :], f.sq[:, :], ALU.add, ALU.mult))
            if new[1]:
                dve.wait_ge(f.scores, count(new, TILES, 0))
            dve.tensor_scalar(f.q[:, :], f.qk[:, :], f.gb[:, 0:1], f.gb[:, 2:3], ALU.mult, ALU.add).then_inc(f.queries, 1)
            dve.tensor_scalar(f.k[:, :], f.qk[:, :], f.gb[:, 1:2], f.gb[:, 3:4], ALU.mult, ALU.add).then_inc(f.keys, 1)
            dve.wait_ge(f.value_gates, count(new, 1, 1))
            dve.tensor_tensor(f.v[:, new[1] % 2, :], f.vb[:, :], f.sv[:, :], ALU.mult).then_inc(f.values_made, 1)
        if now:
            if now[1]:
                dve.wait_ge(f.out, count(now, 1, 0))
            dve.wait_ge(f.halves, count(now, 1, 1))
            dve.tensor_scalar(f.p[:, :], f.g[:, :], 0.5, None, ALU.add).then_inc(f.weights, 1)
            dve.wait_ge(f.weights, count(now, 2, 1))
            for j in range(TILES):
                at = slice(STARTS[j], STARTS[j] + P)
                last = dve.tensor_tensor(f.p[:, at], f.p[:, at], f.causal[:, :], ALU.mult)
            last.then_inc(f.weights, 1)
        if new:
            if new[1]:
                dve.wait_ge(f.signs, count(new, 1, 0))
            for j in range(TILES):
                w = S - j * P
                dve.wait_ge(f.scores, count(new, TILES, j + 1))
                dve.scalar_tensor_tensor(f.y[:, STARTS[j]:STARTS[j] + w], m.bank[4 + j][:, 0:w], 1.0 / (S * DEVIATION),
                                         f.toeplitz[:, 0:w], ALU.mult, ALU.add).then_inc(f.arguments, 1)
            size = f.size[:, new[1] % 2, :]
            dve.wait_ge(f.absolutes, count(new, 1, 1))
            dve.tensor_scalar(size, size, TINY, 8.0, ALU.max, ALU.min).then_inc(f.sizes, 1)

    rounds(dve, body)



HALVES, GROUPS, STATES = 2, 16, 16
NG = HALVES * GROUPS
JUST = P // GROUPS
TAPS = 4
SMALL_EXP = 2.0 ** -7
QUAD = 4
KEPT = 7


def channel_group(i):
    return i % 4 * 4 + i // 4




def mamba_tensor(pe, nc, m, s, f, stage):
    def spread(b, n):
        half, g = divmod(n, GROUPS)
        h = b[1] % 2
        chosen = f.choose[:, channel_group(g), :]
        pe.wait_ge(f.decays, count(b, NG, n + 1))
        pe.matmul(m.bank[2 + n % 2][:, :], chosen, f.high[:, h, 0, half, :], start=True, stop=False)
        pe.matmul(m.bank[2 + n % 2][:, :], chosen, f.low[:, h, 0, half, :], start=False, stop=True).then_inc(f.spread, 1)
        pe.wait_ge(f.driven, count(b, NG, n + 1))
        pe.matmul(m.bank[4 + n % 2][:, :], chosen, f.high[:, h, 1, half, :], start=True, stop=False)
        pe.matmul(m.bank[4 + n % 2][:, :], chosen, f.low[:, h, 1, half, :], start=False, stop=True).then_inc(f.spread, 1)

    def add_states(b, first):
        half, within = first // GROUPS, first % GROUPS // QUAD
        if within == 0:
            pe.wait_ge(f.ended, count(b, HALVES, half + 1))
        pe.wait_ge(f.weighed, count(b, NG, first + QUAD + 8))
        for n in range(first, first + QUAD):
            quarter = n % 4
            last = pe.matmul(m.bank[6 + half][32 * quarter:32 * quarter + 32, :], f.gather[:, within, :], f.hc[:, n % 8, :],
                             start=within == 0, stop=within == 3)
        last.then_inc(f.summed, 1)

    def prepare(b, former):
        h = b[1] % 2
        xt = f.xt[:, h, :]
        yield 3
        if b[1]:
            pe.wait_ge(f.biased, count(b, 2, 0))
        transpose_batch(pe, nc, m, s, b, stage)
        yield 5
        xt_ready(pe, s, b, stage)
        for half in range(HALVES):
            for tap in range(TAPS):
                last = pe.matmul(m.bank[1 - half][:, :], f.w_tap[:, half, tap, :], xt[:, tap:tap + S], start=tap == 0, stop=tap == TAPS - 1)
            last.then_inc(f.inner, 1)
            yield 6
        yield 8
        if former:
            result(former, b)
        for part in range(HALVES):
            yield 9 + part
            pe.wait_ge(f.kept, count(b, KEPT, 2))
            if part and former:
                pe.wait_ge(f.added, count(former, 1, 2))
            pe.matmul(m.bank[part][:, :], f.w_in[:, 2 + part, :], xt[:, TAPS - 1:], start=True, stop=True).then_inc(f.inner, 1)
        yield 11
        pe.wait_ge(f.x_made, count(b, 2, 2))
        pe.wait_ge(f.kept, count(b, KEPT, 3))
        for half in range(HALVES):
            last = pe.matmul(m.bank[0][0:JUST, :], f.w_dt[:, half, :], f.x[:, h, half, :], start=half == 0, stop=half == 1)
        last.then_inc(f.projected, 1)
        for n in range(2):
            yield 12 + n
            pe.wait_ge(f.kept, count(b, KEPT, 4 + n))
            for half in range(HALVES):
                last = pe.matmul(m.bank[1 - n][:, :], f.w_bc[:, half, n, :], f.x[:, h, half, :], start=half == 0, stop=half == 1)
            last.then_inc(f.projected, 1)
        for half in range(HALVES):
            yield 14 + half
            pe.wait_ge(f.kept, count(b, KEPT, 6 + half))
            pe.matmul(m.bank[1 - half][:, :], f.w_delta[:, half, :], f.dt[:, :], start=True, stop=True).then_inc(f.delta_made, 1)

    def result(b, new):
        pe.wait_ge(f.gated, count(b, 1, 1))
        pe.wait_ge(f.added, count(b, 1, 1))
        if new:
            pe.wait_ge(f.kept, count(new, KEPT, 2))
        else:
            pe.wait_ge(f.biased, 2 * BATCHES)
        for t in range(TILES):
            for half in range(HALVES):
                last = pe.matmul(m.bank[1][:, t * P:(t + 1) * P], f.y[:, half, t * P:(t + 1) * P], f.w_out[:, half, :],
                                 start=half == 0, stop=half == 1)
        last.then_inc(f.out, 1)

    def body(new, now, former):
        steps = Beside(prepare(new, former)) if new else None
        for n in range(NG):
            if now:
                if n == 0:
                    pe.wait_ge(f.highs, count(now, 2, 2))
                    pe.wait_ge(f.lows, count(now, 2, 2))
                spread(now, n)
            if steps:
                steps.until(n)
            if former and n == 2:
                add_states(former, NG - QUAD)
            if now and n >= 6 and n % QUAD == 2:
                add_states(now, n - 6)
            if former and not new and n == 8:
                result(former, None)

    pe.wait_ge(f.chosen, 1)
    pe.wait_ge(f.taps_folded, 2 * TAPS)
    rounds(pe, body)


def mamba_scalar(act, nc, m, s, f, stage):
    credit(act, f.decays, 2)
    act.activation(f.rates[:, :], f.rates[:, :], ACT.Exp).then_inc(f.rate_exps, 1)
    act.wait_ge(f.rates_ready, 1)
    steps = Steps(act, f.scalar_steps, 2)

    def prepare(b):
        h = b[1] % 2
        yield 4
        act.wait_ge(s.transposed, count(b, 1, 8 * stage + 3))
        act.activation(f.xt[:, h, TAPS - 1:], m.bank[0][:, :], ACT.Copy).then_inc(s.xt, 1)
        for half in range(HALVES):
            yield 6 + half
            act.wait_ge(f.inner, count(b, 4, half + 1))
            act.activation(f.x_tanh[:, half, :], m.bank[1 - half][:, :], ACT.Tanh, bias=f.taps[:, half, TAPS:TAPS + 1])
            act.activation(f.conv[:, half, :], m.bank[1 - half][:, :], ACT.Identity, bias=f.taps[:, half, TAPS:TAPS + 1]).then_inc(f.kept, 1)
        for half in range(HALVES):
            yield 10 + half
            act.wait_ge(f.inner, count(b, 4, half + 3))
            act.activation(f.z_half[:, half, :], m.bank[half][:, :], ACT.Copy, scale=0.5)
            act.activation(f.z_tanh[:, half, :], m.bank[half][:, :], ACT.Tanh, scale=0.5).then_inc(f.kept, 1)
        yield 12
        act.wait_ge(f.projected, count(b, 3, 1))
        act.activation(f.dt[:, :], m.bank[0][0:JUST, :], ACT.Copy).then_inc(f.kept, 1)
        if b[1] >= 2:
            act.wait_ge(f.weighed, count(b, NG, 8 - NG))
            act.wait_ge(f.driven, count(b, NG, 2 - NG))
        for n in range(2):
            yield 13 + n
            act.wait_ge(f.projected, count(b, 3, n + 2))
            act.activation(f.bc[:, h, n, :], m.bank[1 - n][:, :], ACT.Copy).then_inc(f.kept, 1)
        yield 18
        act.wait_ge(f.biased, count(b, 2, 2))
        steps.begin(b)
        steps.mark(act.activation(f.small[:, :, :], f.v[:, :, :], ACT.Abs))
        yield 19
        steps.need()
        steps.mark(act.activation(f.small[:, :, :], f.small[:, :, :], ACT.Exp, scale=-1.0))
        yield 20
        steps.need()
        act.activation(f.delta[:, :, :], f.small[:, :, :], ACT.Ln, bias=f.one[:, :]).then_inc(f.logs, 1)
        yield 26
        act.wait_ge(f.deltas, count(b, 1, 1))
        act.activation(f.high[:, h, 0, :, :], f.delta[:, :, :], ACT.Copy).then_inc(f.highs, 1)
        yield 28
        act.wait_ge(f.inputs, count(b, 1, 1))
        act.activation(f.high[:, h, 1, :, :], f.du[:, :, :], ACT.Copy).then_inc(f.highs, 1)

    def body(new, now, former):
        beside = Beside(prepare(new)) if new else None
        for n in range(NG):
            if now:
                half, g = divmod(n, GROUPS)
                act.wait_ge(f.spread, count(now, 2 * NG, 2 * n + 1))
                act.wait_ge(f.states, count(now, NG, n + 1))
                col = half * GROUPS + channel_group(g)
                act.activation(f.keep[:, n % 4, :], m.bank[2 + n % 2][:, :], ACT.Exp,
                               scale=f.rates[:, col:col + 1]).then_inc(f.decays, 1)
            if beside:
                beside.until(n)

    rounds(act, body)


def mamba_vector(dve, nc, m, s, f, stage):
    dve.wait_ge(f.rate_exps, 1)
    dve.memset(f.one[:, :], 1.0)
    dve.tensor_scalar(f.taps[:, :, :], f.taps[:, :, :], 0.5, None, ALU.mult).then_inc(f.taps_halved, 1)
    dve.wait_ge(f.raw_loaded, 16)
    dve.tensor_copy(f.choose[:, :, :], f.raw).then_inc(f.chosen, 1)
    dve.tensor_scalar(f.rates[:, :], f.rates[:, :], -1.0, None, ALU.mult).then_inc(f.rates_ready, 1)
    dve.wait_ge(f.taps_halved, 1)
    dve.wait_ge(f.wide_loaded, 16)
    for half in range(HALVES):
        for tap in range(TAPS):
            dve.scalar_tensor_tensor(f.w_tap[:, half, tap, :], f.w_in[:, half, :], 0.5, f.wide_taps[:, half, tap, :], ALU.mult, ALU.mult).then_inc(f.taps_folded, 1)
    dve.wait_ge(f.chosen, 1)
    dve.wait_ge(f.rates_ready, 1)
    credit(dve, f.driven, 2)
    credit(dve, f.states, 4)
    credit(dve, f.ended, 2)
    credit(dve, f.added, 1)
    steps = Steps(dve, f.steps, 3)
    series = Steps(dve, f.series_steps, 4)

    def prepare(b, former):
        h = b[1] % 2
        for half in range(HALVES):
            yield 7 + half
            dve.wait_ge(f.kept, count(b, KEPT, half + 1))
            dve.scalar_tensor_tensor(f.x[:, h, half, :], f.x_tanh[:, half, :], 1.0, f.conv[:, half, :], ALU.add, ALU.mult).then_inc(f.x_made, 1)
        yield 13
        dve.wait_ge(f.kept, count(b, KEPT, 4))
        dve.scalar_tensor_tensor(f.z[:, h, :, :], f.z_tanh[:, :, :], 1.0, f.z_half[:, :, :], ALU.add, ALU.mult)
        for half in range(HALVES):
            yield 15 + half
            dve.wait_ge(f.delta_made, count(b, 2, half + 1))
            if half == 0:
                dve.wait_ge(f.x_made, count(b, 2, 2))
            dve.tensor_scalar(f.v[:, half, :], m.bank[1 - half][:, :], f.delta_bias[:, half:half + 1], None, ALU.add).then_inc(f.biased, 1)
        e, t = f.small[:, :, :], f.series[:, :, :]
        yield 21
        dve.wait_ge(f.logs, count(b, 1, 1))
        series.begin(b)
        dve.tensor_scalar(f.is_small[:, :, :], e, SMALL_EXP, None, ALU.is_lt)
        series.mark(dve.tensor_scalar(t, e, 1.0 / 3, -0.5, ALU.mult, ALU.add))
        yield 22
        series.need()
        series.mark(dve.tensor_tensor(t, t, e, ALU.mult))
        yield 23
        series.need()
        series.mark(dve.scalar_tensor_tensor(t, t, 1.0, e, ALU.add, ALU.mult))
        yield 24
        series.need()
        yield 25
        series.mark(dve.copy_predicated(f.delta[:, :, :], f.is_small[:, :, :], t))
        series.need()
        dve.scalar_tensor_tensor(f.delta[:, :, :], f.v[:, :, :], 0.0, f.delta[:, :, :], ALU.max, ALU.add).then_inc(f.deltas, 1)
        yield 26
        dve.wait_ge(f.deltas, count(b, 1, 1))
        dve.tensor_tensor(f.du[:, :, :], f.delta[:, :, :], f.x[:, h, :, :], ALU.mult).then_inc(f.inputs, 1)
        for n, whole in ((0, f.delta), (1, f.du)):
            yield 27 + 2 * n
            dve.wait_ge(f.highs, count(b, 2, n + 1))
            dve.tensor_tensor(f.low[:, h, n, :, :], whole[:, :, :], f.high[:, h, n, :, :].bitcast(F32), ALU.subtract).then_inc(f.lows, 1)

    def drive(b, n):
        dve.wait_ge(f.spread, count(b, 2 * NG, 2 * n + 2))
        dve.tensor_tensor(f.drive[:, n % 4, :], m.bank[4 + n % 2][:, :], f.bc[:, b[1] % 2, 0, :], ALU.mult).then_inc(f.driven, 1)

    def scan(b, n):
        dve.wait_ge(f.decays, count(b, NG, n + 1 + 2))
        dve.wait_ge(f.driven, count(b, NG, n + 1 + 2))
        dve.wait_ge(f.weighed, count(b, NG, n + 5))
        dve.tensor_tensor_scan(f.state[:, n % 4, :], f.keep[:, n % 4, :], f.drive[:, n % 4, :], 0.0,
                               ALU.mult, ALU.add).then_inc(f.states, 1)

    def end(b, half):
        dve.wait_ge(f.summed, count(b, NG // QUAD, (half + 1) * GROUPS // QUAD))
        if half == 0 and b[1]:
            dve.wait_ge(f.out, count(b, 1, 0))
        dve.scalar_tensor_tensor(f.y[:, half, :], f.x[:, b[1] % 2, half, :], f.skip[:, half:half + 1], m.bank[6 + half][:, :],
                                 ALU.mult, ALU.add).then_inc(f.ended, 1)

    def body(new, now, former):
        beside = Beside(prepare(new, former)) if new else None
        for n in range(NG):
            if now:
                drive(now, n)
            if former and n == 0:
                scan(former, NG - 1)
            if now and n:
                scan(now, n - 1)
            if former:
                if n == 4:
                    end(former, 1)
                if n == 5:
                    dve.wait_ge(f.ended, count(former, HALVES, 2 + 2))
                    dve.tensor_tensor(f.y[:, :, :], f.y[:, :, :], f.z[:, former[1] % 2, :, :], ALU.mult).then_inc(f.gated, 1)
                if n == 10:
                    dve.wait_ge(f.out, count(former, 1, 1))
                    dve.tensor_tensor(m.x[:, rows(former)], m.bank[1][:, :], m.x[:, rows(former)], ALU.add).then_inc(f.added, 1)
            if beside:
                beside.until(n)
            if now and n == 20:
                end(now, 0)
            if new and n == 12:
                if former:
                    dve.wait_ge(f.added, count(former, 1, 2))
                steps.begin(new)
                take_statistics(dve, nc, m, s, after(new, 1), stage, steps)

    rounds(dve, body)


def mamba_pool(pool, nc, m, s, f, stage):
    credit(pool, f.weighed, 8)

    def body(new, now, former):
        for n in range(NG):
            if new and n == 0:
                normalise(pool, nc, m, s, new, stage)
            if now:
                pool.wait_ge(f.states, count(now, NG, n + 1 + 4))
                if now[1] or n >= 8:
                    pool.wait_ge(f.summed, count(now, NG // QUAD, n // QUAD - 1))
                pool.tensor_tensor(f.hc[:, n % 8, :], f.state[:, n % 4, :], f.bc[:, now[1] % 2, 1, :], ALU.mult).then_inc(f.weighed, 1)

    pool.memset(f.xt[:, :, 0:TAPS - 1], 0.0).then_inc(f.padded, 1)
    rounds(pool, body)


def mamba_sync(sp, nc, a, f):
    sp.dma_start(f.raw, a["choose"]).then_inc(f.raw_loaded, 16)
    sp.dma_start(f.wide_taps, a["wide_taps"].partition_broadcast(P)).then_inc(f.wide_loaded, 16)



RWKV, HEADS, LAPLACE, MAMBA, TOP1, TOP2 = "rwkv heads laplace mamba top1 top2".split()
STAGES = [RWKV, TOP1, HEADS, TOP1, LAPLACE, TOP2, MAMBA, TOP2]


WINDOW = S + P


def laplace_buffers(tmp, f):
    f.q, f.k, f.vb, f.sv, f.sq, f.qk = (tmp("lap_" + n, [P, S]) for n in "q k vb sv sq qk".split())
    f.v, f.size, f.sign = tmp("lap_v", [P, 2, S]), tmp("size", [P, 2, PAIRED]), tmp("sign", [P, 2, PAIRED])
    f.y, f.g, f.inverse, f.p = (tmp("lap_" + n, [P, PAIRED]) for n in "y g inverse p".split())


def laplace_constants(nc, a, sb, sem, loads, setup, m):
    f = Names()
    f.values, f.shared, f.queries, f.keys, f.scores, f.values_made, f.added = (
        sem("lap_" + n) for n in "values shared queries keys scores values_made added".split())
    f.weights, f.out, f.values_biased, f.value_gates, f.gates, f.arguments, f.sizes = (
        sem("lap_" + n) for n in "weights out values_biased value_gates gates arguments sizes".split())
    f.gelus, f.steps, f.row, f.row_kept, f.rows_stored, f.skewed = (
        sem("lap_" + n) for n in "gelus steps row row_kept rows_stored skewed".split())
    f.signs, f.absolutes, f.phis, f.halves, f.inverses, f.ahead_steps, f.scalar_steps = (
        sem("lap_" + n) for n in "signs absolutes phis halves inverses ahead_steps scalar_steps".split())
    f.wqk, f.wv, f.bqk, f.gb = sb("wqk", [P, P]), sb("wv", [P, P]), sb("bqk", [P, 1]), sb("gb", [P, 4])
    f.bv, f.toeplitz, f.causal = sb("bv", [P, S]), sb("toeplitz", [P, S]), sb("causal", [P, P])
    buckets, table, row = sb("buckets", [32, WINDOW]), sb("table", [32, 1]), sb("bias_row", [1, WINDOW])
    loads += [(f.wqk[:, :], a["wqk"]), (f.wv[:, :], a["wv"]), (f.bqk[:, :], a["bqk"]), (f.gb[:, :], a["gb"]),
              (f.bv[:, :], a["bv"].partition_broadcast(P)), (f.causal[:, :], a["causal"]),
              (buckets[:, :], a["buckets"]), (table[:, :], a["table"])]
    scratch = nc.dram_tensor("bias_rows", (P * WINDOW,), F32)
    half = WINDOW // 2

    def look_up(pe):
        for n in range(2):
            last = pe.matmul(m.bank[6 + n][0:1, 0:half], table[:, :], buckets[:, n * half:(n + 1) * half], start=True, stop=True)
        last.then_inc(f.row, 1)

    def scale(dve):
        dve.wait_ge(f.row, 1)
        for n in range(2):
            last = dve.tensor_scalar(row[:, n * half:(n + 1) * half], m.bank[6 + n][0:1, 0:half],
                                     math.sqrt(P) / DEVIATION, -CENTRE / DEVIATION, ALU.mult, ALU.add)
        last.then_inc(f.row_kept, 1)

    def skew(sp):
        sp.wait_ge(f.row_kept, 1)
        sp.dma_start(bass.AP(tensor=scratch, offset=0, ap=[[WINDOW, P], [1, WINDOW]]), row[0:1, :].unsqueeze(1).to_broadcast([1, P, WINDOW])).then_inc(f.rows_stored, 16)
        sp.wait_ge(f.rows_stored, 16)
        sp.dma_start(f.toeplitz[:, :], bass.AP(tensor=scratch, offset=P - 1, ap=[[WINDOW - 1, P], [1, S]])).then_inc(f.skewed, 16)

    setup.tensor.append(look_up)
    setup.vector.append(scale)
    setup.sync.append(skew)
    return f


def rwkv_memory(nc, a, sb, tmp, sem, loads, setup, m):
    f = Names()
    f.weights_mixed, f.decayed, f.kvr, f.kept, f.mixed, f.added, f.out = (
        sem("rwkv_" + n) for n in "weights_mixed decayed kvr kept mixed added out".split())
    f.less, f.less_pool, f.exps, f.below, f.logs, f.inverses, f.steps = (
        sem("rwkv_" + n) for n in "less less_pool exps below logs inverses steps".split())
    f.maxima, f.tops, f.sums, f.scaled, f.decay_exp, f.mixes, f.prepared = (
        sem("rwkv_" + n) for n in "maxima tops sums scaled decay_exp mixes prepared".split())
    f.terms, f.ahead_steps = sem("rwkv_terms"), sem("rwkv_ahead_steps")
    f.w_now, f.w_before, f.wo = sb("w_now", [P, 3, P]), sb("w_before", [P, 3, P]), sb("wo", [P, P])
    f.mix, f.unmix, f.decay, f.first = sb("mix", [P, 3]), sb("unmix", [P, 3]), sb("decay", [P, 2]), sb("first", [P, 1])
    f.kvr_kept = tmp("kvr_kept", [P, 2, 3, S])
    f.largest, f.sum_w, f.sum_wv = (tmp(n, [P, 2, S + 1]) for n in ("largest", "sum_w", "sum_wv"))
    f.top, f.ev, f.num, f.den, f.log, f.inverse, f.rw = (tmp("rwkv_" + n, [P, S]) for n in "top ev num den log inverse rw".split())
    f.d, f.e, f.ew = tmp("less", [P, 2, 4, S]), tmp("exps", [P, 2, 4, S]), tmp("rwkv_ew", [P, 2, S])
    loads += [(f.w_now[:, :, :], a["wkvr"]), (f.wo[:, :], a["wo"]), (f.mix[:, :], a["mix"]), (f.decay[:, 0:1], a["decay"]),
              (f.first[:, :], a["first"])]

    def decay_scalar(act):
        act.activation(f.decay[:, 1:2], f.decay[:, 0:1], ACT.Exp).then_inc(f.decay_exp, 1)

    def mix_vector(dve):
        dve.wait_ge(f.decay_exp, 1)
        dve.tensor_scalar(f.decay[:, 1:2], f.decay[:, 1:2], -1.0, None, ALU.mult).then_inc(f.decayed, 1)
        dve.tensor_scalar(f.unmix[:, :], f.mix[:, :], -1.0, 1.0, ALU.mult, ALU.add).then_inc(f.mixes, 1)
        dve.wait_ge(f.mixes, 1)
        for n in range(3):
            dve.tensor_scalar(f.w_before[:, n, :], f.w_now[:, n, :], f.unmix[:, n:n + 1], None, ALU.mult).then_inc(f.weights_mixed, 1)
        dve.wait_ge(f.weights_mixed, 3)
        for n in range(3):
            dve.tensor_scalar(f.w_now[:, n, :], f.w_now[:, n, :], f.mix[:, n:n + 1], None, ALU.mult).then_inc(f.weights_mixed, 1)
        dve.memset(f.largest[:, :, 0:1], -BIG)
        dve.memset(f.sum_w[:, :, 0:1], 0.0)
        dve.memset(f.sum_wv[:, :, 0:1], 0.0).then_inc(f.prepared, 1)
        dve.wait_ge(f.prepared, 1)
        dve.wait_ge(f.decayed, 1)

    setup.scalar.append(decay_scalar)
    setup.vector.append(mix_vector)
    return f


def mamba_memory(nc, a, sb, tmp, sem, loads):
    f = Names()
    f.decays, f.spread, f.driven, f.weighed, f.summed, f.inner, f.x_made = (
        sem("mamba_" + n) for n in "decays spread driven weighed summed inner x_made".split())
    f.kept, f.projected, f.ended, f.delta_made, f.highs, f.lows, f.gated = (
        sem("mamba_" + n) for n in "kept projected ended delta_made highs lows gated".split())
    f.added, f.out, f.chosen, f.rates_ready, f.scalar_steps, f.biased, f.logs = (
        sem("mamba_" + n) for n in "added out chosen rates_ready scalar_steps biased logs".split())
    f.deltas, f.inputs, f.states, f.steps, f.series_steps, f.rate_exps, f.raw_loaded = (
        sem("mamba_" + n) for n in "deltas inputs states steps series_steps rate_exps raw_loaded".split())
    f.wide_loaded, f.taps_halved, f.taps_folded, f.padded = (
        sem("mamba_" + n) for n in "wide_loaded taps_halved taps_folded padded".split())
    f.w_in, f.w_dt, f.w_bc = sb("w_in", [P, 4, P]), sb("w_dt", [P, HALVES, JUST]), sb("w_bc", [P, HALVES, 2, P])
    f.w_delta, f.w_out = sb("w_delta", [JUST, HALVES, P]), sb("w_out", [P, HALVES, P])
    f.taps, f.delta_bias, f.skip = sb("taps", [P, HALVES, TAPS + 1]), sb("delta_bias", [P, HALVES]), sb("skip", [P, HALVES])
    f.rates, f.one, f.gather = sb("rates", [P, NG]), sb("one", [P, 1]), sb("gather", [P, 4, 32])
    f.choose, f.w_tap = tmp("choose", [P, GROUPS, P], F32R), tmp("w_tap", [P, HALVES, TAPS, P])
    f.xt = tmp("m_xt", [P, 2, TAPS - 1 + S])
    f.x, f.z = (tmp("m_" + n, [P, 2, HALVES, S]) for n in "xz")
    f.conv, f.x_tanh, f.z_half, f.z_tanh, f.y = (tmp("m_" + n, [P, HALVES, S]) for n in "conv x_tanh z_half z_tanh y".split())
    f.v, f.small, f.delta, f.series, f.du = f.conv, f.x_tanh, f.z_half, f.z_tanh, f.z_tanh
    f.is_small = tmp("is_small", [P, HALVES, S], mybir.dt.uint32)
    f.high, f.low = tmp("high", [P, 2, 2, HALVES, S], F32R), tmp("low", [P, 2, 2, HALVES, S], F32R)
    f.dt, f.bc = tmp("dt", [JUST, S]), tmp("bc", [P, 2, 2, S])
    f.keep, f.drive, f.state = (tmp("m_" + n, [P, 4, S]) for n in "keep drive state".split())
    f.hc = tmp("m_hc", [P, 2 * QUAD, S])
    f.raw = f.keep[:, :, :].rearrange("p a (b c) -> p (a b) c", c=P)
    f.wide_taps = f.conv[:, :, :].rearrange("p h (t c) -> p h t c", t=TAPS)
    loads += [(f.w_in[:, :, :], a["w_in"]), (f.w_dt[:, :, :], a["w_dt"]), (f.w_bc[:, :, :, :], a["w_bc"]),
              (f.w_delta[:, :, :], a["w_delta"]), (f.w_out[:, :, :], a["w_out"]), (f.taps[:, :, :], a["taps"]),
              (f.delta_bias[:, :], a["delta_bias"]), (f.skip[:, :], a["skip"]), (f.rates[:, :], a["a_log"]),
              (f.gather[:, :, :], a["gather"])]
    return f


def heads_weights(a, sb, sem, loads):
    f = Names()
    f.scored, f.summed, f.turned, f.ring_read, f.ring_made, f.exps, f.out_kept = (
        sem("heads_" + n) for n in "scored summed turned ring_read ring_made exps out_kept".split())
    f.half_maxima, f.maxima_turned, f.highs, f.less_highs, f.steps, f.ahead_steps, f.less_rests = (
        sem("heads_" + n) for n in "half_maxima maxima_turned highs less_highs steps ahead_steps less_rests".split())
    f.added, f.middles, f.parted, f.less_middles, f.less_parted, f.stacked0, f.stacked1 = (
        sem("heads_" + n) for n in "added middles parted less_middles less_parted stacked0 stacked1".split())
    f.lowered0, f.lowered1, f.cleared, f.stack_cleared = (
        sem("heads_" + n) for n in "lowered0 lowered1 cleared stack_cleared".split())
    f.stacked, f.lowered = (f.stacked0, f.stacked1), (f.lowered0, f.lowered1)
    f.zeroed = sem("heads_zeroed")
    f.wq, f.wk, f.wv = (sb("h_w" + n, [P, P]) for n in "qkv")
    loads += [(f.wq[:, :], a["h_wq"]), (f.wk[:, :], a["h_wk"]), (f.wv[:, :], a["h_wv"])]
    return f


def heads_buffers(tmp, f):
    BF16 = mybir.dt.bfloat16
    f.part, f.rest = tmp("part", [P, 2, 3, S], BF16), tmp("rest", [P, 2, S])
    f.less, f.less_rest = tmp("h_less", [HALF_HEADS, 3, S], BF16), tmp("less_rest", [HALF_HEADS, S])
    f.p, f.o = tmp("h_p", [P, 2, 4, S]), tmp("h_o", [P, S])
    f.maxima, f.inverse, f.mean = tmp("maxima", [P, TILES, NHEADS]), tmp("h_inverse", [P, TILES, 4]), tmp("h_mean", [P, TILES, 4, HD])
    f.zero = tmp("zero", [P, 1])
    f.nothing = tmp("nothing", [4, S], BF16)
    f.v = tmp("h_v", [P, 2, TILES, NHEADS, 32])
    f.qs, f.ks = (tmp(n, [P, 2, NHEADS, S], BF16) for n in ("qs", "ks"))


def build(nc, a, out, stages):
    ctx = ExitStack()
    with ctx:
        def sem(name):
            return ctx.enter_context(nc.semaphore(name))

        def into(stack):
            return lambda name, shape, dtype=F32: stack.enter_context(nc.sbuf_tensor(name, shape, dtype))

        sb = into(ctx)

        m = Names()
        m.banks = ctx.enter_context(nc.psum_tensor("banks", [P, 8, 512], F32))
        m.bank = [m.banks[:, i, :] for i in range(8)]
        m.x = sb("x", [P, BATCHES * S])
        m.ident = sb("ident", [P, P])
        m.minus_half = sb("minus_half", [P, TILES])
        m.bn = sb("bn", [P, 2, TILES, 6])
        m.mean_var = sb("mean_var", [P, 2, TILES, 2])
        m.half_stats = sb("half_stats", [P, 5, TILES])
        m.rstd = sb("rstd", [P, 2, TILES])
        m.xn = sb("xn", [P, 2, S])
        m.xt = sb("xt", [P, 2, S + 1])
        m.order = sb("order", [P, TILES * 8])
        m.r_l, m.r_d, m.r_exp, m.r_hot, m.r_two = (sb(n, [P, TILES * 8]) for n in ("r_l", "r_d", "r_exp", "r_hot", "r_two"))
        m.r_col = sb("r_col", [P, 3, TILES])
        m.gates = sb("gates", [P, TILES, 8])
        m.gates_t = sb("gates_t", [8, S])
        s = Names()
        s.loaded, s.filled, s.stats, s.rstd, s.centred, s.normed, s.transposed = (
            sem("s_" + n) for n in "loaded filled stats rstd centred normed transposed".split())
        s.xt, s.first_steps, s.stage, s.stored, s.late = (
            sem("s_" + n) for n in "xt first_steps stage stored late".split())

        loads, late_loads = [], []
        x_view = a["x"].rearrange("b (t p) d -> p b t d", p=P)
        for b in range(BATCHES):
            loads.append((by_tile(m.x[:, b * S:(b + 1) * S]), x_view[:, b]))
        loads += [(m.ident[:, :], a["ident"]), (m.order[:, :], a["order"])]

        plans = [None] * len(stages)
        setup = Names()
        setup.tensor, setup.vector, setup.scalar, setup.sync = [], [], [], []

        def experts_weights(pre, blocks, into, take):
            w = Names()
            w.gates_kept, w.logits, w.first, w.hidden, w.out, w.added, w.gates = (
                sem(pre + "_" + name) for name in "gates_kept logits first hidden out added gates".split())
            w.gates_turned, w.shifted, w.exps, w.steps = (
                sem(pre + "_" + name) for name in "gates_turned shifted exps steps".split())
            w.split, w.x_high, w.x_low = (sem(pre + "_" + name) for name in "split x_high x_low".split())
            w.w1 = into(pre + "w1", [P, 8, blocks * P])
            w.w2 = into(pre + "w2", [P, 8 * blocks * P])
            w.b1 = into(pre + "b1", [P, 8 * blocks])
            w.b2 = into(pre + "b2", [8, P])
            w.wr = into(pre + "wr", [P, 8])
            take += [(w.w1[:, :, :], a[pre + "w1"].rearrange("e d f -> d e f")),
                     (w.w2[:, :].rearrange("p (e j d) -> p e j d", e=8, j=blocks), a[pre + "w2"].rearrange("e (j p) d -> p e j d", p=P)),
                     (w.b1[:, :], a[pre + "b1"]), (w.b2[:, :], a[pre + "b2"]), (w.wr[:, :], a[pre + "wr"])]
            return w

        def experts_plan(n, w, blocks, top, func):
            f = Names()
            f.blocks, f.top, f.func, f.use = blocks, top, func, stages[:n].count(stages[n])
            f.w1, f.w2, f.b1, f.b2, f.wr = w.w1, w.w2, w.b1, w.b2, w.wr
            f.split, f.x_high, f.x_low = w.split, w.x_high, w.x_low
            if top == 1:
                f.br = w.br
            f.gates_kept, f.logits, f.first, f.hidden, f.out, f.added = (
                w.gates_kept, w.logits, w.first, w.hidden, w.out, w.added)
            f.gates, f.gates_turned, f.shifted, f.exps, f.steps = w.gates, w.gates_turned, w.shifted, w.exps, w.steps
            with ExitStack() as own:
                if top == 1:
                    f.xh, f.xl = w.xh, w.xl
                else:
                    f.xh, f.xl = (into(own)(f"{name}{n}", [P, 2, S], F32R) for name in ("x_high", "x_low"))
                f.hid = into(own)(f"hid{n}", [P, 2, blocks, S])
                f.w_high, f.w_low = (into(own)(f"{name}{n}", [P, 8, blocks * P], F32R) for name in ("w_high", "w_low"))
            plans[n] = (f, experts_tensor, experts_scalar, experts_vector, experts_pool)

        if LAPLACE in stages:
            lap = laplace_constants(nc, a, sb, sem, loads, setup, m)
        with ExitStack() as early:
            if TOP1 in stages:
                w = experts_weights("t1", 4, into(early), loads)
                br = into(early)("t1br", [P, TILES * 8])
                w.br = br[:, :]
                w.xh, w.xl = (into(early)(name, [P, 2, S], F32R) for name in ("x_high", "x_low"))
                loads.append((w.br, a["t1br"].partition_broadcast(P)))
            if HEADS in stages:
                heads = heads_weights(a, into(early), sem, loads)
            if RWKV in stages:
                with ExitStack() as own:
                    f = rwkv_memory(nc, a, into(early), into(own), sem, loads, setup, m)
                    plans[stages.index(RWKV)] = (f, rwkv_tensor, rwkv_scalar, rwkv_vector, rwkv_pool)
            if HEADS in stages:
                with ExitStack() as own:
                    heads_buffers(into(own), heads)
                    plans[stages.index(HEADS)] = (heads, heads_tensor, heads_scalar, heads_vector, heads_pool)
            for n, kind in enumerate(stages):
                if kind == TOP1:
                    experts_plan(n, w, 4, 1, ACT.Gelu)
        if TOP2 in stages:
            w = experts_weights("t2", 2, sb, late_loads)
        if MAMBA in stages:
            with ExitStack() as own:
                mamba = mamba_memory(nc, a, sb, into(own), sem, late_loads)
                plans[stages.index(MAMBA)] = (mamba, mamba_tensor, mamba_scalar, mamba_vector, mamba_pool)
        for n, kind in enumerate(stages):
            if kind == TOP2:
                experts_plan(n, w, 2, 2, ACT.Relu)
        if LAPLACE in stages:
            with ExitStack() as own:
                laplace_buffers(into(own), lap)
                plans[stages.index(LAPLACE)] = (lap, laplace_tensor, laplace_scalar, laplace_vector, experts_pool)

        block = ctx.enter_context(nc.Block())

        def between(eng, n):
            eng.drain().then_inc(s.stage, 1)
            eng.wait_ge(s.stage, 4 * (n + 1))

        late = max([n + 1 for n, kind in enumerate(stages) if kind in (RWKV, TOP1, HEADS)], default=0)
        filling = stages.index(HEADS) - 1 if HEADS in stages else None

        def arrived(eng, kind, n):
            if kind in (TOP2, MAMBA) and late_loads:
                eng.wait_ge(s.late, 16 * len(late_loads))

        @block.sync
        def _(sp):
            for tile, dram in loads:
                sp.dma_start(tile, dram).then_inc(s.loaded, 16)
            for do in setup.sync:
                do(sp)
            if late_loads and late == 0:
                for tile, dram in late_loads:
                    sp.dma_start(tile, dram).then_inc(s.late, 16)
            for n, kind in enumerate(stages):
                if n:
                    sp.wait_ge(s.stage, 4 * n)
                if n == late and n:
                    for tile, dram in late_loads:
                        sp.dma_start(tile, dram).then_inc(s.late, 16)
                if kind == HEADS:
                    heads_sync(sp, nc, m, s, heads, n)
                if kind == MAMBA:
                    mamba_sync(sp, nc, a, mamba)
            sp.wait_ge(s.stage, 4 * len(stages))
            for b in range(BATCHES):
                sp.dma_start(out.rearrange("b (t p) d -> p b t d", p=P)[:, b], by_tile(m.x[:, b * S:(b + 1) * S])).then_inc(s.stored, 16)
            sp.wait_ge(s.stored, 16 * BATCHES)

        @block.tensor
        def _(pe):
            pe.wait_ge(s.loaded, 16 * len(loads))
            credit(pe, s.transposed, 2)
            for do in setup.tensor:
                do(pe)
            for n, (f, tensor, _, _, _) in enumerate(plans):
                arrived(pe, stages[n], n)
                tensor(pe, nc, m, s, f, n)
                between(pe, n)

        @block.scalar
        def _(act):
            act.wait_ge(s.loaded, 16 * len(loads))
            act.wait_ge(s.filled, 1)
            credit(act, s.xt, 1)
            for do in setup.scalar:
                do(act)
            for n, (f, _, scalar, _, _) in enumerate(plans):
                arrived(act, stages[n], n)
                scalar(act, nc, m, s, f, n)
                between(act, n)

        @block.vector
        def _(dve):
            dve.wait_ge(s.loaded, 16 * len(loads))
            first = Steps(dve, s.first_steps, 3)
            first.begin((0, 0))
            for do in setup.vector:
                do(dve)
            statistics_of(dve, nc, m, s, bass.ds(0, S), 0, first)
            for n, (f, _, _, vector, _) in enumerate(plans):
                arrived(dve, stages[n], n)
                vector(dve, nc, m, s, f, n)
                between(dve, n)

        @block.gpsimd
        def _(pool):
            pool.wait_ge(s.loaded, 16 * len(loads))
            pool.memset(m.minus_half[:, :], -0.5)
            pool.memset(m.xt[:, :, 0:1], 0.0).then_inc(s.filled, 1)
            pool.wait_ge(s.filled, 1)
            credit(pool, s.normed, 2)
            if filling == -1:
                heads_fill(pool, s, heads, 0)
            for n, (f, _, _, _, run) in enumerate(plans):
                arrived(pool, stages[n], n)
                run(pool, nc, m, s, f, n)
                if filling == n:
                    heads_fill(pool, s, heads, n + 1)
                between(pool, n)




def lay_out(i, np):
    def f(v):
        return np.ascontiguousarray(np.asarray(v))

    d = {"x": f(i["L0_attn_a_x"]), "ident": np.eye(P, dtype=np.float32)}
    d["order"] = f(np.tile(np.arange(8, 0, -1, dtype=np.float32), (P, TILES)))
    for pre, w1, b1, w2, b2, wr in (("t1", "L0_ffn_W1", "L0_ffn_b1", "L0_ffn_W2", "L0_ffn_b2", "L0_ffn_Wr"),
                                    ("t2", "L1_ffn_W1", "L1_ffn_b1", "L1_ffn_W2", "L1_ffn_b2", "L1_ffn_gate")):
        d[pre + "w1"], d[pre + "w2"], d[pre + "b2"], d[pre + "wr"] = f(i[w1]), f(i[w2]), f(i[b2]), f(i[wr])
        d[pre + "b1"] = f(np.asarray(i[b1]).reshape(-1, P).T)
    d["wqk"], d["wv"], d["table"] = f(i["L1_attn_a_wqk"]), f(i["L1_attn_a_wv"]), f(i["L1_attn_a_rel_bias"]).reshape(32, 1)
    d["bqk"] = f(i["L1_attn_a_bqk"]).reshape(P, 1)
    d["gb"] = f(np.concatenate([np.asarray(i["L1_attn_a_gamma"]), np.asarray(i["L1_attn_a_beta"])]).T)
    d["bv"] = f(np.tile(np.asarray(i["L1_attn_a_bv"]), TILES))
    key, query = np.arange(P)[:, None], np.arange(P)[None]
    d["causal"] = f(np.where(query >= key, np.float32(1), np.float32(0)))
    n = np.maximum(np.arange(WINDOW) - (P - 1), 0)
    large = 16 + (np.log(np.maximum(n, 1).astype(np.float32) / 16) / math.log(128 / 16) * 16).astype(np.int32)
    bucket = np.where(n < 16, n, np.minimum(large, 31))
    d["buckets"] = f((np.arange(32)[:, None] == bucket[None]).astype(np.float32))
    d["wkvr"] = f(np.stack([np.asarray(i["L0_attn_a_" + w]).T for w in ("Wk", "Wv", "Wr")], 1))
    d["wo"] = f(np.asarray(i["L0_attn_a_Wo"]).T)
    d["mix"] = f(np.stack([np.asarray(i["L0_attn_a_time_mix_" + w]).reshape(P) for w in "kvr"], 1))
    d["decay"], d["first"] = f(i["L0_attn_a_time_decay"]).reshape(P, 1), f(i["L0_attn_a_time_first"]).reshape(P, 1)
    w = {n: np.asarray(i["L1_attn_b_" + n]) for n in ("in_proj_w", "conv_w", "conv_b", "x_proj_w", "dt_proj_w", "dt_proj_b",
                                                       "A_log", "D", "out_proj_w")}
    d["w_in"] = f(w["in_proj_w"].reshape(4, P, P).transpose(2, 0, 1))
    by_half = w["x_proj_w"].T.reshape(HALVES, P, -1).transpose(1, 0, 2)
    d["w_dt"] = f(by_half[:, :, :JUST])
    d["w_bc"] = f(np.tile(by_half[:, :, JUST:].reshape(P, HALVES, 2, 1, STATES), (1, 1, 1, JUST, 1)).reshape(P, HALVES, 2, P))
    d["w_delta"] = f(w["dt_proj_w"].T.reshape(JUST, HALVES, P))
    d["w_out"] = f(w["out_proj_w"].T.reshape(HALVES, P, P).transpose(1, 0, 2))
    d["taps"] = f(np.concatenate([w["conv_w"][:, 0], w["conv_b"][:, None]], 1).reshape(HALVES, P, TAPS + 1).transpose(1, 0, 2))
    d["wide_taps"] = f(w["conv_w"][:, 0].reshape(HALVES, P, TAPS).transpose(0, 2, 1))
    d["delta_bias"], d["skip"] = f(w["dt_proj_b"].reshape(HALVES, P).T), f(w["D"].reshape(HALVES, P).T)
    d["a_log"] = f(w["A_log"].reshape(HALVES * GROUPS, JUST * STATES).T)
    part, channel = np.arange(P), np.arange(P)
    d["choose"] = f((channel[:, None, None] == np.arange(GROUPS)[None, :, None] * JUST + part // STATES).astype(np.float32))
    d["gather"] = f((np.arange(32)[None, None] == np.arange(4)[None, :, None] * JUST + (part // STATES)[:, None, None]).astype(np.float32))
    for n in "qkv":
        w = np.asarray(i["L0_attn_b_W" + n]).T
        if n != "v":
            w = w.reshape(P, 2, HALF_HEADS, HD).transpose(0, 1, 3, 2).reshape(P, P)
        d["h_w" + n] = f(w)
    d["t1br"] = f(np.tile(np.asarray(i["L0_ffn_br"]), TILES))
    return d


def kernel(**inputs):
    import numpy as np
    import concourse.bacc as bacc
    from concourse.bass_utils import run_bass_kernel_spmd

    nc = bacc.Bacc("TRN2", target_bir_lowering=False, num_devices=1)
    arrays = {f"in_{k}": v for k, v in lay_out(inputs, np).items()}
    aps = {k[3:]: nc.dram_tensor(k, v.shape, mybir.dt.from_np(v.dtype), kind="ExternalInput").ap() for k, v in arrays.items()}
    out = nc.dram_tensor("out_x", (BATCHES, S, P), F32, kind="ExternalOutput").ap()
    build(nc, aps, out, STAGES)
    r = run_bass_kernel_spmd(nc, [arrays], core_ids=[0])
    return r.results[0]["out_x"]
```

```python
from contextlib import ExitStack
import math

import concourse.bass as bass
from concourse import mybir

F32 = mybir.dt.float32
F32R = mybir.dt.float32r
ALU = mybir.AluOpType
ACT = mybir.ActivationFunctionType
AX_X = mybir.AxisListType.X

P = 128
BATCHES = 8
S = 512
TILES = S // P
EPS = 1e-5
BIG = 1e30


class Names:
    pass


def count(b, per, n):
    loop, constant = b
    return loop * (2 * per) + (constant * per + n)


def after(b, n):
    return b[0], b[1] + n


def credit(eng, sem, n):
    eng.nop().then_inc(sem, n)


class Steps:

    def __init__(self, eng, sem, per):
        self.eng, self.sem, self.per, self.n = eng, sem, per, 0

    def begin(self, b):
        assert self.n in (0, self.per), (self.n, self.per)
        self.b, self.n = b, 0

    def mark(self, instruction):
        self.n += 1
        instruction.then_inc(self.sem, 1)

    def need(self):
        self.eng.wait_ge(self.sem, count(self.b, self.per, self.n))

    def done(self, instruction):
        self.mark(instruction)
        self.need()


class Beside:

    def __init__(self, steps):
        self.steps = steps
        self.turn = next(steps)

    def until(self, turn):
        while self.turn <= turn:
            self.turn = next(self.steps, BATCHES * S)


def rows(b, tile=0, tiles=TILES):
    loop, constant = b
    return bass.ds(loop * (2 * S) + (constant * S + tile * P), tiles * P)


def by_tile(ap):
    return ap.rearrange("p (t d) -> p t d", t=TILES)


def over_batches(eng, body):
    with eng.Fori(0, BATCHES // 2) as loop:
        for half in range(2):
            body((loop, half))


def rounds(eng, body, roles=3):
    def straight(r):
        body(*[(0, r - n) if 0 <= r - n < BATCHES else None for n in range(roles)])

    before = roles - 1 + (BATCHES - roles + 1) % 2
    for r in range(before):
        straight(r)
    with eng.Fori(0, (BATCHES - before) // 2) as loop:
        for half in range(2):
            body(*[(loop, before + half - n) for n in range(roles)])
    for r in range(BATCHES, BATCHES + roles - 1):
        straight(r)




def take_statistics(dve, nc, m, s, b, stage, steps):
    loop, n = b
    first = loop * (2 * S) + n * S if n < 2 else (loop * 2 + n) % BATCHES * S
    if stage == 0:
        dve.wait_ge(s.x_loaded, 16 * (BATCHES - 1))
    dve.wait_ge(s.normed, count(b, 1, 8 * stage + 1))
    statistics_of(dve, nc, m, s, bass.ds(first, S), n % 2, steps)


def statistics_of(dve, nc, m, s, columns, h, steps):
    x = m.x[:, columns]
    for t in range(TILES):
        last = dve.bn_stats(m.bn[:, h, t, :], x[:, t * P:(t + 1) * P])
    steps.done(last)
    even, odd, mv, half = m.bn[:, h, :, 0:3], m.bn[:, h, :, 3:6], m.mean_var[:, h], m.half_stats
    dve.tensor_tensor(half[:, 0, :], even[:, :, 1], odd[:, :, 1], ALU.add)
    dve.tensor_tensor(half[:, 1, :], even[:, :, 1], odd[:, :, 1], ALU.subtract)
    steps.done(dve.tensor_tensor(half[:, 2, :], even[:, :, 2], odd[:, :, 2], ALU.add))
    dve.tensor_scalar(mv[:, :, 0], half[:, 0, :], 0.5, None, ALU.mult)
    dve.scalar_tensor_tensor(half[:, 3, :], half[:, 1, :], 0.25, half[:, 1, :], ALU.mult, ALU.mult)
    steps.done(dve.tensor_scalar(half[:, 4, :], half[:, 2, :], 1.0 / P, EPS, ALU.mult, ALU.add))
    dve.tensor_tensor(mv[:, :, 1], half[:, 3, :], half[:, 4, :], ALU.add).then_inc(s.stats, 1)


def normalise(pool, nc, m, s, b, stage):
    h = b[1] % 2
    mv, rstd = m.mean_var[:, h], m.rstd[:, h]
    pool.wait_ge(s.stats, count(b, 1, 8 * stage + 1))
    pool.tensor_tensor(rstd, mv[:, :, 1], m.minus_half[:, :], ALU.pow).then_inc(s.rstd, 1)
    pool.wait_ge(s.transposed, count(b, 1, 8 * stage + 1))
    wide = [P, TILES, P]
    pool.tensor_tensor(by_tile(m.xn[:, h, :]), by_tile(m.x[:, rows(b)]), mv[:, :, 0:1].to_broadcast(wide),
                       ALU.subtract).then_inc(s.centred, 1)
    pool.wait_ge(s.rstd, count(b, 1, 8 * stage + 1))
    pool.wait_ge(s.centred, count(b, 1, 8 * stage + 1))
    pool.tensor_tensor(by_tile(m.xn[:, h, :]), by_tile(m.xn[:, h, :]), rstd.unsqueeze(2).to_broadcast(wide),
                       ALU.mult).then_inc(s.normed, 1)


def transpose_batch(pe, nc, m, s, b, stage):
    pe.wait_ge(s.normed, count(b, 1, 8 * stage + 3))
    pe.wait_ge(s.xt, count(b, 1, 8 * stage + 1))
    for t in range(TILES):
        last = pe.transpose(m.bank[0][:, t * P:(t + 1) * P], m.xn[:, b[1] % 2, t * P:(t + 1) * P], m.ident[:, :])
    last.then_inc(s.transposed, 1)


def keep_transposed(act, nc, m, s, b, stage):
    act.wait_ge(s.transposed, count(b, 1, 8 * stage + 3))
    act.activation(m.xt[:, b[1] % 2, 1:S + 1], m.bank[0][:, :], ACT.Copy).then_inc(s.xt, 1)


def xt_ready(eng, s, b, stage):
    eng.wait_ge(s.xt, count(b, 1, 8 * stage + 2))




AHEAD = 6


def experts_tensor(pe, nc, m, s, f, stage):
    NB, E = f.blocks, 8
    outs = E + 1
    if f.use == 0:
        credit(pe, f.out, 3)

    def first_layer(b, u, e):
        h = b[1] % 2
        if e == 0:
            pe.wait_ge(f.x_low, count(u, 1, 1))
        pe.wait_ge(f.split, 2 * E * f.use + 2 * e + 2)
        for j in range(NB):
            n = e * NB + j
            pe.wait_ge(f.hidden, count(u, E * NB, n + 1))
            out, block = m.bank[2 + n % 4][:, :], slice(j * P, (j + 1) * P)
            pe.matmul(out, f.w_high[:, e, block], f.xh[:, h, :], start=True, stop=False)
            pe.matmul(out, f.w_high[:, e, block], f.xl[:, h, :], start=False, stop=False)
            pe.matmul(out, f.w_low[:, e, block], f.xh[:, h, :], start=False, stop=True).then_inc(f.first, 1)

    def second_layer(b, u, e):
        pe.wait_ge(f.hidden, count(u, E * NB, (e + 1) * NB + 4))
        pe.wait_ge(f.added, count(u, outs, e + 1))
        out = m.bank[6 + (b[1] * outs + e) % 2]
        for t in range(TILES):
            for j in range(NB):
                last = pe.matmul(out[:, t * P:(t + 1) * P], f.hid[:, e % 2, j, t * P:(t + 1) * P],
                                 f.w2[:, (e * NB + j) * P:(e * NB + j + 1) * P], start=j == 0, stop=j == NB - 1)
        last.then_inc(f.out, 1)

    def logits(b, u):
        xt = m.xt[:, b[1] % 2, 1:S + 1]
        xt_ready(pe, s, b, stage)
        if b[1]:
            pe.wait_ge(f.gates_kept, count(u, 1, 0))
        for t in range(TILES):
            last = pe.matmul(m.bank[1][:, t * E:(t + 1) * E], xt[:, t * P:(t + 1) * P], f.wr[:, :], start=True, stop=True)
        last.then_inc(f.logits, 1)

    def second_biases(b, u):
        for t in range(TILES):
            last = pe.transpose(m.bank[1][0:E, t * P:(t + 1) * P], f.gates[:, b[1] % 2, t, :], m.ident[:, :])
        last.then_inc(f.gates_turned, 1)
        pe.wait_ge(f.gates_kept, count(u, 1, 2))
        pe.wait_ge(f.added, count(u, outs, E + 1))
        out = m.bank[6 + (b[1] * outs + E) % 2]
        for t in range(TILES):
            last = pe.matmul(out[:, t * P:(t + 1) * P], m.gates_t[0:E, t * P:(t + 1) * P], f.b2[:, :], start=True, stop=True)
        last.then_inc(f.out, 1)

    def body(new, now):
        v = after(new, BATCHES * f.use) if new else None
        if not now:
            transpose_batch(pe, nc, m, s, new, stage)
            logits(new, v)
            return
        u = after(now, BATCHES * f.use)
        for e in range(E):
            if e == AHEAD and new:
                transpose_batch(pe, nc, m, s, new, stage)
            first_layer(now, u, e)
            if e:
                second_layer(now, u, e - 1)
            if e == AHEAD and new:
                logits(new, v)
        second_layer(now, u, E - 1)
        pe.wait_ge(f.gates_made, count(u, 1, 1))
        if new:
            pe.wait_ge(f.shifted, count(v, 1, 1))
        second_biases(now, u)

    rounds(pe, body, 2)


def experts_scalar(act, nc, m, s, f, stage):
    NB, E = f.blocks, 8
    outs = E + 1
    if f.use == 0:
        credit(act, f.hidden, 4)
        credit(act, f.gates_kept, 1)

    def keep(b):
        act.wait_ge(s.transposed, count(b, 1, 8 * stage + 3))
        act.activation(f.xh[:, b[1] % 2, :], m.bank[0][:, :], ACT.Copy).then_inc(f.x_high, 1)
        keep_transposed(act, nc, m, s, b, stage)

    def exponentials(v):
        act.wait_ge(f.shifted, count(v, 1, 1))
        act.activation(m.r_exp[:, :], m.r_d[:, :], ACT.Exp).then_inc(f.exps, 1)

    def body(new, now):
        v = after(new, BATCHES * f.use) if new else None
        if not now:
            keep(new)
            exponentials(v)
            return
        u = after(now, BATCHES * f.use)
        for e in range(E):
            if e == AHEAD and new:
                keep(new)
            act.wait_ge(f.out, count(u, outs, e + 2 if e >= 2 else e + 1))
            for j in range(NB):
                n = e * NB + j
                act.wait_ge(f.first, count(u, E * NB, n + 1))
                act.activation(f.hid[:, e % 2, j, :], m.bank[2 + n % 4][:, :], f.func,
                               bias=f.b1[:, n:n + 1]).then_inc(f.hidden, 1)
        if new:
            exponentials(v)
        act.wait_ge(f.gates_turned, count(u, 1, 1))
        act.activation(m.gates_t[0:E, :], m.bank[1][0:E, :], ACT.Copy).then_inc(f.gates_kept, 1)

    rounds(act, body, 2)


def experts_pool(pool, nc, m, s, f, stage):
    normalise(pool, nc, m, s, (0, 1), stage)
    with pool.Fori(0, BATCHES // 2 - 1) as loop:
        for n in range(2, 4):
            normalise(pool, nc, m, s, (loop, n), stage)


def experts_vector(dve, nc, m, s, f, stage):
    E = 8
    outs = E + 1
    if f.use == 0:
        credit(dve, f.added, 2)
    steps = Steps(dve, f.steps, 8 if f.top == 1 else 21)
    ahead = Steps(dve, f.ahead_steps, 3)

    def wide(column):
        return column.unsqueeze(2).to_broadcast([P, TILES, E])

    order = m.order[:, :].rearrange("p (t e) -> p t e", e=E)

    def first_largest(source, hot, peak, top):
        steps.done(dve.tensor_tensor(hot, source, wide(peak), ALU.is_equal))
        steps.done(dve.tensor_tensor(hot, hot, order, ALU.mult))
        steps.done(dve.reduce_max(top, hot, AX_X))
        steps.done(dve.tensor_tensor(hot, hot, wide(top), ALU.is_equal))

    def x_rest(b, u):
        h = b[1] % 2
        dve.wait_ge(f.x_high, count(u, 1, 1))
        xt_ready(dve, s, b, stage)
        dve.tensor_tensor(f.xl[:, h, :], m.xt[:, h, 1:S + 1], f.xh[:, h, :].bitcast(F32), ALU.subtract).then_inc(f.x_low, 1)

    def split(e):
        dve.tensor_copy(f.w_high[:, e, :], f.w1[:, e, :]).then_inc(f.split, 1)
        dve.wait_ge(f.split, 2 * E * f.use + 2 * e + 1)
        dve.tensor_tensor(f.w_low[:, e, :], f.w1[:, e, :], f.w_high[:, e, :].bitcast(F32), ALU.subtract).then_inc(f.split, 1)

    def route(b, u):
        steps.begin(u)
        gates = f.gates[:, b[1] % 2, :, :]
        lg, d, ex = (v.rearrange("p (t e) -> p t e", e=E) for v in (m.r_l[:, :], m.r_d[:, :], m.r_exp[:, :]))
        hot = m.r_hot[:, :].rearrange("p (t e) -> p t e", e=E)
        two = m.r_two[:, :].rearrange("p (t e) -> p t e", e=E)
        peak, top, total = m.r_col[:, 0, :], m.r_col[:, 1, :], m.r_col[:, 2, :]
        dve.wait_ge(f.logits, count(u, 1, 1))
        ps = m.bank[1][:, 0:TILES * E]
        if f.top == 1:
            steps.done(dve.tensor_tensor(m.r_l[:, :], ps, f.br, ALU.add))
        else:
            steps.done(dve.tensor_copy(m.r_l[:, :], ps))
        steps.done(dve.reduce_max(peak, lg, AX_X))
        dve.tensor_tensor(d, lg, wide(peak), ALU.subtract).then_inc(f.shifted, 1)
        if f.top == 1:
            first_largest(lg, hot, peak, top)
            dve.wait_ge(f.exps, count(u, 1, 1))
            steps.done(dve.reduce_sum(total, ex, AX_X))
            steps.done(dve.reciprocal(total, total))
            dve.tensor_tensor(gates, hot, wide(total), ALU.mult).then_inc(f.gates_made, 1)
        else:
            dve.wait_ge(f.exps, count(u, 1, 1))
            steps.done(dve.reduce_sum(total, ex, AX_X))
            steps.done(dve.reciprocal(total, total))
            steps.done(dve.tensor_tensor(ex, ex, wide(total), ALU.mult))
            steps.done(dve.reduce_max(peak, ex, AX_X))
            first_largest(ex, hot, peak, top)
            steps.done(dve.scalar_tensor_tensor(m.r_l[:, :], m.r_hot[:, :], -2.0, m.r_exp[:, :], ALU.mult, ALU.add))
            steps.done(dve.reduce_max(peak, lg, AX_X))
            first_largest(lg, two, peak, top)
            steps.done(dve.tensor_tensor(two, two, hot, ALU.add))
            steps.done(dve.tensor_tensor(ex, ex, two, ALU.mult))
            steps.done(dve.reduce_sum(total, ex, AX_X))
            steps.done(dve.tensor_scalar(total, total, 1e-12, None, ALU.max))
            steps.done(dve.reciprocal(total, total))
            dve.tensor_tensor(gates, ex, wide(total), ALU.mult).then_inc(f.gates_made, 1)

    def body(new, now):
        if new:
            v = after(new, BATCHES * f.use)
            ahead.begin(v)
        if not now:
            split(0)
            x_rest(new, v)
            split(1)
            split(2)
            route(new, v)
            take_statistics(dve, nc, m, s, after(new, 1), stage, ahead)
            for e in range(3, E):
                split(e)
            return
        u = after(now, BATCHES * f.use)
        dve.wait_ge(f.gates_made, count(u, 1, 1))
        for e in range(outs):
            if new and e == 1:
                take_statistics(dve, nc, m, s, after(new, 1), stage, ahead)
            if new and e == AHEAD + 1:
                x_rest(new, v)
                route(new, v)
            dve.wait_ge(f.out, count(u, outs, e + 4))
            dve.wait_ge(f.added, count(u, outs, e + 2))
            out = m.bank[6 + (now[1] * outs + e) % 2]
            if e < E:
                for t in range(TILES):
                    last = dve.scalar_tensor_tensor(m.x[:, rows(now, t, 1)], out[:, t * P:(t + 1) * P],
                                                    f.gates[:, now[1] % 2, t, e:e + 1], m.x[:, rows(now, t, 1)], ALU.mult, ALU.add)
            else:
                last = dve.tensor_tensor(m.x[:, rows(now)], out[:, :], m.x[:, rows(now)], ALU.add)
            last.then_inc(f.added, 1)

    rounds(dve, body, 2)






def rwkv_tensor(pe, nc, m, s, f, stage):
    pe.wait_ge(f.weights_mixed, 6)

    def body(new, now, late, done):
        if new:
            h = new[1] % 2
            after_it, before = m.xt[:, h, 1:S + 1], m.xt[:, h, 0:S]
            transpose_batch(pe, nc, m, s, new, stage)
            xt_ready(pe, s, new, stage)
            if new[1]:
                pe.wait_ge(f.k_kept, count(new, 1, 0))
            if late:
                pe.wait_ge(f.vr_kept, count(late, 2, 2))
            for n, bank in enumerate((2, 3 + h, 5 + h)):
                pe.matmul(m.bank[bank][:, :], f.w_now[:, n, :], after_it, start=True, stop=False)
                pe.matmul(m.bank[bank][:, :], f.w_before[:, n, :], before, start=False, stop=True).then_inc(f.kvr, 1)
        if late:
            pe.wait_ge(f.mixed, count(late, 1, 1))
            pe.wait_ge(f.added, count(late, 1, 1))
            for t in range(TILES):
                last = pe.matmul(m.bank[1][:, t * P:(t + 1) * P], f.rw[:, t * P:(t + 1) * P], f.wo[:, :], start=True, stop=True)
            last.then_inc(f.out, 1)

    rounds(pe, body, 4)


def rwkv_scalar(act, nc, m, s, f, stage):
    act.wait_ge(f.decayed, 1)

    def body(new, now, late, done):
        if new:
            keep_transposed(act, nc, m, s, new, stage)
        if now:
            h = now[1] % 2
            if done:
                act.wait_ge(f.mixed, count(done, 1, 1))
            act.wait_ge(f.kvr, count(now, 3, 3))
            act.activation(f.vr[:, h, 0, :], m.bank[3 + h][:, :], ACT.Copy).then_inc(f.vr_kept, 1)
            act.activation(f.vr[:, h, 1, :], m.bank[5 + h][:, :], ACT.Tanh, scale=0.5).then_inc(f.vr_kept, 1)
        if late:
            act.wait_ge(f.below, count(late, 1, 1))
            act.activation(f.log[:, :], f.den[:, :], ACT.Ln).then_inc(f.logs, 1)
            act.wait_ge(f.logs, count(late, 1, 1))
            act.activation(f.inverse[:, :], f.log[:, :], ACT.Exp, scale=-1.0).then_inc(f.inverses, 1)
        if now:
            act.wait_ge(f.less, count(now, 2, 2))
            act.wait_ge(f.less_pool, count(now, 2, 2))
            act.activation(f.e[:, h, 0, :], f.d[:, 0, :], ACT.Exp, bias=f.decay[:, 1:2]).then_inc(f.exps, 1)
            act.activation(f.e[:, h, 1:4, :], f.d[:, 1:4, :], ACT.Exp).then_inc(f.exps, 1)
        if new:
            if late:
                act.wait_ge(f.less, count(late, 2, 2))
            act.wait_ge(f.kvr, count(new, 3, 1))
            act.activation(f.k[:, new[1] % 2, :], m.bank[2][:, :], ACT.Copy).then_inc(f.k_kept, 1)

    rounds(act, body, 4)


def rwkv_vector(dve, nc, m, s, f, stage):
    credit(dve, f.added, 1)
    steps = Steps(dve, f.steps, 3)
    ahead = Steps(dve, f.ahead_steps, 3)
    u = f.first[:, :]

    def body(new, now, late, done):
        if late:
            h = late[1] % 2
            v, tanh_r = f.vr[:, h, 0, :], f.vr[:, h, 1, :]
            steps.begin(late)
            dve.wait_ge(f.exps, count(late, 2, 2))
            dve.tensor_tensor_scan(f.sum_w[:, h, 1:S + 1], f.e[:, h, 0, :], f.e[:, h, 1, :], 0.0, ALU.mult, ALU.add).then_inc(f.sums, 1)
            steps.mark(dve.tensor_tensor(f.ev[:, :], f.e[:, h, 1, :], v, ALU.mult))
        if now:
            n = now[1] % 2
            k, old, largest = f.k[:, n, :], f.largest[:, n, 0:S], f.largest[:, n, 1:S + 1]
            dve.wait_ge(f.k_kept, count(now, 1, 1))
            dve.tensor_tensor_scan(largest, f.decay[:, 1:2].to_broadcast([P, S]), k, -BIG, ALU.add, ALU.max).then_inc(f.maxima, 1)
        if late:
            steps.need()
            dve.tensor_tensor_scan(f.sum_wv[:, h, 1:S + 1], f.e[:, h, 0, :], f.ev[:, :], 0.0, ALU.mult, ALU.add).then_inc(f.sums, 1)
        if now:
            dve.wait_ge(f.maxima, count(now, 1, 1))
            dve.scalar_tensor_tensor(f.top[:, :], k, u, old, ALU.add, ALU.max).then_inc(f.tops, 1)
            dve.tensor_tensor(f.d[:, 1, :], k, largest, ALU.subtract).then_inc(f.less, 1)
            dve.wait_ge(f.tops, count(now, 1, 1))
            dve.scalar_tensor_tensor(f.d[:, 3, :], k, u, f.top[:, :], ALU.add, ALU.subtract).then_inc(f.less, 1)
        if late:
            dve.tensor_tensor(f.num[:, :], f.e[:, h, 3, :], v, ALU.mult).then_inc(f.terms, 1)
            dve.wait_ge(f.scaled, count(late, 2, 1))
            dve.tensor_tensor(f.den[:, :], f.ew[:, 0, :], f.e[:, h, 3, :], ALU.add).then_inc(f.below, 1)
        if done:
            dve.wait_ge(f.out, count(done, 1, 1))
            dve.tensor_tensor(m.x[:, rows(done)], m.bank[1][:, :], m.x[:, rows(done)], ALU.add).then_inc(f.added, 1)
        if late:
            dve.wait_ge(f.terms, count(late, 1, 1))
            dve.wait_ge(f.scaled, count(late, 2, 2))
            steps.mark(dve.tensor_tensor(f.num[:, :], f.ew[:, 1, :], f.num[:, :], ALU.add))
        if new:
            if done:
                dve.wait_ge(f.added, count(done, 1, 2))
            ahead.begin(new)
            take_statistics(dve, nc, m, s, after(new, 1), stage, ahead)
        if late:
            steps.need()
            steps.done(dve.scalar_tensor_tensor(f.num[:, :], tanh_r, 1.0, f.num[:, :], ALU.add, ALU.mult))
            dve.wait_ge(f.inverses, count(late, 1, 1))
            dve.scalar_tensor_tensor(f.rw[:, :], f.num[:, :], 0.5, f.inverse[:, :], ALU.mult, ALU.mult).then_inc(f.mixed, 1)

    rounds(dve, body, 4)


def rwkv_pool(pool, nc, m, s, f, stage):
    def body(ahead, new, now, late):
        if late:
            h = late[1] % 2
            pool.wait_ge(f.sums, count(late, 2, 1))
            pool.tensor_tensor(f.ew[:, 0, :], f.e[:, h, 2, :], f.sum_w[:, h, 0:S], ALU.mult).then_inc(f.scaled, 1)
        if now:
            n = now[1] % 2
            pool.wait_ge(f.maxima, count(now, 1, 1))
            pool.tensor_tensor(f.d[:, 0, :], f.largest[:, n, 0:S], f.largest[:, n, 1:S + 1], ALU.subtract).then_inc(f.less_pool, 1)
        if late:
            pool.wait_ge(f.sums, count(late, 2, 2))
            pool.tensor_tensor(f.ew[:, 1, :], f.e[:, h, 2, :], f.sum_wv[:, h, 0:S], ALU.mult).then_inc(f.scaled, 1)
        if now:
            pool.wait_ge(f.tops, count(now, 1, 1))
            pool.tensor_tensor(f.d[:, 2, :], f.largest[:, n, 0:S], f.top[:, :], ALU.subtract).then_inc(f.less_pool, 1)
        if ahead and ahead[1]:
            normalise(pool, nc, m, s, ahead, stage)

    rounds(pool, body, 4)



NHEADS, HD = 16, 8
HALF_HEADS = NHEADS // 2
PAIRS = [(i, j) for i in range(3) for j in range(3)]
ONES = len(PAIRS) * HD
SLOTS = 16
RING = 3 + SLOTS * TILES
TAKE_V = 2
TAKE_QK = 5
QK = TAKE_QK * TILES + 1
STACKS = 16 * (2 * len(PAIRS) + 1)


def ring(b, n):
    return count(b, RING, 2 + n), 2 + (b[1] + n) % 2


def score_place(slot, tile, with_qk):
    n = slot * TILES + tile
    if slot >= TAKE_V:
        n += 1
    return n + 2 if slot >= TAKE_QK and with_qk else n


def heads_fill(pool, s, f, stage):
    pool.wait_ge(s.normed, BATCHES * stage + 3)
    pool.memset(f.qs[64:P, :, :, :], 0.0).then_inc(f.stack_cleared, 1)
    pool.wait_ge(f.stack_cleared, 1)
    pool.memset(f.ks[64:P, :, :, :], 1.0).then_inc(f.stack_cleared, 1)
    pool.wait_ge(f.stack_cleared, 2)


def heads_tensor(pe, nc, m, s, f, stage):
    credit(pe, f.scored, 4 * SLOTS)
    credit(pe, f.summed, 2)
    credit(pe, f.turned, 1)

    def take_qk(new, now):
        xt_ready(pe, s, new, stage)
        for n, w in ((0, f.wq), (1, f.wk)):
            value, bank = ring(now, QK + n) if now else (n, 2 + n)
            pe.wait_ge(f.ring_read, value + 1)
            pe.matmul(m.bank[bank][:, :], w[:, :], m.xt[:, new[1] % 2, 1:S + 1], start=True, stop=True).then_inc(f.ring_made, 1)

    def take_v(now):
        value, bank = ring(now, TAKE_V * TILES)
        xt = m.xt[:, now[1] % 2, 1:S + 1]
        pe.wait_ge(f.ring_read, value + 1)
        for t in range(TILES):
            last = pe.matmul(m.bank[bank][:, t * P:(t + 1) * P], xt[:, t * P:(t + 1) * P], f.wv[:, :], start=True, stop=True)
        last.then_inc(f.ring_made, 1)

    def scores(now, head, tile, with_qk):
        value, bank = ring(now, score_place(head, tile, with_qk))
        h = now[1] % 2
        pe.wait_ge(f.ring_read, value + 1)
        pe.matmul(m.bank[bank][:, :], f.qs[:, h, head, tile * P:(tile + 1) * P], f.ks[:, h, head, :],
                  start=True, stop=True).then_inc(f.ring_made, 1)

    def shifted_scores(b, slot, n):
        group, tile, h = slot // 4, slot % 4, b[1] % 2
        pe.wait_ge(f.exps, count(b, 2 * SLOTS, 2 * slot + n + 1))
        for j in (2 * n, 2 * n + 1):
            head = 4 * group + j
            last = pe.matmul(m.bank[4 + j][:, :], f.ks[:, h, head, tile * P:(tile + 1) * P], f.qs[:, h, head, :],
                             start=True, stop=True)
        last.then_inc(f.scored, 1)

    def weighted_sums(b, slot):
        group, tile, h = slot // 4, slot % 4, b[1] % 2
        if tile == 0:
            pe.wait_ge(f.out_kept, count(b, 4, group + 1))
        pe.wait_ge(f.exps, count(b, 2 * SLOTS, 2 * slot + 2 + 2))
        for j in range(4):
            last = pe.matmul(m.bank[1][32 * j:32 * j + 32, :], f.v[:, h, tile, 4 * group + j, :], f.p[:, slot % 2, j, :],
                             start=tile == 0, stop=tile == 3)
        last.then_inc(f.summed, 1)

    def turn_maxima(b, half):
        pe.wait_ge(f.half_maxima, count(b, 2, half + 1))
        for t in range(TILES):
            last = pe.transpose(m.bank[0][0:HALF_HEADS, t * P:(t + 1) * P],
                                f.maxima[:, t, half * HALF_HEADS:(half + 1) * HALF_HEADS], m.ident[:, :])
        last.then_inc(f.maxima_turned, 1)

    def turn_sums(b, group):
        pe.wait_ge(f.out_kept, count(b, 4, group + 1 + 1))
        for t in range(TILES):
            last = pe.transpose(m.bank[0][:, t * P:(t + 1) * P], f.o[:, t * P:(t + 1) * P], m.ident[:, :])
        last.then_inc(f.turned, 1)

    def body(new, now, former):
        for slot in range(SLOTS):
            if slot == TAKE_V and now:
                take_v(now)
            if slot == TAKE_QK and new:
                take_qk(new, now)
            if now:
                if slot % HALF_HEADS == 0:
                    pe.wait_ge(f.stacked[slot // HALF_HEADS], count(now, STACKS, STACKS))
            for tile in range(TILES):
                if now:
                    scores(now, slot, tile, bool(new))
                if former and tile == 0 and slot % HALF_HEADS == 0:
                    pe.wait_ge(f.lowered[slot // HALF_HEADS], count(former, 48, 48))
                if former and tile < 2:
                    shifted_scores(former, slot, tile)
                if former and slot and tile == 2:
                    weighted_sums(former, slot - 1)
            if new and slot == TAKE_QK - 1:
                if former:
                    pe.wait_ge(f.less_rests, count(former, 2, 2))
                transpose_batch(pe, nc, m, s, new, stage)
            if former and slot == 2:
                pe.wait_ge(f.added, count(former, 4, 1))
                turn_maxima(former, 1)
            if slot in (6, 10, 14) and former:
                group = slot // 4 - 1
                if group == 0:
                    pe.wait_ge(f.less_rests, count(former, 2, 2))
                pe.wait_ge(f.added, count(former, 4, group + 1))
                if group == 2 and now:
                    pe.wait_ge(f.less_rests, count(now, 2, 1))
                turn_sums(former, group)
            if now and slot == 12:
                if former:
                    pe.wait_ge(f.added, count(former, 4, 3))
                turn_maxima(now, 0)
        if former:
            weighted_sums(former, SLOTS - 1)
            pe.wait_ge(f.added, count(former, 4, 4))
            turn_sums(former, 3)

    rounds(pe, body)


def heads_scalar(act, nc, m, s, f, stage):
    credit(act, f.exps, 2)
    credit(act, f.out_kept, 1)

    def highs(new, now):
        if new[1]:
            for half in range(2):
                act.wait_ge(f.stacked[half], count(new, STACKS, 0))
        for n in range(2):
            value, bank = ring(now, QK + n) if now else (n, 2 + n)
            act.wait_ge(f.ring_made, value + 1)
            act.activation(f.part[:, n, 0, :], m.bank[bank][:, :], ACT.Copy).then_inc(f.highs, 1)

    def minus_maxima(b, half):
        act.wait_ge(f.maxima_turned, count(b, 2, half + 1))
        if half or b[1]:
            act.wait_ge(f.lowered[1 - half], count(b, 48, 48 * half))
        act.activation(f.less[:, 0, :], m.bank[0][0:HALF_HEADS, :], ACT.Copy, scale=-1.0).then_inc(f.less_highs, 1)

    def body(new, now, former):
        for slot in range(SLOTS):
            if slot == TAKE_QK and new:
                highs(new, now)
            if former:
                act.wait_ge(f.summed, count(former, SLOTS, slot + 1))
                for n in range(2):
                    act.wait_ge(f.scored, count(former, 2 * SLOTS, 4 * SLOTS + 2 * slot + n + 1))
                    act.activation(f.p[:, slot % 2, 2 * n:2 * n + 2, :], m.banks[:, 4 + 2 * n:6 + 2 * n, :], ACT.Exp,
                                   scale=1.0 / math.sqrt(HD)).then_inc(f.exps, 1)
                if slot and slot % 4 == 0:
                    keep_sums(former, slot // 4 - 1)
                if slot == 2:
                    minus_maxima(former, 1)
            if new and slot == TAKE_QK - 1:
                keep_transposed(act, nc, m, s, new, stage)
            if now and slot == 12:
                minus_maxima(now, 0)
        if former:
            keep_sums(former, 3)

    def keep_sums(b, group):
        act.wait_ge(f.summed, count(b, SLOTS, 2 + 4 * group + 4))
        act.wait_ge(f.turned, count(b, 4, group + 1))
        act.activation(f.o[:, :], m.bank[1][:, :], ACT.Copy).then_inc(f.out_kept, 1)

    rounds(act, body)


def heads_vector(dve, nc, m, s, f, stage):
    credit(dve, f.ring_read, 2)
    credit(dve, f.added, 1)
    steps = Steps(dve, f.steps, 4 * 2)

    def rests(new, now):
        for n in range(2):
            value, bank = ring(now, QK + n) if now else (n, 2 + n)
            dve.wait_ge(f.highs, count(new, 2, n + 1))
            dve.tensor_tensor(f.rest[:, n, :], m.bank[bank][:, :], f.part[:, n, 0, :], ALU.subtract).then_inc(f.ring_read, 1)

    def keep_v(now):
        value, bank = ring(now, TAKE_V * TILES)
        dve.wait_ge(f.ring_made, value + 1)
        dve.tensor_copy(f.v[:, now[1] % 2, :, :, 0:HD], m.bank[bank][:, :].rearrange("p (t h d) -> p t h d", t=TILES, h=NHEADS)
                        ).then_inc(f.ring_read, 1)

    def maxima(now, head, with_qk):
        for tile in range(TILES):
            value, bank = ring(now, score_place(head, tile, with_qk))
            dve.wait_ge(f.ring_made, value + 1)
            dve.reduce_max(f.maxima[:, tile, head:head + 1], m.bank[bank][:, :], AX_X).then_inc(f.ring_read, 1)
        if head % HALF_HEADS == HALF_HEADS - 1:
            dve.wait_ge(f.ring_read, value + 1 + 2)
            dve.nop().then_inc(f.half_maxima, 1)

    def rest_of_maxima(b, half):
        dve.wait_ge(f.less_highs, count(b, 2, half + 1))
        dve.scalar_tensor_tensor(f.less_rest[:, :], m.bank[0][0:HALF_HEADS, :], -1.0, f.less[:, 0, :],
                                 ALU.mult, ALU.subtract).then_inc(f.less_rests, 1)

    def add_sums(b, group):
        o = m.bank[0][:, :].rearrange("p (t j c) -> p t j c", t=TILES, j=4)
        x = m.x[:, rows(b)].rearrange("p (t h d) -> p t h d", t=TILES, h=NHEADS)[:, :, 4 * group:4 * group + 4, :]
        dve.wait_ge(f.turned, count(b, 4, group + 1 + 1))
        steps.b, steps.n = b, 2 * group
        steps.done(dve.reciprocal(f.inverse[:, :, :], o[:, :, :, HD]))
        steps.done(dve.tensor_tensor(f.mean[:, :, :, :], o[:, :, :, 0:HD], f.inverse[:, :, :].unsqueeze(3).to_broadcast([P, TILES, 4, HD]),
                                     ALU.mult))
        dve.tensor_tensor(x, f.mean[:, :, :, :], x, ALU.add).then_inc(f.added, 1)
        dve.wait_ge(f.added, count(b, 4, group + 2))

    def body(new, now, former):
        for slot in range(SLOTS):
            if slot == TAKE_V and now:
                keep_v(now)
            if slot == TAKE_QK and new:
                rests(new, now)
            if now:
                maxima(now, slot, bool(new))
            if former and slot == 3:
                rest_of_maxima(former, 1)
            if new and slot == 9:
                ahead_steps.b, ahead_steps.n = new, 0
                take_statistics(dve, nc, m, s, after(new, 1), stage, ahead_steps)
            if former and slot in (7, 11, 15):
                add_sums(former, slot // 4 - 1)
            if now and slot == 13:
                rest_of_maxima(now, 0)
        if former:
            add_sums(former, 3)

    ahead_steps = Steps(dve, f.ahead_steps, 3)
    dve.memset(f.v[:, :, :, :, :], 0.0).then_inc(f.cleared, 1)
    dve.wait_ge(f.cleared, 1)
    dve.memset(f.v[:, :, :, :, HD:HD + 1], 1.0).then_inc(f.cleared, 1)
    dve.wait_ge(f.cleared, 2)
    rounds(dve, body)


def heads_pool(pool, nc, m, s, f, stage):
    def less(b, half):
        pool.wait_ge(f.less_rests, count(b, 2, half + 1))
        pool.tensor_tensor(f.less[:, 1, :], f.less_rest[:, :], f.zero[0:HALF_HEADS, :].to_broadcast([HALF_HEADS, S]), ALU.add).then_inc(f.less_middles, 1)
        pool.wait_ge(f.less_middles, count(b, 2, half + 1))
        pool.tensor_tensor(f.less[:, 2, :], f.less_rest[:, :], f.less[:, 1, :], ALU.subtract).then_inc(f.less_parted, 1)

    def body(new, now, former):
        if new and new[1]:
            normalise(pool, nc, m, s, new, stage)
        if former:
            less(former, 1)
        if new:
            value = ring(now, QK + 2)[0] if now else 2
            pool.wait_ge(f.ring_read, value + 2)
            pool.tensor_tensor(f.part[:, :, 1, :], f.rest[:, :, :], f.zero[:, :].unsqueeze(2).to_broadcast([P, 2, S]), ALU.add).then_inc(f.middles, 1)
            pool.wait_ge(f.middles, count(new, 1, 1))
            pool.tensor_tensor(f.part[:, :, 2, :], f.rest[:, :, :], f.part[:, :, 1, :], ALU.subtract).then_inc(f.parted, 1)
        if now:
            less(now, 0)

    pool.wait_ge(s.normed, BATCHES * stage + 3)
    pool.memset(f.nothing[:, :], 0.0)
    pool.memset(f.zero[:, :], 0.0).then_inc(f.zeroed, 1)
    pool.wait_ge(f.zeroed, 1)
    rounds(pool, body)


def heads_sync(sp, nc, m, s, f, stage):
    def stack(b, half):
        h, heads = b[1] % 2, slice(half * HALF_HEADS, (half + 1) * HALF_HEADS)
        free = sp.to_reg(count(b, 2 * SLOTS, SLOTS * (half + 1)))
        high, other = sp.to_reg(count(b, 2, 2)), sp.to_reg(count(b, 1, 1))
        sp.wait_ge(f.scored, free)
        rows_of = slice(half * HALF_HEADS * HD, (half + 1) * HALF_HEADS * HD)
        for part, (made, value) in enumerate(((f.highs, high), (f.middles, other), (f.parted, other))):
            sp.wait_ge(made, value)
            for pair, parts in enumerate(PAIRS):
                for n, stacked in ((0, f.qs), (1, f.ks)):
                    if parts[n] == part:
                        sp.dma_start(stacked[pair * HD:(pair + 1) * HD, h, heads, :],
                                     f.part[rows_of, n, part, :]).then_inc(f.stacked[half], 16)
        sp.dma_start(f.qs[ONES:ONES + 3, h, heads, :], f.nothing[0:3, :].unsqueeze(1).to_broadcast([3, HALF_HEADS, S])).then_inc(f.stacked[half], 16)

    def lower(b, half):
        h, heads = b[1] % 2, slice(half * HALF_HEADS, (half + 1) * HALF_HEADS)
        sp.wait_ge(f.less_parted, count(b, 2, half + 1))
        for part in range(3):
            sp.dma_start(f.qs[ONES + part:ONES + part + 1, h, heads, :], f.less[:, part, :]).then_inc(f.lowered[half], 16)

    def body(new, now, former):
        if former:
            lower(former, 1)
        if new:
            stack(new, 0)
        if now:
            lower(now, 0)
        if new:
            stack(new, 1)

    sp.wait_ge(f.stack_cleared, 2)
    sp.wait_ge(f.zeroed, 1)
    rounds(sp, body)



DEVIATION = math.sqrt(0.25 * math.pi)
TINY = 2.0 ** -24
CENTRE = math.sqrt(0.5)
STARTS = [sum(S - i * P for i in range(j)) for j in range(TILES + 1)]
PAIRED = STARTS[TILES]


def laplace_tensor(pe, nc, m, s, f, stage):
    def body(new, now, late, done):
        if new:
            xt = m.xt[:, new[1] % 2, 1:S + 1]
            transpose_batch(pe, nc, m, s, new, stage)
            xt_ready(pe, s, new, stage)
            if new[1]:
                pe.wait_ge(f.queries, count(new, 1, 0))
            pe.matmul(m.bank[2][:, :], f.wqk[:, :], xt, start=True, stop=True).then_inc(f.shared, 1)
            if new[1]:
                pe.wait_ge(f.values_biased, count(new, 1, 0))
            for t in range(TILES):
                last = pe.matmul(m.bank[3][:, t * P:(t + 1) * P], xt[:, t * P:(t + 1) * P], f.wv[:, :], start=True, stop=True)
            last.then_inc(f.values, 1)
            pe.wait_ge(f.queries, count(new, 1, 1))
            pe.wait_ge(f.keys, count(new, 1, 1))
            if new[1]:
                pe.wait_ge(f.arguments, count(new, TILES, 0))
            for j in range(TILES):
                pe.matmul(m.bank[4 + j][:, 0:S - j * P], f.k[:, j * P:(j + 1) * P], f.q[:, j * P:S],
                          start=True, stop=True).then_inc(f.scores, 1)
        if late:
            h = late[1] % 2
            pe.wait_ge(f.values_made, count(late, 1, 1))
            pe.wait_ge(f.added, count(late, 1, 1))
            pe.wait_ge(f.weights, count(late, 2, 2))
            for i in range(TILES):
                for j in range(i + 1):
                    at = STARTS[j] + (i - j) * P
                    last = pe.matmul(m.bank[1][:, i * P:(i + 1) * P], f.p[:, at:at + P],
                                     f.v[:, h, j * P:(j + 1) * P], start=j == 0, stop=j == i)
            last.then_inc(f.out, 1)

    rounds(pe, body, 4)


def laplace_scalar(act, nc, m, s, f, stage):
    steps = Steps(act, f.scalar_steps, 1)

    def body(new, now, late, done):
        if new:
            h = new[1] % 2
            keep_transposed(act, nc, m, s, new, stage)
            act.wait_ge(f.shared, count(new, 1, 1))
            if new[1]:
                act.wait_ge(f.queries, count(new, 1, 0))
            act.activation(f.sq[:, :], m.bank[2][:, :], ACT.Sigmoid, bias=f.bqk[:, :]).then_inc(f.gates, 1)
            act.wait_ge(f.values_biased, count(new, 1, 1))
            if late:
                act.wait_ge(f.values_made, count(late, 1, 1))
            act.activation(f.sv[:, h, :], f.vb[:, h, :], ACT.Sigmoid).then_inc(f.value_gates, 1)
        if now:
            n = now[1] % 2
            if done:
                act.wait_ge(f.weights, count(done, 2, 2))
            act.wait_ge(f.sizes, count(now, 1, 1))
            act.activation(f.g[:, n, :], f.size[:, n, :], ACT.Gelu)
            steps.begin(now)
            steps.done(act.activation(f.inverse[:, n, :], f.size[:, n, :], ACT.Ln))
            act.activation(f.inverse[:, n, :], f.inverse[:, n, :], ACT.Exp, scale=-1.0).then_inc(f.inverses, 1)
            act.activation(f.sign[:, n, :], f.y[:, n, :], ACT.Sign).then_inc(f.signs, 1)
        if new:
            act.wait_ge(f.arguments, count(new, TILES, TILES))
            act.activation(f.size[:, h, :], f.y[:, h, :], ACT.Abs).then_inc(f.absolutes, 1)

    rounds(act, body, 4)


def laplace_vector(dve, nc, m, s, f, stage):
    credit(dve, f.added, 1)
    dve.wait_ge(f.skewed, 16)
    steps = Steps(dve, f.steps, 1)
    ahead = Steps(dve, f.ahead_steps, 3)

    def body(new, now, late, done):
        if done:
            dve.wait_ge(f.out, count(done, 1, 1))
            dve.tensor_tensor(m.x[:, rows(done)], m.bank[1][:, :], m.x[:, rows(done)], ALU.add).then_inc(f.added, 1)
        if new:
            if done:
                dve.wait_ge(f.added, count(done, 1, 2))
            ahead.begin(new)
            take_statistics(dve, nc, m, s, after(new, 1), stage, ahead)
        if late:
            g = f.g[:, late[1] % 2, :]
            dve.wait_ge(f.inverses, count(late, 1, 1))
            dve.tensor_tensor(g, g, f.inverse[:, late[1] % 2, :], ALU.mult).then_inc(f.phis, 1)
        if new:
            dve.wait_ge(f.values, count(new, 1, 1))
            dve.tensor_tensor(f.vb[:, new[1] % 2, :], m.bank[3][:, :], f.bv[:, :], ALU.add).then_inc(f.values_biased, 1)
        if late:
            dve.wait_ge(f.phis, count(late, 1, 1))
            dve.wait_ge(f.signs, count(late, 1, 1))
            dve.scalar_tensor_tensor(g, g, -0.5, f.sign[:, late[1] % 2, :], ALU.add, ALU.mult).then_inc(f.halves, 1)
        if new:
            dve.wait_ge(f.gates, count(new, 1, 1))
            steps.begin(new)
            steps.done(dve.scalar_tensor_tensor(f.qk[:, :], m.bank[2][:, :], f.bqk[:, :], f.sq[:, :], ALU.add, ALU.mult))
            if new[1]:
                dve.wait_ge(f.scores, count(new, TILES, 0))
            dve.tensor_scalar(f.q[:, :], f.qk[:, :], f.gb[:, 0:1], f.gb[:, 2:3], ALU.mult, ALU.add).then_inc(f.queries, 1)
            dve.tensor_scalar(f.k[:, :], f.qk[:, :], f.gb[:, 1:2], f.gb[:, 3:4], ALU.mult, ALU.add).then_inc(f.keys, 1)
        if now:
            h = now[1] % 2
            dve.wait_ge(f.value_gates, count(now, 1, 1))
            dve.tensor_tensor(f.v[:, h, :], f.vb[:, h, :], f.sv[:, h, :], ALU.mult).then_inc(f.values_made, 1)
        if late:
            dve.wait_ge(f.halves, count(late, 1, 1))
            dve.tensor_scalar(f.p[:, :], g, 0.5, None, ALU.add).then_inc(f.weights, 1)
            dve.wait_ge(f.weights, count(late, 2, 1))
            for j in range(TILES):
                at = slice(STARTS[j], STARTS[j] + P)
                last = dve.tensor_tensor(f.p[:, at], f.p[:, at], f.causal[:, :], ALU.mult)
            last.then_inc(f.weights, 1)
        if new:
            h = new[1] % 2
            if late:
                dve.wait_ge(f.signs, count(late, 1, 1))
            for j in range(TILES):
                w = S - j * P
                dve.wait_ge(f.scores, count(new, TILES, j + 1))
                dve.scalar_tensor_tensor(f.y[:, h, STARTS[j]:STARTS[j] + w], m.bank[4 + j][:, 0:w], 1.0 / (S * DEVIATION),
                                         f.toeplitz[:, 0:w], ALU.mult, ALU.add).then_inc(f.arguments, 1)
            size = f.size[:, h, :]
            dve.wait_ge(f.absolutes, count(new, 1, 1))
            dve.tensor_scalar(size, size, TINY, 8.0, ALU.max, ALU.min).then_inc(f.sizes, 1)

    rounds(dve, body, 4)



HALVES, GROUPS, STATES = 2, 16, 16
NG = HALVES * GROUPS
JUST = P // GROUPS
TAPS = 4
SMALL_EXP = 2.0 ** -7
QUAD = 4
KEPT = 7


def channel_group(i):
    return i % 4 * 4 + i // 4




def mamba_tensor(pe, nc, m, s, f, stage):
    def spread(b, n):
        half, g = divmod(n, GROUPS)
        h = b[1] % 2
        chosen = f.choose[:, channel_group(g), :]
        pe.wait_ge(f.decays, count(b, NG, n + 1))
        pe.matmul(m.bank[2 + n % 2][:, :], chosen, f.high[:, h, 0, half, :], start=True, stop=False)
        pe.matmul(m.bank[2 + n % 2][:, :], chosen, f.low[:, h, 0, half, :], start=False, stop=True).then_inc(f.spread, 1)
        pe.wait_ge(f.driven, count(b, NG, n + 1))
        pe.matmul(m.bank[4 + n % 2][:, :], chosen, f.high[:, h, 1, half, :], start=True, stop=False)
        pe.matmul(m.bank[4 + n % 2][:, :], chosen, f.low[:, h, 1, half, :], start=False, stop=True).then_inc(f.spread, 1)

    def add_states(b, first):
        half, within = first // GROUPS, first % GROUPS // QUAD
        if within == 0:
            pe.wait_ge(f.ended, count(b, HALVES, half + 1))
        pe.wait_ge(f.weighed, count(b, NG, first + QUAD + 8))
        for n in range(first, first + QUAD):
            quarter = n % 4
            last = pe.matmul(m.bank[6 + half][32 * quarter:32 * quarter + 32, :], f.gather[:, within, :], f.hc[:, n % 8, :],
                             start=within == 0, stop=within == 3)
        last.then_inc(f.summed, 1)

    def prepare(b, former):
        h = b[1] % 2
        xt = f.xt[:, h, :]
        yield 0
        if b[1]:
            pe.wait_ge(f.biased, count(b, 2, 0))
        transpose_batch(pe, nc, m, s, b, stage)
        yield 2
        xt_ready(pe, s, b, stage)
        for half in range(HALVES):
            for tap in range(TAPS):
                yield 2 + 2 * half + tap // 2
                last = pe.matmul(m.bank[1 - half][:, :], f.w_tap[:, half, tap, :], xt[:, tap:tap + S], start=tap == 0, stop=tap == TAPS - 1)
            last.then_inc(f.inner, 1)
        yield 7
        if former:
            result(former, b)
        for part in range(HALVES):
            yield 8 + 2 * part
            pe.wait_ge(f.kept, count(b, KEPT, 2))
            if part and former:
                pe.wait_ge(f.added, count(former, 1, 2))
            pe.matmul(m.bank[part][:, :], f.w_in[:, 2 + part, :], xt[:, TAPS - 1:], start=True, stop=True).then_inc(f.inner, 1)
        yield 11
        pe.wait_ge(f.x_made, count(b, 2, 2))
        pe.wait_ge(f.kept, count(b, KEPT, 3))
        for half in range(HALVES):
            last = pe.matmul(m.bank[0][0:JUST, :], f.w_dt[:, half, :], f.x[:, h, half, :], start=half == 0, stop=half == 1)
        last.then_inc(f.projected, 1)
        for n in range(2):
            for half in range(HALVES):
                yield 12 + 2 * n + half
                if half == 0:
                    pe.wait_ge(f.kept, count(b, KEPT, 4 + n))
                last = pe.matmul(m.bank[1 - n][:, :], f.w_bc[:, half, n, :], f.x[:, h, half, :], start=half == 0, stop=half == 1)
            last.then_inc(f.projected, 1)
        for half in range(HALVES):
            yield 16 + half
            pe.wait_ge(f.kept, count(b, KEPT, 6 + half))
            pe.matmul(m.bank[1 - half][:, :], f.w_delta[:, half, :], f.dt[:, :], start=True, stop=True).then_inc(f.delta_made, 1)

    def result(b, new):
        pe.wait_ge(f.gated, count(b, 1, 1))
        pe.wait_ge(f.added, count(b, 1, 1))
        if new:
            pe.wait_ge(f.kept, count(new, KEPT, 2))
        else:
            pe.wait_ge(f.biased, 2 * BATCHES)
        for t in range(TILES):
            for half in range(HALVES):
                last = pe.matmul(m.bank[1][:, t * P:(t + 1) * P], f.y[:, half, t * P:(t + 1) * P], f.w_out[:, half, :],
                                 start=half == 0, stop=half == 1)
        last.then_inc(f.out, 1)

    def body(new, now, former):
        steps = Beside(prepare(new, former)) if new else None
        for n in range(NG):
            if now:
                if n == 0:
                    pe.wait_ge(f.highs, count(now, 2, 2))
                    pe.wait_ge(f.lows, count(now, 2, 2))
                spread(now, n)
            if steps:
                steps.until(n)
            if former and n == 2:
                add_states(former, NG - QUAD)
            if now and n >= 6 and n % QUAD == 2:
                add_states(now, n - 6)
            if former and not new and n == 8:
                result(former, None)

    pe.wait_ge(f.chosen, 1)
    pe.wait_ge(f.taps_folded, 2 * TAPS)
    pe.wait_ge(f.padded, 1)
    rounds(pe, body)


def mamba_scalar(act, nc, m, s, f, stage):
    credit(act, f.decays, 2)
    act.activation(f.rates[:, :], f.rates[:, :], ACT.Exp).then_inc(f.rate_exps, 1)
    act.wait_ge(f.rates_ready, 1)
    steps = Steps(act, f.scalar_steps, 2)

    def prepare(b):
        h = b[1] % 2
        yield 1
        act.wait_ge(s.transposed, count(b, 1, 8 * stage + 3))
        act.activation(f.xt[:, h, TAPS - 1:], m.bank[0][:, :], ACT.Copy).then_inc(s.xt, 1)
        for half in range(HALVES):
            yield 4 + 2 * half
            act.wait_ge(f.inner, count(b, 4, half + 1))
            act.activation(f.x_tanh[:, half, :], m.bank[1 - half][:, :], ACT.Tanh, bias=f.taps[:, half, TAPS:TAPS + 1])
            act.activation(f.conv[:, half, :], m.bank[1 - half][:, :], ACT.Identity, bias=f.taps[:, half, TAPS:TAPS + 1]).then_inc(f.kept, 1)
        for half in range(HALVES):
            yield 9 + 2 * half
            act.wait_ge(f.inner, count(b, 4, half + 3))
            act.activation(f.z_half[:, half, :], m.bank[half][:, :], ACT.Copy, scale=0.5)
            act.activation(f.z_tanh[:, half, :], m.bank[half][:, :], ACT.Tanh, scale=0.5).then_inc(f.kept, 1)
        yield 12
        act.wait_ge(f.projected, count(b, 3, 1))
        act.activation(f.dt[:, :], m.bank[0][0:JUST, :], ACT.Copy).then_inc(f.kept, 1)
        if b[1] >= 2:
            act.wait_ge(f.weighed, count(b, NG, 8 - NG))
            act.wait_ge(f.driven, count(b, NG, 2 - NG))
        for n in range(2):
            yield 14 + 2 * n
            act.wait_ge(f.projected, count(b, 3, n + 2))
            act.activation(f.bc[:, h, n, :], m.bank[1 - n][:, :], ACT.Copy).then_inc(f.kept, 1)
        for half in range(HALVES):
            yield 17 + half
            act.wait_ge(f.delta_made, count(b, 2, half + 1))
            if half == 0:
                act.wait_ge(f.x_made, count(b, 2, 2))
            act.activation(f.v[:, half, :], m.bank[1 - half][:, :], ACT.Identity, bias=f.delta_bias[:, half:half + 1]).then_inc(f.biased, 1)
        act.wait_ge(f.biased, count(b, 2, 2))
        steps.begin(b)
        steps.mark(act.activation(f.small[:, :, :], f.v[:, :, :], ACT.Abs))
        yield 19
        steps.need()
        steps.mark(act.activation(f.small[:, :, :], f.small[:, :, :], ACT.Exp, scale=-1.0))
        yield 20
        steps.need()
        act.wait_ge(f.z_made, count(b, 1, 1))
        act.activation(f.delta[:, :, :], f.small[:, :, :], ACT.Ln, bias=f.one[:, :]).then_inc(f.logs, 1)
        yield 26
        act.wait_ge(f.deltas, count(b, 1, 1))
        act.activation(f.high[:, h, 0, :, :], f.delta[:, :, :], ACT.Copy).then_inc(f.highs, 1)
        yield 28
        act.wait_ge(f.inputs, count(b, 1, 1))
        act.activation(f.high[:, h, 1, :, :], f.du[:, :, :], ACT.Copy).then_inc(f.highs, 1)

    def body(new, now, former):
        beside = Beside(prepare(new)) if new else None
        for n in range(NG):
            if now:
                half, g = divmod(n, GROUPS)
                act.wait_ge(f.spread, count(now, 2 * NG, 2 * n + 1))
                act.wait_ge(f.states, count(now, NG, n + 1))
                col = half * GROUPS + channel_group(g)
                act.activation(f.keep[:, n % 4, :], m.bank[2 + n % 2][:, :], ACT.Exp,
                               scale=f.rates[:, col:col + 1]).then_inc(f.decays, 1)
            if beside:
                beside.until(n)

    rounds(act, body)


def mamba_vector(dve, nc, m, s, f, stage):
    dve.wait_ge(f.rate_exps, 1)
    dve.memset(f.one[:, :], 1.0)
    dve.tensor_scalar(f.taps[:, :, :], f.taps[:, :, :], 0.5, None, ALU.mult).then_inc(f.taps_halved, 1)
    dve.wait_ge(f.raw_loaded, 16)
    dve.tensor_copy(f.choose[:, :, :], f.raw).then_inc(f.chosen, 1)
    dve.tensor_scalar(f.rates[:, :], f.rates[:, :], -1.0, None, ALU.mult).then_inc(f.rates_ready, 1)
    dve.wait_ge(f.taps_halved, 1)
    dve.wait_ge(f.wide_loaded, 16)
    for half in range(HALVES):
        for tap in range(TAPS):
            dve.scalar_tensor_tensor(f.w_tap[:, half, tap, :], f.w_in[:, half, :], 0.5, f.wide_taps[:, half, tap, :], ALU.mult, ALU.mult).then_inc(f.taps_folded, 1)
    dve.wait_ge(f.chosen, 1)
    dve.wait_ge(f.rates_ready, 1)
    credit(dve, f.driven, 2)
    credit(dve, f.states, 4)
    credit(dve, f.ended, 2)
    credit(dve, f.added, 1)
    steps = Steps(dve, f.steps, 3)
    series = Steps(dve, f.series_steps, 4)

    def prepare(b, former):
        h = b[1] % 2
        for half in range(HALVES):
            yield 5 + 2 * half
            dve.wait_ge(f.kept, count(b, KEPT, half + 1))
            dve.scalar_tensor_tensor(f.x[:, h, half, :], f.x_tanh[:, half, :], 1.0, f.conv[:, half, :], ALU.add, ALU.mult).then_inc(f.x_made, 1)
        yield 12
        dve.wait_ge(f.kept, count(b, KEPT, 4))
        dve.scalar_tensor_tensor(f.z[:, h, :, :], f.z_tanh[:, :, :], 1.0, f.z_half[:, :, :], ALU.add, ALU.mult).then_inc(f.z_made, 1)
        e, t = f.small[:, :, :], f.series[:, :, :]
        yield 21
        dve.wait_ge(f.logs, count(b, 1, 1))
        series.begin(b)
        dve.tensor_scalar(f.is_small[:, :, :], e, SMALL_EXP, None, ALU.is_lt)
        series.mark(dve.tensor_scalar(t, e, 1.0 / 3, -0.5, ALU.mult, ALU.add))
        yield 22
        series.need()
        series.mark(dve.tensor_tensor(t, t, e, ALU.mult))
        yield 23
        series.need()
        series.mark(dve.scalar_tensor_tensor(t, t, 1.0, e, ALU.add, ALU.mult))
        yield 24
        series.need()
        yield 25
        series.mark(dve.copy_predicated(f.delta[:, :, :], f.is_small[:, :, :], t))
        series.need()
        dve.scalar_tensor_tensor(f.delta[:, :, :], f.v[:, :, :], 0.0, f.delta[:, :, :], ALU.max, ALU.add).then_inc(f.deltas, 1)
        yield 26
        dve.wait_ge(f.deltas, count(b, 1, 1))
        dve.tensor_tensor(f.du[:, :, :], f.delta[:, :, :], f.x[:, h, :, :], ALU.mult).then_inc(f.inputs, 1)
        yield 29
        dve.wait_ge(f.highs, count(b, 2, 2))
        dve.tensor_tensor(f.low[:, h, 1, :, :], f.du[:, :, :], f.high[:, h, 1, :, :].bitcast(F32), ALU.subtract).then_inc(f.lows, 1)

    def drive(b, n):
        dve.wait_ge(f.spread, count(b, 2 * NG, 2 * n + 2))
        dve.tensor_tensor(f.drive[:, n % 4, :], m.bank[4 + n % 2][:, :], f.bc[:, b[1] % 2, 0, :], ALU.mult).then_inc(f.driven, 1)

    def scan(b, n):
        dve.wait_ge(f.decays, count(b, NG, n + 1 + 2))
        dve.wait_ge(f.driven, count(b, NG, n + 1 + 2))
        dve.wait_ge(f.weighed, count(b, NG, n + 5))
        dve.tensor_tensor_scan(f.state[:, n % 4, :], f.keep[:, n % 4, :], f.drive[:, n % 4, :], 0.0,
                               ALU.mult, ALU.add).then_inc(f.states, 1)

    def end(b, half):
        dve.wait_ge(f.summed, count(b, NG // QUAD, (half + 1) * GROUPS // QUAD))
        if half == 0 and b[1]:
            dve.wait_ge(f.out, count(b, 1, 0))
        dve.scalar_tensor_tensor(f.y[:, half, :], f.x[:, b[1] % 2, half, :], f.skip[:, half:half + 1], m.bank[6 + half][:, :],
                                 ALU.mult, ALU.add).then_inc(f.ended, 1)

    def body(new, now, former):
        beside = Beside(prepare(new, former)) if new else None
        for n in range(NG):
            if now:
                drive(now, n)
            if former and n == 0:
                scan(former, NG - 1)
            if now and n:
                scan(now, n - 1)
            if former:
                if n == 4:
                    end(former, 1)
                if n == 5:
                    dve.wait_ge(f.ended, count(former, HALVES, 2 + 2))
                    dve.tensor_tensor(f.y[:, :, :], f.y[:, :, :], f.z[:, former[1] % 2, :, :], ALU.mult).then_inc(f.gated, 1)
                if n == 9:
                    dve.wait_ge(f.out, count(former, 1, 1))
                    dve.tensor_tensor(m.x[:, rows(former)], m.bank[1][:, :], m.x[:, rows(former)], ALU.add).then_inc(f.added, 1)
            if beside:
                beside.until(n)
            if now and n == 20:
                end(now, 0)
            if new and n == 12:
                if former:
                    dve.wait_ge(f.added, count(former, 1, 2))
                steps.begin(new)
                take_statistics(dve, nc, m, s, after(new, 1), stage, steps)

    rounds(dve, body)


def mamba_pool(pool, nc, m, s, f, stage):
    credit(pool, f.weighed, 8)

    def body(ahead, new, now, former):
        for n in range(NG):
            if ahead and ahead[1] and n == 20:
                normalise(pool, nc, m, s, ahead, stage)
            if new and n == 28:
                h = new[1] % 2
                pool.wait_ge(f.highs, count(new, 2, 1))
                pool.tensor_tensor(f.low[:, h, 0, :, :], f.delta[:, :, :], f.high[:, h, 0, :, :].bitcast(F32), ALU.subtract).then_inc(f.lows, 1)
            if now:
                pool.wait_ge(f.states, count(now, NG, n + 1 + 4))
                if now[1] or n >= 8:
                    pool.wait_ge(f.summed, count(now, NG // QUAD, n // QUAD - 1))
                pool.tensor_tensor(f.hc[:, n % 8, :], f.state[:, n % 4, :], f.bc[:, now[1] % 2, 1, :], ALU.mult).then_inc(f.weighed, 1)

    pool.memset(f.xt[:, :, 0:TAPS - 1], 0.0).then_inc(f.padded, 1)
    rounds(pool, body, 4)


def mamba_sync(sp, nc, a, f):
    sp.dma_start(f.raw, a["choose"]).then_inc(f.raw_loaded, 16)
    sp.dma_start(f.wide_taps, a["wide_taps"].partition_broadcast(P)).then_inc(f.wide_loaded, 16)



RWKV, HEADS, LAPLACE, MAMBA, TOP1, TOP2 = "rwkv heads laplace mamba top1 top2".split()
STAGES = [RWKV, TOP1, HEADS, TOP1, LAPLACE, TOP2, MAMBA, TOP2]


WINDOW = S + P


def laplace_buffers(tmp, f):
    f.q, f.k, f.sq, f.qk = (tmp("lap_" + n, [P, S]) for n in "q k sq qk".split())
    f.v, f.vb, f.sv = (tmp("lap_" + n, [P, 2, S]) for n in "v vb sv".split())
    f.y, f.size, f.sign, f.g, f.inverse = (tmp("lap_" + n, [P, 2, PAIRED]) for n in "y size sign g inverse".split())
    f.p = tmp("lap_p", [P, PAIRED])



def laplace_constants(nc, a, sb, sem, loads, setup, m):
    f = Names()
    f.values, f.shared, f.queries, f.keys, f.scores, f.values_made, f.added = (
        sem("lap_" + n) for n in "values shared queries keys scores values_made added".split())
    f.weights, f.out, f.values_biased, f.value_gates, f.gates, f.arguments, f.sizes = (
        sem("lap_" + n) for n in "weights out values_biased value_gates gates arguments sizes".split())
    f.steps, f.row, f.row_kept, f.rows_stored, f.skewed = (
        sem("lap_" + n) for n in "steps row row_kept rows_stored skewed".split())
    f.signs, f.absolutes, f.phis, f.halves, f.inverses, f.ahead_steps, f.scalar_steps = (
        sem("lap_" + n) for n in "signs absolutes phis halves inverses ahead_steps scalar_steps".split())
    f.wqk, f.wv, f.bqk, f.gb = sb("wqk", [P, P]), sb("wv", [P, P]), sb("bqk", [P, 1]), sb("gb", [P, 4])
    f.bv, f.toeplitz, f.causal = sb("bv", [P, S]), sb("toeplitz", [P, S]), sb("causal", [P, P])
    buckets, table, row = sb("buckets", [32, WINDOW]), sb("table", [32, 1]), sb("bias_row", [1, WINDOW])
    loads += [(f.wqk[:, :], a["wqk"]), (f.wv[:, :], a["wv"]), (f.bqk[:, :], a["bqk"]), (f.gb[:, :], a["gb"]),
              (f.bv[:, :], a["bv"].partition_broadcast(P)), (f.causal[:, :], a["causal"]),
              (buckets[:, :], a["buckets"]), (table[:, :], a["table"])]
    scratch = nc.dram_tensor("bias_rows", (P * WINDOW,), F32)
    half = WINDOW // 2

    def look_up(pe):
        for n in range(2):
            last = pe.matmul(m.bank[6 + n][0:1, 0:half], table[:, :], buckets[:, n * half:(n + 1) * half], start=True, stop=True)
        last.then_inc(f.row, 1)
        pe.wait_ge(f.row_kept, 1)

    def scale(dve):
        dve.wait_ge(f.row, 1)
        for n in range(2):
            last = dve.tensor_scalar(row[:, n * half:(n + 1) * half], m.bank[6 + n][0:1, 0:half],
                                     math.sqrt(P) / DEVIATION, -CENTRE / DEVIATION, ALU.mult, ALU.add)
        last.then_inc(f.row_kept, 1)

    def skew(sp):
        sp.wait_ge(f.row_kept, 1)
        sp.dma_start(bass.AP(tensor=scratch, offset=0, ap=[[WINDOW, P], [1, WINDOW]]), row[0:1, :].unsqueeze(1).to_broadcast([1, P, WINDOW])).then_inc(f.rows_stored, 16)
        sp.wait_ge(f.rows_stored, 16)
        sp.dma_start(f.toeplitz[:, :], bass.AP(tensor=scratch, offset=P - 1, ap=[[WINDOW - 1, P], [1, S]])).then_inc(f.skewed, 16)

    setup.late_tensor.append(look_up)
    setup.late_vector.append(scale)
    setup.late_sync.append(skew)
    return f


def rwkv_memory(nc, a, sb, tmp, sem, loads, setup, m):
    f = Names()
    f.weights_mixed, f.decayed, f.kvr, f.mixed, f.added, f.out = (
        sem("rwkv_" + n) for n in "weights_mixed decayed kvr mixed added out".split())
    f.less, f.less_pool, f.exps, f.below, f.logs, f.inverses, f.steps = (
        sem("rwkv_" + n) for n in "less less_pool exps below logs inverses steps".split())
    f.maxima, f.tops, f.sums, f.scaled, f.decay_exp, f.mixes, f.prepared = (
        sem("rwkv_" + n) for n in "maxima tops sums scaled decay_exp mixes prepared".split())
    f.terms, f.ahead_steps, f.k_kept, f.vr_kept = (sem("rwkv_" + n) for n in "terms ahead_steps k_kept vr_kept".split())
    f.w_now, f.w_before, f.wo = sb("w_now", [P, 3, P]), sb("w_before", [P, 3, P]), sb("wo", [P, P])
    f.mix, f.unmix, f.decay, f.first = sb("mix", [P, 3]), sb("unmix", [P, 3]), sb("decay", [P, 2]), sb("first", [P, 1])
    f.k, f.vr = tmp("rwkv_k", [P, 2, S]), tmp("rwkv_vr", [P, 2, 2, S])
    f.largest, f.sum_w, f.sum_wv = (tmp(n, [P, 2, S + 1]) for n in ("largest", "sum_w", "sum_wv"))
    f.top, f.ev, f.num, f.den, f.log, f.inverse, f.rw = (tmp("rwkv_" + n, [P, S]) for n in "top ev num den log inverse rw".split())
    f.d, f.e, f.ew = tmp("less", [P, 4, S]), tmp("exps", [P, 2, 4, S]), tmp("rwkv_ew", [P, 2, S])
    loads += [(f.w_now[:, :, :], a["wkvr"]), (f.wo[:, :], a["wo"]), (f.mix[:, :], a["mix"]), (f.decay[:, 0:1], a["decay"]),
              (f.first[:, :], a["first"])]

    def decay_scalar(act):
        act.activation(f.decay[:, 1:2], f.decay[:, 0:1], ACT.Exp).then_inc(f.decay_exp, 1)

    def mix_vector(dve):
        dve.wait_ge(f.decay_exp, 1)
        dve.tensor_scalar(f.decay[:, 1:2], f.decay[:, 1:2], -1.0, None, ALU.mult).then_inc(f.decayed, 1)
        dve.tensor_scalar(f.unmix[:, :], f.mix[:, :], -1.0, 1.0, ALU.mult, ALU.add).then_inc(f.mixes, 1)
        dve.wait_ge(f.mixes, 1)
        for n in range(3):
            dve.tensor_scalar(f.w_before[:, n, :], f.w_now[:, n, :], f.unmix[:, n:n + 1], None, ALU.mult).then_inc(f.weights_mixed, 1)
        dve.wait_ge(f.weights_mixed, 3)
        for n in range(3):
            dve.tensor_scalar(f.w_now[:, n, :], f.w_now[:, n, :], f.mix[:, n:n + 1], None, ALU.mult).then_inc(f.weights_mixed, 1)
        dve.memset(f.largest[:, :, 0:1], -BIG)
        dve.memset(f.sum_w[:, :, 0:1], 0.0)
        dve.memset(f.sum_wv[:, :, 0:1], 0.0).then_inc(f.prepared, 1)
        dve.wait_ge(f.prepared, 1)
        dve.wait_ge(f.decayed, 1)

    setup.scalar.append(decay_scalar)
    setup.vector.append(mix_vector)
    return f


def mamba_memory(nc, a, sb, tmp, sem, loads):
    f = Names()
    f.decays, f.spread, f.driven, f.weighed, f.summed, f.inner, f.x_made = (
        sem("mamba_" + n) for n in "decays spread driven weighed summed inner x_made".split())
    f.kept, f.projected, f.ended, f.delta_made, f.highs, f.lows, f.gated = (
        sem("mamba_" + n) for n in "kept projected ended delta_made highs lows gated".split())
    f.added, f.out, f.chosen, f.rates_ready, f.scalar_steps, f.biased, f.logs = (
        sem("mamba_" + n) for n in "added out chosen rates_ready scalar_steps biased logs".split())
    f.deltas, f.inputs, f.states, f.steps, f.series_steps, f.rate_exps, f.raw_loaded = (
        sem("mamba_" + n) for n in "deltas inputs states steps series_steps rate_exps raw_loaded".split())
    f.wide_loaded, f.taps_halved, f.taps_folded, f.padded = (
        sem("mamba_" + n) for n in "wide_loaded taps_halved taps_folded padded".split())
    f.z_made = sem("mamba_z_made")
    f.w_in, f.w_dt, f.w_bc = sb("w_in", [P, 4, P]), sb("w_dt", [P, HALVES, JUST]), sb("w_bc", [P, HALVES, 2, P])
    f.w_delta, f.w_out = sb("w_delta", [JUST, HALVES, P]), sb("w_out", [P, HALVES, P])
    f.taps, f.delta_bias, f.skip = sb("taps", [P, HALVES, TAPS + 1]), sb("delta_bias", [P, HALVES]), sb("skip", [P, HALVES])
    f.rates, f.one, f.gather = sb("rates", [P, NG]), sb("one", [P, 1]), sb("gather", [P, 4, 32])
    f.choose, f.w_tap = tmp("choose", [P, GROUPS, P], F32R), tmp("w_tap", [P, HALVES, TAPS, P])
    f.xt = tmp("m_xt", [P, 2, TAPS - 1 + S])
    f.x, f.z = (tmp("m_" + n, [P, 2, HALVES, S]) for n in "xz")
    f.conv, f.x_tanh, f.z_half, f.z_tanh, f.y = (tmp("m_" + n, [P, HALVES, S]) for n in "conv x_tanh z_half z_tanh y".split())
    f.v, f.small, f.delta, f.series, f.du = f.conv, f.x_tanh, f.z_half, f.z_tanh, f.z_tanh
    f.is_small = tmp("is_small", [P, HALVES, S], mybir.dt.uint32)
    f.high, f.low = tmp("high", [P, 2, 2, HALVES, S], F32R), tmp("low", [P, 2, 2, HALVES, S], F32R)
    f.dt, f.bc = tmp("dt", [JUST, S]), tmp("bc", [P, 2, 2, S])
    f.keep, f.drive, f.state = (tmp("m_" + n, [P, 4, S]) for n in "keep drive state".split())
    f.hc = tmp("m_hc", [P, 2 * QUAD, S])
    f.raw = f.keep[:, :, :].rearrange("p a (b c) -> p (a b) c", c=P)
    f.wide_taps = f.conv[:, :, :].rearrange("p h (t c) -> p h t c", t=TAPS)
    loads += [(f.w_in[:, :, :], a["w_in"]), (f.w_dt[:, :, :], a["w_dt"]), (f.w_bc[:, :, :, :], a["w_bc"]),
              (f.w_delta[:, :, :], a["w_delta"]), (f.w_out[:, :, :], a["w_out"]), (f.taps[:, :, :], a["taps"]),
              (f.delta_bias[:, :], a["delta_bias"]), (f.skip[:, :], a["skip"]), (f.rates[:, :], a["a_log"]),
              (f.gather[:, :, :], a["gather"])]
    return f


def heads_weights(a, sb, sem, loads):
    f = Names()
    f.scored, f.summed, f.turned, f.ring_read, f.ring_made, f.exps, f.out_kept = (
        sem("heads_" + n) for n in "scored summed turned ring_read ring_made exps out_kept".split())
    f.half_maxima, f.maxima_turned, f.highs, f.less_highs, f.steps, f.ahead_steps, f.less_rests = (
        sem("heads_" + n) for n in "half_maxima maxima_turned highs less_highs steps ahead_steps less_rests".split())
    f.added, f.middles, f.parted, f.less_middles, f.less_parted, f.stacked0, f.stacked1 = (
        sem("heads_" + n) for n in "added middles parted less_middles less_parted stacked0 stacked1".split())
    f.lowered0, f.lowered1, f.cleared, f.stack_cleared = (
        sem("heads_" + n) for n in "lowered0 lowered1 cleared stack_cleared".split())
    f.stacked, f.lowered = (f.stacked0, f.stacked1), (f.lowered0, f.lowered1)
    f.zeroed = sem("heads_zeroed")
    f.wq, f.wk, f.wv = (sb("h_w" + n, [P, P]) for n in "qkv")
    loads += [(f.wq[:, :], a["h_wq"]), (f.wk[:, :], a["h_wk"]), (f.wv[:, :], a["h_wv"])]
    return f


def heads_buffers(tmp, f):
    BF16 = mybir.dt.bfloat16
    f.part, f.rest = tmp("part", [P, 2, 3, S], BF16), tmp("rest", [P, 2, S])
    f.less, f.less_rest = tmp("h_less", [HALF_HEADS, 3, S], BF16), tmp("less_rest", [HALF_HEADS, S])
    f.p, f.o = tmp("h_p", [P, 2, 4, S]), tmp("h_o", [P, S])
    f.maxima, f.inverse, f.mean = tmp("maxima", [P, TILES, NHEADS]), tmp("h_inverse", [P, TILES, 4]), tmp("h_mean", [P, TILES, 4, HD])
    f.zero = tmp("zero", [P, 1])
    f.nothing = tmp("nothing", [4, S], BF16)
    f.v = tmp("h_v", [P, 2, TILES, NHEADS, 32])
    f.qs, f.ks = (tmp(n, [P, 2, NHEADS, S], BF16) for n in ("qs", "ks"))


def build(nc, a, out, stages):
    ctx = ExitStack()
    with ctx:
        def sem(name):
            return ctx.enter_context(nc.semaphore(name))

        def into(stack):
            return lambda name, shape, dtype=F32: stack.enter_context(nc.sbuf_tensor(name, shape, dtype))

        sb = into(ctx)

        m = Names()
        m.banks = ctx.enter_context(nc.psum_tensor("banks", [P, 8, 512], F32))
        m.bank = [m.banks[:, i, :] for i in range(8)]
        m.x = sb("x", [P, BATCHES * S])
        m.ident = sb("ident", [P, P])
        m.minus_half = sb("minus_half", [P, TILES])
        m.bn = sb("bn", [P, 2, TILES, 6])
        m.mean_var = sb("mean_var", [P, 2, TILES, 2])
        m.half_stats = sb("half_stats", [P, 5, TILES])
        m.rstd = sb("rstd", [P, 2, TILES])
        m.xn = sb("xn", [P, 2, S])
        m.xt = sb("xt", [P, 2, S + 1])
        m.order = sb("order", [P, TILES * 8])
        m.r_l, m.r_d, m.r_exp, m.r_hot, m.r_two = (sb(n, [P, TILES * 8]) for n in ("r_l", "r_d", "r_exp", "r_hot", "r_two"))
        m.r_col = sb("r_col", [P, 3, TILES])
        m.gates = sb("gates", [P, 2, TILES, 8])
        m.gates_t = sb("gates_t", [8, S])
        s = Names()
        s.first_loaded, s.x_loaded = sem("s_first_loaded"), sem("s_x_loaded")
        s.loaded, s.filled, s.stats, s.rstd, s.centred, s.normed, s.transposed = (
            sem("s_" + n) for n in "loaded filled stats rstd centred normed transposed".split())
        s.xt, s.first_steps, s.stage, s.stored, s.late = (
            sem("s_" + n) for n in "xt first_steps stage stored late".split())

        first_loads, loads, late_loads = [], [], []
        x_view = a["x"].rearrange("b (t p) d -> p b t d", p=P)
        x_loads = [(by_tile(m.x[:, b * S:(b + 1) * S]), x_view[:, b]) for b in range(BATCHES)]
        first_loads += [x_loads[0], (m.ident[:, :], a["ident"])]
        loads.append((m.order[:, :], a["order"]))

        plans = [None] * len(stages)
        setup = Names()
        setup.vector, setup.scalar, setup.late_tensor, setup.late_vector, setup.late_sync = [], [], [], [], []

        def experts_weights(pre, blocks, into, take):
            w = Names()
            w.gates_kept, w.logits, w.first, w.hidden, w.out, w.added, w.gates_made = (
                sem(pre + "_" + name) for name in "gates_kept logits first hidden out added gates_made".split())
            w.gates_turned, w.shifted, w.exps, w.steps = (
                sem(pre + "_" + name) for name in "gates_turned shifted exps steps".split())
            w.split, w.x_high, w.x_low, w.ahead_steps = (sem(pre + "_" + name) for name in "split x_high x_low ahead_steps".split())
            w.w1 = into(pre + "w1", [P, 8, blocks * P])
            w.w2 = into(pre + "w2", [P, 8 * blocks * P])
            w.b1 = into(pre + "b1", [P, 8 * blocks])
            w.b2 = into(pre + "b2", [8, P])
            w.wr = into(pre + "wr", [P, 8])
            take += [(w.w1[:, :, :], a[pre + "w1"].rearrange("e d f -> d e f")),
                     (w.w2[:, :].rearrange("p (e j d) -> p e j d", e=8, j=blocks), a[pre + "w2"].rearrange("e (j p) d -> p e j d", p=P)),
                     (w.b1[:, :], a[pre + "b1"]), (w.b2[:, :], a[pre + "b2"]), (w.wr[:, :], a[pre + "wr"])]
            return w

        def experts_plan(n, w, blocks, top, func):
            f = Names()
            f.blocks, f.top, f.func, f.use = blocks, top, func, stages[:n].count(stages[n])
            f.w1, f.w2, f.b1, f.b2, f.wr = w.w1, w.w2, w.b1, w.b2, w.wr
            f.split, f.x_high, f.x_low, f.ahead_steps, f.gates = w.split, w.x_high, w.x_low, w.ahead_steps, m.gates
            if top == 1:
                f.br = w.br
            f.gates_kept, f.logits, f.first, f.hidden, f.out, f.added = (
                w.gates_kept, w.logits, w.first, w.hidden, w.out, w.added)
            f.gates_made, f.gates_turned, f.shifted, f.exps, f.steps = w.gates_made, w.gates_turned, w.shifted, w.exps, w.steps
            with ExitStack() as own:
                if top == 1:
                    f.xh, f.xl = w.xh, w.xl
                else:
                    f.xh, f.xl = (into(own)(f"{name}{n}", [P, 2, S], F32R) for name in ("x_high", "x_low"))
                f.hid = into(own)(f"hid{n}", [P, 2, blocks, S])
                f.w_high, f.w_low = (into(own)(f"{name}{n}", [P, 8, blocks * P], F32R) for name in ("w_high", "w_low"))
            plans[n] = (f, experts_tensor, experts_scalar, experts_vector, experts_pool)

        if LAPLACE in stages:
            lap = laplace_constants(nc, a, sb, sem, loads, setup, m)
        with ExitStack() as early:
            if TOP1 in stages:
                w = experts_weights("t1", 4, into(early), loads)
                br = into(early)("t1br", [P, TILES * 8])
                w.br = br[:, :]
                w.xh, w.xl = (into(early)(name, [P, 2, S], F32R) for name in ("x_high", "x_low"))
                loads.append((w.br, a["t1br"].partition_broadcast(P)))
            if HEADS in stages:
                heads = heads_weights(a, into(early), sem, loads)
            if RWKV in stages:
                with ExitStack() as own:
                    f = rwkv_memory(nc, a, into(early), into(own), sem, first_loads, setup, m)
                    plans[stages.index(RWKV)] = (f, rwkv_tensor, rwkv_scalar, rwkv_vector, rwkv_pool)
            if HEADS in stages:
                with ExitStack() as own:
                    heads_buffers(into(own), heads)
                    plans[stages.index(HEADS)] = (heads, heads_tensor, heads_scalar, heads_vector, heads_pool)
            for n, kind in enumerate(stages):
                if kind == TOP1:
                    experts_plan(n, w, 4, 1, ACT.Gelu)
        if TOP2 in stages:
            w = experts_weights("t2", 2, sb, late_loads)
        if MAMBA in stages:
            with ExitStack() as own:
                mamba = mamba_memory(nc, a, sb, into(own), sem, late_loads)
                plans[stages.index(MAMBA)] = (mamba, mamba_tensor, mamba_scalar, mamba_vector, mamba_pool)
        for n, kind in enumerate(stages):
            if kind == TOP2:
                experts_plan(n, w, 2, 2, ACT.Relu)
        if LAPLACE in stages:
            with ExitStack() as own:
                laplace_buffers(into(own), lap)
                plans[stages.index(LAPLACE)] = (lap, laplace_tensor, laplace_scalar, laplace_vector, experts_pool)

        block = ctx.enter_context(nc.Block())

        def between(eng, n):
            eng.drain().then_inc(s.stage, 1)
            eng.wait_ge(s.stage, 4 * (n + 1))

        late = max([n + 1 for n, kind in enumerate(stages) if kind in (RWKV, TOP1, HEADS)], default=0)
        filling = stages.index(HEADS) - 1 if HEADS in stages else None

        all_loaded = 1 if stages[0] == RWKV and len(stages) > 1 else 0

        def arrived(eng, kind, n):
            if n == all_loaded:
                eng.wait_ge(s.loaded, 16 * len(loads))
            if kind in (TOP2, MAMBA) and late_loads:
                eng.wait_ge(s.late, 16 * len(late_loads))

        @block.sync
        def _(sp):
            for tile, dram in first_loads:
                sp.dma_start(tile, dram).then_inc(s.first_loaded, 16)
            for tile, dram in x_loads[1:]:
                sp.dma_start(tile, dram).then_inc(s.x_loaded, 16)
            for tile, dram in loads:
                sp.dma_start(tile, dram).then_inc(s.loaded, 16)
            if late_loads and late == 0:
                for tile, dram in late_loads:
                    sp.dma_start(tile, dram).then_inc(s.late, 16)
            for n, kind in enumerate(stages):
                if n:
                    sp.wait_ge(s.stage, 4 * n)
                if n == all_loaded:
                    for do in setup.late_sync:
                        do(sp)
                if n == late and n:
                    for tile, dram in late_loads:
                        sp.dma_start(tile, dram).then_inc(s.late, 16)
                if kind == HEADS:
                    heads_sync(sp, nc, m, s, heads, n)
                if kind == MAMBA:
                    mamba_sync(sp, nc, a, mamba)
            last = plans[-1][0]
            for b in range(BATCHES):
                if stages[-1] in (TOP1, TOP2):
                    sp.wait_ge(last.added, 9 * (BATCHES * last.use + b + 1) + 2)
                elif b == 0:
                    sp.wait_ge(s.stage, 4 * len(stages))
                sp.dma_start(out.rearrange("b (t p) d -> p b t d", p=P)[:, b], by_tile(m.x[:, b * S:(b + 1) * S])).then_inc(s.stored, 16)
            sp.wait_ge(s.stored, 16 * BATCHES)

        @block.tensor
        def _(pe):
            pe.wait_ge(s.first_loaded, 16 * len(first_loads))
            credit(pe, s.transposed, 2)
            for n, (f, tensor, _, _, _) in enumerate(plans):
                arrived(pe, stages[n], n)
                if n == all_loaded:
                    for do in setup.late_tensor:
                        do(pe)
                tensor(pe, nc, m, s, f, n)
                between(pe, n)

        @block.scalar
        def _(act):
            act.wait_ge(s.first_loaded, 16 * len(first_loads))
            act.wait_ge(s.filled, 1)
            credit(act, s.xt, 1)
            for do in setup.scalar:
                do(act)
            for n, (f, _, scalar, _, _) in enumerate(plans):
                arrived(act, stages[n], n)
                scalar(act, nc, m, s, f, n)
                between(act, n)

        @block.vector
        def _(dve):
            dve.wait_ge(s.first_loaded, 16 * len(first_loads))
            first = Steps(dve, s.first_steps, 3)
            first.begin((0, 0))
            statistics_of(dve, nc, m, s, bass.ds(0, S), 0, first)
            for do in setup.vector:
                do(dve)
            for n, (f, _, _, vector, _) in enumerate(plans):
                arrived(dve, stages[n], n)
                if n == all_loaded:
                    for do in setup.late_vector:
                        do(dve)
                vector(dve, nc, m, s, f, n)
                between(dve, n)

        @block.gpsimd
        def _(pool):
            pool.wait_ge(s.first_loaded, 16 * len(first_loads))
            pool.memset(m.minus_half[:, :], -0.5)
            pool.memset(m.xt[:, :, 0:1], 0.0).then_inc(s.filled, 1)
            pool.wait_ge(s.filled, 1)
            credit(pool, s.normed, 2)
            normalise(pool, nc, m, s, (0, 0), 0)
            if filling == -1:
                heads_fill(pool, s, heads, 0)
            for n, (f, _, _, _, run) in enumerate(plans):
                arrived(pool, stages[n], n)
                run(pool, nc, m, s, f, n)
                if n + 1 < len(stages):
                    normalise(pool, nc, m, s, (0, 0), n + 1)
                if filling == n:
                    heads_fill(pool, s, heads, n + 1)
                between(pool, n)




def lay_out(i, np):
    def f(v):
        return np.ascontiguousarray(np.asarray(v))

    d = {"x": f(i["L0_attn_a_x"]), "ident": np.eye(P, dtype=np.float32)}
    d["order"] = f(np.tile(np.arange(8, 0, -1, dtype=np.float32), (P, TILES)))
    for pre, w1, b1, w2, b2, wr in (("t1", "L0_ffn_W1", "L0_ffn_b1", "L0_ffn_W2", "L0_ffn_b2", "L0_ffn_Wr"),
                                    ("t2", "L1_ffn_W1", "L1_ffn_b1", "L1_ffn_W2", "L1_ffn_b2", "L1_ffn_gate")):
        d[pre + "w1"], d[pre + "w2"], d[pre + "b2"], d[pre + "wr"] = f(i[w1]), f(i[w2]), f(i[b2]), f(i[wr])
        d[pre + "b1"] = f(np.asarray(i[b1]).reshape(-1, P).T)
    d["wqk"], d["wv"], d["table"] = f(i["L1_attn_a_wqk"]), f(i["L1_attn_a_wv"]), f(i["L1_attn_a_rel_bias"]).reshape(32, 1)
    d["bqk"] = f(i["L1_attn_a_bqk"]).reshape(P, 1)
    d["gb"] = f(np.concatenate([np.asarray(i["L1_attn_a_gamma"]), np.asarray(i["L1_attn_a_beta"])]).T)
    d["bv"] = f(np.tile(np.asarray(i["L1_attn_a_bv"]), TILES))
    key, query = np.arange(P)[:, None], np.arange(P)[None]
    d["causal"] = f(np.where(query >= key, np.float32(1), np.float32(0)))
    n = np.maximum(np.arange(WINDOW) - (P - 1), 0)
    large = 16 + (np.log(np.maximum(n, 1).astype(np.float32) / 16) / math.log(128 / 16) * 16).astype(np.int32)
    bucket = np.where(n < 16, n, np.minimum(large, 31))
    d["buckets"] = f((np.arange(32)[:, None] == bucket[None]).astype(np.float32))
    d["wkvr"] = f(np.stack([np.asarray(i["L0_attn_a_" + w]).T for w in ("Wk", "Wv", "Wr")], 1))
    d["wo"] = f(np.asarray(i["L0_attn_a_Wo"]).T)
    d["mix"] = f(np.stack([np.asarray(i["L0_attn_a_time_mix_" + w]).reshape(P) for w in "kvr"], 1))
    d["decay"], d["first"] = f(i["L0_attn_a_time_decay"]).reshape(P, 1), f(i["L0_attn_a_time_first"]).reshape(P, 1)
    w = {n: np.asarray(i["L1_attn_b_" + n]) for n in ("in_proj_w", "conv_w", "conv_b", "x_proj_w", "dt_proj_w", "dt_proj_b",
                                                       "A_log", "D", "out_proj_w")}
    d["w_in"] = f(w["in_proj_w"].reshape(4, P, P).transpose(2, 0, 1))
    by_half = w["x_proj_w"].T.reshape(HALVES, P, -1).transpose(1, 0, 2)
    d["w_dt"] = f(by_half[:, :, :JUST])
    d["w_bc"] = f(np.tile(by_half[:, :, JUST:].reshape(P, HALVES, 2, 1, STATES), (1, 1, 1, JUST, 1)).reshape(P, HALVES, 2, P))
    d["w_delta"] = f(w["dt_proj_w"].T.reshape(JUST, HALVES, P))
    d["w_out"] = f(w["out_proj_w"].T.reshape(HALVES, P, P).transpose(1, 0, 2))
    d["taps"] = f(np.concatenate([w["conv_w"][:, 0], w["conv_b"][:, None]], 1).reshape(HALVES, P, TAPS + 1).transpose(1, 0, 2))
    d["wide_taps"] = f(w["conv_w"][:, 0].reshape(HALVES, P, TAPS).transpose(0, 2, 1))
    d["delta_bias"], d["skip"] = f(w["dt_proj_b"].reshape(HALVES, P).T), f(w["D"].reshape(HALVES, P).T)
    d["a_log"] = f(w["A_log"].reshape(HALVES * GROUPS, JUST * STATES).T)
    part, channel = np.arange(P), np.arange(P)
    d["choose"] = f((channel[:, None, None] == np.arange(GROUPS)[None, :, None] * JUST + part // STATES).astype(np.float32))
    d["gather"] = f((np.arange(32)[None, None] == np.arange(4)[None, :, None] * JUST + (part // STATES)[:, None, None]).astype(np.float32))
    for n in "qkv":
        w = np.asarray(i["L0_attn_b_W" + n]).T
        if n != "v":
            w = w.reshape(P, 2, HALF_HEADS, HD).transpose(0, 1, 3, 2).reshape(P, P)
        d["h_w" + n] = f(w)
    d["t1br"] = f(np.tile(np.asarray(i["L0_ffn_br"]), TILES))
    return d


def kernel(**inputs):
    import numpy as np
    import concourse.bacc as bacc
    from concourse.bass_utils import run_bass_kernel_spmd

    nc = bacc.Bacc("TRN2", target_bir_lowering=False, num_devices=1)
    arrays = {f"in_{k}": v for k, v in lay_out(inputs, np).items()}
    aps = {k[3:]: nc.dram_tensor(k, v.shape, mybir.dt.from_np(v.dtype), kind="ExternalInput").ap() for k, v in arrays.items()}
    out = nc.dram_tensor("out_x", (BATCHES, S, P), F32, kind="ExternalOutput").ap()
    build(nc, aps, out, STAGES)
    r = run_bass_kernel_spmd(nc, [arrays], core_ids=[0])
    return r.results[0]["out_x"]
```
